# Optimizing a Trainium2 kernel written in Bass

```python
import numpy as np
import jax
import jax.numpy as jnp

def _softmax(x, axis=-1):
    return jax.nn.softmax(x, axis=axis)

def _gelu(x):
    return jax.nn.gelu(x, approximate=True)

def _silu(x):
    return jax.nn.silu(x)

def _sigmoid(x):
    return jax.nn.sigmoid(x)

def _layernorm(x, axis=-1, eps=1e-05):
    m = jnp.mean(x, axis=axis, keepdims=True)
    v = jnp.var(x, axis=axis, keepdims=True)
    return (x - m) / jnp.sqrt(v + eps)

def _scatter_add(tgt, idx, src, axis=0):
    return tgt.at[idx].add(src)

def _segment_sum(src, seg, n):
    return jax.ops.segment_sum(src, seg, n)
kernel_name = 'mk_seq_postln_d1_jaxref_r4_454550'

def setup_inputs(seed: int=0):
    np.random.seed(seed)
    _w = jnp.asarray

    def _L0_attn_setup():
        import jax, jax.numpy as jnp
        import numpy as np
        D_MODEL = 256
        D_STATE = 16
        EXPAND = 2
        D_INNER = D_MODEL * EXPAND
        DT_RANK = (D_MODEL + 15) // 16
        BATCH = 2
        SEQ = 256

        def _s6_forward(x, W_in, W_conv, W_x, W_dt, b_dt, A_log, D_param, W_out):
            B, L, _ = x.shape
            u, res = jnp.split(x @ W_in, 2, axis=-1)
            up = jnp.pad(u, ((0, 0), (2, 0), (0, 0)))
            u = up[:, :L] * W_conv[:, 0] + up[:, 1:L + 1] * W_conv[:, 1] + up[:, 2:L + 2] * W_conv[:, 2]
            u = jax.nn.silu(u)
            x_dbl = u @ W_x
            dt, Bm, Cm = jnp.split(x_dbl, [DT_RANK, DT_RANK + D_STATE], axis=-1)
            delta = jax.nn.softplus(dt @ W_dt + b_dt)
            A = -jnp.exp(A_log)
            deltaA = jnp.exp(jnp.einsum('bld,dn->bldn', delta, A))
            deltaB_u = jnp.einsum('bld,bln->bldn', delta * u, Bm)

            def step(h, inp):
                dA, dbu, c = inp
                h = dA * h + dbu
                y = jnp.einsum('bdn,bn->bd', h, c)
                return (h, y)
            h0 = jnp.zeros((B, D_INNER, D_STATE), dtype=u.dtype)
            _, ys = jax.lax.scan(step, h0, (jnp.moveaxis(deltaA, 1, 0), jnp.moveaxis(deltaB_u, 1, 0), jnp.moveaxis(Cm, 1, 0)))
            y = jnp.moveaxis(ys, 0, 1)
            y = y + u * D_param
            y = y * jax.nn.silu(res)
            return y @ W_out
        key = jax.random.key(seed)
        ks = jax.random.split(key, 8)

        def nrm(k, shape, scale):
            return jax.random.normal(k, shape, dtype=jnp.float32) * scale
        x = jax.random.normal(ks[0], (BATCH, SEQ, D_MODEL), dtype=jnp.float32)
        W_in = nrm(ks[1], (D_MODEL, 2 * D_INNER), D_MODEL ** (-0.5))
        W_conv = nrm(ks[2], (D_INNER, 3), 3 ** (-0.5))
        W_x = nrm(ks[3], (D_INNER, DT_RANK + 2 * D_STATE), D_INNER ** (-0.5))
        W_dt = nrm(ks[4], (DT_RANK, D_INNER), DT_RANK ** (-0.5))
        b_dt = nrm(ks[5], (D_INNER,), 0.1)
        A_log = jnp.log(jnp.tile(jnp.arange(1, D_STATE + 1, dtype=jnp.float32), (D_INNER, 1)))
        D_param = jnp.ones((D_INNER,), dtype=jnp.float32)
        W_out = nrm(ks[6], (D_INNER, D_MODEL), D_INNER ** (-0.5))
        return {'x': x, 'W_in': W_in, 'W_conv': W_conv, 'W_x': W_x, 'W_dt': W_dt, 'b_dt': b_dt, 'A_log': A_log, 'D_param': D_param, 'W_out': W_out}
    _L0_attn_in = _L0_attn_setup()

    def _L0_ffn_setup():
        import jax, jax.numpy as jnp
        import numpy as np
        E = 8
        K = 2
        CF = 1.25
        key = jax.random.key(seed)
        kx, kr, kg, ku, kd = jax.random.split(key, 5)
        D, F = (256, 1024)
        x = jax.random.normal(kx, (4, 512, D), dtype=jnp.float32)
        router_w = 0.02 * jax.random.normal(kr, (E, D), dtype=jnp.float32)
        wg = jax.random.normal(kg, (E, D, F), dtype=jnp.float32) / np.sqrt(D)
        wu = jax.random.normal(ku, (E, D, F), dtype=jnp.float32) / np.sqrt(D)
        wd = jax.random.normal(kd, (E, F, D), dtype=jnp.float32) / np.sqrt(F)
        return {'x': x, 'router_w': router_w, 'wg': wg, 'wu': wu, 'wd': wd}
    _L0_ffn_in = _L0_ffn_setup()
    _d = {'L0_attn_x': _L0_attn_in['x'], 'L0_attn_W_in': _L0_attn_in['W_in'], 'L0_attn_W_conv': _L0_attn_in['W_conv'], 'L0_attn_W_x': _L0_attn_in['W_x'], 'L0_attn_W_dt': _L0_attn_in['W_dt'], 'L0_attn_b_dt': _L0_attn_in['b_dt'], 'L0_attn_A_log': _L0_attn_in['A_log'], 'L0_attn_D_param': _L0_attn_in['D_param'], 'L0_attn_W_out': _L0_attn_in['W_out'], 'L0_ffn_router_w': _L0_ffn_in['router_w'], 'L0_ffn_wg': _L0_ffn_in['wg'], 'L0_ffn_wu': _L0_ffn_in['wu'], 'L0_ffn_wd': _L0_ffn_in['wd']}
    _x0 = _d['L0_attn_x']
    _d['L0_attn_x'] = jax.random.normal(jax.random.fold_in(jax.random.key(seed), 1), (8, 1024, 256), dtype=_x0.dtype)
    del _x0
    return _d

def reference(L0_attn_x, L0_attn_W_in, L0_attn_W_conv, L0_attn_W_x, L0_attn_W_dt, L0_attn_b_dt, L0_attn_A_log, L0_attn_D_param, L0_attn_W_out, L0_ffn_router_w, L0_ffn_wg, L0_ffn_wu, L0_ffn_wd):

    def _L0_attn_ref(x, W_in, W_conv, W_x, W_dt, b_dt, A_log, D_param, W_out):
        import jax, jax.numpy as jnp
        import numpy as np
        D_MODEL = 256
        D_STATE = 16
        EXPAND = 2
        D_INNER = D_MODEL * EXPAND
        DT_RANK = (D_MODEL + 15) // 16
        BATCH = 2
        SEQ = 256

        def _s6_forward(x, W_in, W_conv, W_x, W_dt, b_dt, A_log, D_param, W_out):
            B, L, _ = x.shape
            u, res = jnp.split(x @ W_in, 2, axis=-1)
            up = jnp.pad(u, ((0, 0), (2, 0), (0, 0)))
            u = up[:, :L] * W_conv[:, 0] + up[:, 1:L + 1] * W_conv[:, 1] + up[:, 2:L + 2] * W_conv[:, 2]
            u = jax.nn.silu(u)
            x_dbl = u @ W_x
            dt, Bm, Cm = jnp.split(x_dbl, [DT_RANK, DT_RANK + D_STATE], axis=-1)
            delta = jax.nn.softplus(dt @ W_dt + b_dt)
            A = -jnp.exp(A_log)
            deltaA = jnp.exp(jnp.einsum('bld,dn->bldn', delta, A))
            deltaB_u = jnp.einsum('bld,bln->bldn', delta * u, Bm)

            def step(h, inp):
                dA, dbu, c = inp
                h = dA * h + dbu
                y = jnp.einsum('bdn,bn->bd', h, c)
                return (h, y)
            h0 = jnp.zeros((B, D_INNER, D_STATE), dtype=u.dtype)
            _, ys = jax.lax.scan(step, h0, (jnp.moveaxis(deltaA, 1, 0), jnp.moveaxis(deltaB_u, 1, 0), jnp.moveaxis(Cm, 1, 0)))
            y = jnp.moveaxis(ys, 0, 1)
            y = y + u * D_param
            y = y * jax.nn.silu(res)
            return y @ W_out
        return _s6_forward(x, W_in, W_conv, W_x, W_dt, b_dt, A_log, D_param, W_out)

    def _L0_ffn_ref(x, router_w, wg, wu, wd):
        import jax, jax.numpy as jnp
        import numpy as np
        E = 8
        K = 2
        CF = 1.25
        B, L, D = x.shape
        xf = x.reshape(-1, D)
        N = xf.shape[0]
        capacity = max(1, int(CF * N / E))
        logits = xf @ router_w.T
        probs = jax.nn.softmax(logits, axis=-1)
        topw, topi = jax.lax.top_k(probs, K)
        topw = topw / (topw.sum(-1, keepdims=True) + 1e-06)
        fe = topi.reshape(-1)
        fw = topw.reshape(-1)
        ft = jnp.repeat(jnp.arange(N), K)
        order = jnp.lexsort((-fw, fe))
        se, sw, st = (fe[order], fw[order], ft[order])
        counts = jax.ops.segment_sum(jnp.ones_like(se), se, num_segments=E)
        starts = jnp.cumsum(counts) - counts
        rank = jnp.arange(N * K) - starts[se]
        keep = rank < capacity
        pos = jnp.where(keep, rank, capacity)
        disp = jnp.zeros((E, capacity + 1, D), x.dtype).at[se, pos].set(xf[st])
        disp = disp[:, :capacity]
        g = jnp.einsum('ecd,edf->ecf', disp, wg)
        u = jnp.einsum('ecd,edf->ecf', disp, wu)
        eo = jnp.einsum('ecf,efd->ecd', jax.nn.silu(g) * u, wd)
        gathered = eo[se, jnp.minimum(pos, capacity - 1)]
        contrib = gathered * (sw * keep.astype(x.dtype))[:, None]
        out = jnp.zeros_like(xf).at[st].add(contrib)
        return out.reshape(B, L, D)
    x = L0_attn_x
    x = _layernorm(x + _L0_attn_ref(x, L0_attn_W_in, L0_attn_W_conv, L0_attn_W_x, L0_attn_W_dt, L0_attn_b_dt, L0_attn_A_log, L0_attn_D_param, L0_attn_W_out), axis=-1)
    x = _layernorm(x + _L0_ffn_ref(x, L0_ffn_router_w, L0_ffn_wg, L0_ffn_wu, L0_ffn_wd), axis=-1)
    return x

_drawn_inputs = setup_inputs


def setup_inputs(seed=0):
    import zlib

    import numpy as np

    out = dict(_drawn_inputs(seed))
    spreads = {'L0_attn_D_param': (1.0, 0.2)}
    factors = {}
    for name, (base, spread) in spreads.items():
        noise = np.random.default_rng([zlib.crc32(name.encode()), seed]).standard_normal(out[name].shape)
        drawn = base * np.exp(spread * noise) if base else spread * noise
        out[name] = jnp.asarray(drawn.astype(out[name].dtype))
    for name, factor in factors.items():
        out[name] = (out[name] * factor).astype(out[name].dtype)
    return out
```

```python
from contextlib import ExitStack

import concourse.bass as bass
from concourse import mybir

F32 = mybir.dt.float32
BF16 = mybir.dt.bfloat16
I32 = mybir.dt.int32
U32 = mybir.dt.uint32
ACT = mybir.ActivationFunctionType
ALU = mybir.AluOpType
AX = mybir.AxisListType

P = 128
BATCH, SEQ, DM = 8, 1024, 256
TOK = BATCH * SEQ
DI, NST, RANK = 512, 16, 16
XD = RANK + 2 * NST
CL = 512
CHUNKS = TOK // CL
DT = DI // P
LT = CL // P
KD = DM // P
TILES = TOK // P
EPS = 1e-5
NE, FF = 8, 1024
CAP = max(1, int(1.25 * TOK / NE))

PROJECT = [f"u{t}" for t in range(DT)] + [f"r{l}" for l in range(LT)] + ["xd", "cT"] + \
          [f"d{t}" for t in range(DT)] + [f"ud{l}" for l in range(LT)]
CLOSE = [f"yT{t}" for t in range(DT)] + ["o0", "o1", "xt0", "xt1", "lg"]
STEP = {"u0": 1, "u1": 1, "u2": 2, "u3": 2, "yT0": 3, "yT1": 3, "yT2": 4, "yT3": 4, "r0": 5, "r1": 5,
        "r2": 6, "r3": 6, "o0": 7, "o1": 7, "xd": 8, "cT": 9, "d0": 9, "d1": 10, "d2": 11, "d3": 11,
        "xt0": 12, "xt1": 12, "lg": 13, "ud0": 13, "ud1": 13, "ud2": 14, "ud3": 14}
USES = {"first": [n for n in STEP if n in PROJECT],
        "mid": list(STEP),
        "last": [n for n in STEP if n in CLOSE]}


def count_of(c, name):
    if name in PROJECT:
        return (c + 1) * len(PROJECT) + [n for n in STEP if n in PROJECT].index(name) + 1
    return (c - 1) * len(CLOSE) + [n for n in STEP if n in CLOSE].index(name) + 1


def bank_of(parity, kind, name):
    k = USES[kind].index(name)
    swapped = {"first": 0, "mid": 1 - parity, "last": 1 - parity}[kind]
    return (k + swapped) % 2


def two_before(c, kind, name):
    k = USES[kind].index(name)
    if k >= 2:
        return c, USES[kind][k - 2]
    if kind == "first" and isinstance(c, int) and c < 0:
        return None
    before = USES["last"] if kind == "last" and isinstance(c, int) and c == CHUNKS else USES["first"]
    return c - 1, before[k - 2]


def over_chunks(eng, emit):
    emit(-1, 1, "first", False)
    emit(0, 0, "first", True)
    with eng.Fori(0, (CHUNKS - 2) // 2) as i:
        emit(i * 2 + 1, 1, "mid", True)
        emit(i * 2 + 2, 0, "mid", True)
    emit(CHUNKS - 1, 1, "last", True)
    emit(CHUNKS, 0, "last", False)


def attention(nc, a, dram, logits, ident):
    with ExitStack() as ctx:
        def sb(name, shape, dt=F32):
            return ctx.enter_context(nc.sbuf_tensor(name, shape, dt))

        def sem(name):
            return ctx.enter_context(nc.semaphore(name))

        w_in = sb("w_in", [P, KD, 2 * DI])
        w_x = sb("w_x", [P, DT, XD])
        w_dt = sb("w_dt", [RANK, DI])
        w_out = sb("w_out", [P, DT, DM])
        w_rt = sb("w_rt", [P, KD, NE])
        w_conv = sb("w_conv", [P, DT, 3])
        b_dt = sb("b_dt", [P, DT])
        d_par = sb("d_par", [P, DT])
        a_log = sb("a_log", [P, DT, NST])
        a_exp = sb("a_exp", [P, DT, NST])
        a_neg = sb("a_neg", [P, DT, NST])
        diag_d = sb("diag_d", [P, DT, P])
        minus_half = sb("minus_half", [P, LT])
        xT = sb("xT", [P, KD, CL])
        x_rows = sb("x_rows", [P, LT, DM])
        u_pad = sb("u_pad", [P, DT, CL + 2])
        tmp = sb("tmp", [P, DT, CL])
        u = sb("u", [P, DT, CL])
        gate = [sb(f"gate{i}", [P, LT, DI]) for i in range(2)]
        delta = [sb(f"delta{i}", [P, DT, CL]) for i in range(2)]
        du = [sb(f"du{i}", [P, DT, CL]) for i in range(2)]
        xdT = sb("xdT", [XD, CL])
        c_tok = [sb(f"c_tok{i}", [P, LT, XD]) for i in range(2)]
        yacc = [sb(f"yacc{i}", [P, LT, DI]) for i in range(2)]
        b_all = [sb(f"b_all{i}", [P, 4, CL]) for i in range(2)]
        dbu = [sb(f"dbu{i}", [P, DT, CL]) for i in range(2)]
        hst = [sb(f"hst{i}", [P, DT, CL]) for i in range(2)]
        carry = sb("carry", [P, NST, DT])
        yT = sb("yT", [P, DT, CL])
        resid = sb("resid", [P, LT, DM])
        x1 = sb("x1", [P, LT, DM])
        x1T = sb("x1T", [P, KD, CL])
        stats = sb("stats", [P, LT, 6])
        mean_var = sb("mean_var", [P, LT, 2])
        var_eps = sb("var_eps", [P, LT])
        rstd = sb("rstd", [P, LT])
        shift = sb("shift", [P, LT])
        da_bank = [ctx.enter_context(nc.psum_tensor(f"da{i}", [P, CL], F32)) for i in range(DT)]
        ht_bank = [ctx.enter_context(nc.psum_tensor(f"ht{i}", [P, DI], F32)) for i in range(2)]
        gen_bank = [ctx.enter_context(nc.psum_tensor(f"gen{i}", [P, 512], F32)) for i in range(2)]

        weights_in = sem("weights_in")
        setup = sem("setup")
        a_step = sem("a_step")
        xt_loaded = sem("xt_loaded")
        rows_loaded = sem("rows_loaded")
        full = {True: sem("project_full"), False: sem("close_full")}
        read = {True: sem("project_read"), False: sem("close_read")}
        conv_step = sem("conv_step")
        pad_ready = sem("pad_ready")
        u_ready = sem("u_ready")
        gate_ready = sem("gate_ready")
        soft_step = sem("soft_step")
        delta_ready = sem("delta_ready")
        du_ready = sem("du_ready")
        b_stored = sem("b_stored")
        b_loaded = [sem(f"b_loaded{i}") for i in range(2)]
        dbu_ready = sem("dbu_ready")
        da_ready = sem("da_ready")
        scanned = sem("scanned")
        carried = sem("carried")
        ht_ready = sem("ht_ready")
        summed = sem("summed")
        gated = sem("gated")
        stats_step = sem("stats_step")
        var_ready = sem("var_ready")
        rstd_ready = sem("rstd_ready")
        shift_ready = sem("shift_ready")
        x1_ready = sem("x1_ready")
        x1_stored = sem("x1_stored")
        N_WEIGHTS = 9

        xT_d = a["xT"].rearrange("(k p) t -> p k t", p=P)
        rows_d = a["x"].rearrange("b s d -> (b s) d")
        b_rows = dram["b_rows"]

        def wait_full(eng, c, name):
            eng.wait_ge(full[name in PROJECT], count_of(c, name))

        def wait_read(eng, c, name):
            eng.wait_ge(read[name in PROJECT], count_of(c, name))

        block = ctx.enter_context(nc.Block())

        @block.sync
        def _(sp):
            for dst, src in ((w_in, a["W_in"].rearrange("(k p) n -> p k n", p=P)),
                             (w_x, a["W_x"].rearrange("(k p) n -> p k n", p=P)),
                             (w_dt, a["W_dt"]),
                             (w_out, a["W_out"].rearrange("(k p) n -> p k n", p=P)),
                             (w_rt, a["router_wT"].rearrange("(k p) n -> p k n", p=P)),
                             (w_conv, a["W_conv"].rearrange("(k p) n -> p k n", p=P)),
                             (b_dt, a["b_dt"]),
                             (d_par, a["D_param"]),
                             (a_log, a["A_log"].rearrange("(k p) n -> p k n", p=P))):
                sp.dma_start(dst[:], src).then_inc(weights_in, 16)

            def chunk(c, parity, kind, main):
                def value(x):
                    return x if isinstance(x, int) else sp.snap(x)

                xd_now, o1_now = value(count_of(c, "xd")), value(count_of(c, "o1"))
                used = [value(c * NST + 4 * (g - 1)) for g in range(NST // 4)]
                normalised, rows_of_b = value(c * LT), value(c * 16 + 16)
                token0, token_prev = value(c * CL), value((c - 1) * CL)
                if main:
                    sp.wait_ge(b_stored, rows_of_b)
                if kind != "last":
                    sp.dma_start(xT[:], xT_d[:, :, bass.ds(token0 + CL, CL)]).then_inc(xt_loaded, 16)
                for g in range(NST // 4) if main else ():
                    if kind != "first" or g >= 2:
                        sp.wait_ge(dbu_ready, used[g])
                    src = b_rows[parity:parity + 1, 4 * g:4 * g + 4, :]
                    sp.dma_start(b_all[g % 2][:], src.to_broadcast([P, 4, CL])).then_inc(b_loaded[g % 2], 16)
                if kind != "first":
                    sp.wait_ge(x1_ready, normalised)
                    for dst in (dram["x1"], dram["acc"]):
                        sp.dma_start(dst[bass.ds(token_prev, CL), :].rearrange("(l p) d -> p l d", p=P),
                                     x1[:]).then_inc(x1_stored, 16)
                if main:
                    if kind != "first":
                        sp.wait_ge(read[False], o1_now)
                    sp.dma_start(x_rows[:], rows_d[bass.ds(token0, CL), :].rearrange("(l p) d -> p l d", p=P)
                                 ).then_inc(rows_loaded, 16)
                if kind != "last":
                    sp.wait_ge(read[True], xd_now)
                    sp.dma_start(b_rows[1 - parity, :, :], xdT[RANK:RANK + NST, :]).then_inc(b_stored, 16)

            over_chunks(sp, chunk)
            sp.wait_ge(x1_stored, CHUNKS * 32)

        @block.gpsimd
        def _(pool):
            nc.gpsimd.memset(minus_half[:], -0.5).then_inc(setup, 1)
            pool.wait_ge(setup, 1)

            def chunk(c, parity, kind, main):
                other = 1 - parity
                for n in range(NST):
                    if main:
                        if n == 0:
                            pool.wait_ge(du_ready, c + 1)
                        if n % 4 == 0:
                            pool.wait_ge(b_loaded[n // 4 % 2], c * 32 + n // 8 * 16 + 16)
                        if kind != "first" or n >= 2:
                            pool.wait_ge(scanned, c * 64 + 4 * (n - 1))
                        b_n = b_all[n // 4 % 2][:, n % 4:n % 4 + 1, :].to_broadcast([P, DT, CL])
                        nc.gpsimd.tensor_tensor(dbu[n % 2][:], du[parity][:], b_n, ALU.mult).then_inc(dbu_ready, 1)
                    if n == 1 and kind != "first":
                        pool.wait_ge(summed, c * 64)
                        pool.wait_ge(gate_ready, c)
                        nc.gpsimd.tensor_tensor(yacc[other][:], yacc[other][:], gate[other][:],
                                                ALU.mult).then_inc(gated, 1)
                    if n == 9 and kind != "first":
                        pool.wait_ge(var_ready, c)
                        nc.gpsimd.tensor_tensor(rstd[:], var_eps[:], minus_half[:], ALU.pow).then_inc(rstd_ready, 1)
                    if n == 13 and kind != "last":
                        pool.wait_ge(soft_step, 2 * (c + 2))
                        nc.gpsimd.tensor_tensor(delta[other][:], delta[other][:], tmp[:], ALU.add
                                                ).then_inc(delta_ready, 1)
                        pool.wait_ge(delta_ready, c + 2)
                        nc.gpsimd.tensor_tensor(du[other][:], delta[other][:], u[:], ALU.mult
                                                ).then_inc(du_ready, 1)

            over_chunks(pool, chunk)

        @block.scalar
        def _(act):
            act.wait_ge(weights_in, N_WEIGHTS * 16)
            nc.scalar.activation(a_exp[:], a_log[:], ACT.Exp).then_inc(a_step, 1)
            act.wait_ge(a_step, 1)
            nc.scalar.activation(a_neg[:], a_exp[:], ACT.Copy, scale=-1.0).then_inc(a_step, 1)
            act.wait_ge(a_step, 2)

            def copy_out(c, parity, kind, main, name):
                other = 1 - parity
                bank = gen_bank[bank_of(parity, kind, name)]
                project = name in PROJECT
                wait_full(act, c, name)
                what, j = name.rstrip("0123"), int(name[-1]) if name[-1].isdigit() else 0
                if what == "u":
                    if j == 0:
                        act.wait_ge(pad_ready, c + 2)
                        if main:
                            act.wait_ge(delta_ready, c + 1)
                    nc.scalar.activation(u_pad[:, j, 2:], bank[:], ACT.Copy)
                    last = nc.scalar.activation(tmp[:, j, :], bank[:], ACT.Copy, scale=w_conv[:, j, 2:3])
                elif what == "r":
                    if j == 0 and kind != "first":
                        act.wait_ge(gated, c)
                    last = nc.scalar.activation(gate[other][:, j, :], bank[:], ACT.Copy)
                elif what == "xd":
                    if main:
                        act.wait_ge(b_stored, c * 16 + 16)
                    last = nc.scalar.activation(xdT[:], bank[0:XD, :], ACT.Copy)
                elif what == "cT":
                    if kind != "first":
                        act.wait_ge(summed, c * 64)
                    last = nc.scalar.activation(c_tok[other][:], bank[:, 0:LT * XD].rearrange(
                        "p (l n) -> p l n", l=LT), ACT.Copy)
                elif what == "d":
                    if j == 0:
                        act.wait_ge(u_ready, c + 2)
                    nc.scalar.activation(tmp[:, j, :], bank[:], ACT.Abs, bias=b_dt[:, j:j + 1])
                    last = nc.scalar.activation(delta[other][:, j, :], bank[:], ACT.Relu, bias=b_dt[:, j:j + 1])
                elif what == "ud":
                    last = nc.scalar.activation(yacc[other][:, j, :], bank[:], ACT.Copy)
                elif what == "yT":
                    last = nc.scalar.activation(yT[:, j, :], bank[:], ACT.Copy)
                elif what == "o":
                    last = nc.scalar.activation(resid[:, 2 * j:2 * j + 2, :], bank[:].rearrange(
                        "p (l d) -> p l d", l=2), ACT.Copy)
                elif what == "xt":
                    last = nc.scalar.activation(x1T[:, j, :], bank[:], ACT.Copy)
                else:
                    dst = logits[:, bass.ds((c - 1) * (LT * NE), LT * NE)]
                    last = nc.scalar.activation(dst, bank[:, 0:LT * NE], ACT.Copy)
                last.then_inc(read[project], 1)

            def chunk(c, parity, kind, main):
                other = 1 - parity
                for n in range(NST):
                    for t in range(DT) if main else ():
                        if n == 0 and t == 0:
                            act.wait_ge(delta_ready, c + 1)
                        if kind != "first" or n >= 1:
                            act.wait_ge(scanned, c * 64 + 4 * n + t - 3)
                        nc.scalar.activation(da_bank[t][:], delta[parity][:, t, :], ACT.Exp,
                                             scale=a_neg[:, t, n:n + 1]).then_inc(da_ready, 1)
                    if n == 11 and kind != "first":
                        act.wait_ge(shift_ready, c)
                        for l in range(LT):
                            nc.scalar.activation(x1[:, l, :], resid[:, l, :], ACT.Identity, bias=shift[:, l:l + 1],
                                                 scale=rstd[:, l:l + 1]).then_inc(x1_ready, 1)
                    for name in USES[kind]:
                        if STEP[name] == n - 1:
                            copy_out(c, parity, kind, main, name)
                    if n == 7 and kind != "last":
                        act.wait_ge(conv_step, (c + 2) * 2 * DT)
                        if main:
                            act.wait_ge(du_ready, c + 1)
                        nc.scalar.activation(u[:], tmp[:], ACT.Silu).then_inc(u_ready, 1)
                        wait_read(act, c, "r3")
                        nc.scalar.activation(gate[other][:], gate[other][:], ACT.Silu).then_inc(gate_ready, 1)
                    if n == 12 and kind != "last":
                        wait_read(act, c, "d3")
                        nc.scalar.activation(tmp[:], tmp[:], ACT.Exp, scale=-1.0).then_inc(soft_step, 1)
                        act.wait_ge(soft_step, 2 * (c + 1) + 1)
                        nc.scalar.activation(tmp[:], tmp[:], ACT.Ln, bias=1.0).then_inc(soft_step, 1)
                    if n == 15 and kind != "first":
                        act.wait_ge(x1_stored, c * 32)

            over_chunks(act, chunk)

        @block.vector
        def _(dve):
            dve.wait_ge(weights_in, N_WEIGHTS * 16)
            for t in range(DT):
                nc.vector.tensor_scalar(diag_d[:, t, :], ident[:], d_par[:, t:t + 1], None, ALU.mult
                                        ).then_inc(setup, 1)
            nc.vector.memset(u_pad[:, :, 0:2], 0.0).then_inc(pad_ready, 1)

            def add_state(c, parity, n, l):
                dve.wait_ge(ht_ready, c * 64 + 4 * n + l + 1)
                if n == 0:
                    wait_read(dve, c - 1, f"ud{l}")
                else:
                    dve.wait_ge(summed, c * 64 + 4 * (n - 1) + l + 1)
                nc.vector.scalar_tensor_tensor(
                    out=yacc[parity][:, l, :], in0=ht_bank[l % 2][:],
                    scalar=c_tok[parity][:, l, RANK + NST + n:RANK + NST + n + 1],
                    in1=yacc[parity][:, l, :], op0=ALU.mult, op1=ALU.add).then_inc(summed, 1)

            def chunk(c, parity, kind, main):
                other = 1 - parity
                for n in range(NST):
                    for t in range(DT):
                        if main:
                            dve.wait_ge(da_ready, c * 64 + 4 * n + t + 1)
                            if t == 0:
                                dve.wait_ge(dbu_ready, c * NST + n + 1)
                                if kind != "first" or n >= 2:
                                    dve.wait_ge(ht_ready, c * 64 + 4 * (n - 1))
                                if parity == 1 and n < 2:
                                    dve.wait_ge(carried, (c - 1) * (NST // 2) + NST - 1 + n)
                                if parity == 0 and n >= 2:
                                    dve.wait_ge(carried, c * (NST // 2) + n - 1)
                            initial = carry[:, n, t:t + 1] if parity == 1 else 0.0
                            nc.vector.tensor_tensor_scan(hst[n % 2][:, t, :], da_bank[t][:], dbu[n % 2][:, t, :],
                                                         initial, ALU.mult, ALU.add).then_inc(scanned, 1)
                        if main and n > 0:
                            add_state(c, parity, n - 1, t)
                        if n == 0 and kind != "first":
                            add_state(c - 1, other, NST - 1, t)
                        if t == 1 and (main and parity == 0 and n > 0 or main and parity == 1 and n == 0):
                            m = (n - 1) % NST
                            dve.wait_ge(scanned, c * 64 + 4 * n)
                            nc.vector.tensor_copy(carry[:, m, :], hst[m % 2][:, :, CL - 1]).then_inc(carried, 1)
                    if kind != "last" and n in (3, 4):
                        for t in ((0, 1) if n == 3 else (2, 3)):
                            wait_read(dve, c, f"u{t}")
                            for tap, shifted in ((1, u_pad[:, t, 1:CL + 1]), (0, u_pad[:, t, 0:CL])):
                                if tap == 0:
                                    dve.wait_ge(conv_step, (c + 1) * 2 * DT + 2 * t + 1)
                                nc.vector.scalar_tensor_tensor(
                                    out=tmp[:, t, :], in0=shifted, scalar=w_conv[:, t, tap:tap + 1],
                                    in1=tmp[:, t, :], op0=ALU.mult, op1=ALU.add).then_inc(conv_step, 1)
                    if kind != "last" and n == 5:
                        dve.wait_ge(conv_step, (c + 2) * 2 * DT)
                        if parity == 1:
                            nc.vector.tensor_copy(u_pad[:, :, 0:2], u_pad[:, :, CL:CL + 2]).then_inc(pad_ready, 1)
                        else:
                            nc.vector.memset(u_pad[:, :, 0:2], 0.0).then_inc(pad_ready, 1)
                    if n == 9 and kind != "first":
                        wait_read(dve, c, "o1")
                        for l in range(LT):
                            nc.vector.bn_stats(stats[:, l, :], resid[:, l, :])
                        dve.drain()
                        for l in range(LT):
                            nc.vector.bn_aggr(mean_var[:, l, :], stats[:, l, :]).then_inc(stats_step, 1)
                        dve.wait_ge(stats_step, c * LT)
                        nc.vector.tensor_scalar(var_eps[:], mean_var[:, :, 1], EPS, None, ALU.add).then_inc(var_ready, 1)
                    if n == 10 and kind != "first":
                        dve.wait_ge(rstd_ready, c)
                        nc.vector.scalar_tensor_tensor(out=shift[:], in0=mean_var[:, :, 0], scalar=-1.0, in1=rstd[:],
                                                       op0=ALU.mult, op1=ALU.mult).then_inc(shift_ready, 1)

            over_chunks(dve, chunk)

        @block.tensor
        def _(pe):
            pe.wait_ge(weights_in, N_WEIGHTS * 16)
            pe.wait_ge(setup, 1 + DT)

            def fill(c, parity, kind, name):
                other = 1 - parity
                bank = gen_bank[bank_of(parity, kind, name)]
                before = two_before(c, kind, name)
                if before is not None:
                    wait_read(pe, *before)
                what, j = name.rstrip("0123"), int(name[-1]) if name[-1].isdigit() else 0
                if what == "u":
                    if j == 0:
                        pe.wait_ge(xt_loaded, c * 16 + 32)
                    for k in range(KD):
                        last = nc.tensor.matmul(bank[:], w_in[:, k, j * P:(j + 1) * P], xT[:, k, :],
                                                start=k == 0, stop=k == KD - 1)
                elif what == "r":
                    for k in range(KD):
                        last = nc.tensor.matmul(bank[:], xT[:, k, j * P:(j + 1) * P], w_in[:, k, DI:],
                                                start=k == 0, stop=k == KD - 1)
                elif what == "xd":
                    pe.wait_ge(u_ready, c + 2)
                    for t in range(DT):
                        last = nc.tensor.matmul(bank[0:XD, :], w_x[:, t, :], u[:, t, :], start=t == 0, stop=t == DT - 1)
                elif what == "cT":
                    wait_read(pe, c, "xd")
                    for l in range(LT):
                        last = nc.tensor.matmul(bank[:, l * XD:(l + 1) * XD], xdT[:, l * P:(l + 1) * P],
                                                ident[0:XD, 0:XD], start=True, stop=True)
                elif what == "d":
                    last = nc.tensor.matmul(bank[:], w_dt[:, j * P:(j + 1) * P], xdT[0:RANK, :], start=True, stop=True)
                elif what == "ud":
                    for t in range(DT):
                        last = nc.tensor.matmul(bank[:, t * P:(t + 1) * P], u[:, t, j * P:(j + 1) * P],
                                                diag_d[:, t, :], start=True, stop=True)
                elif what == "yT":
                    if j == 0:
                        pe.wait_ge(gated, c)
                    for l in range(LT):
                        last = nc.tensor.transpose(bank[:, l * P:(l + 1) * P], yacc[other][:, l, j * P:(j + 1) * P],
                                                   ident[:])
                elif what == "o":
                    if j == 0:
                        wait_read(pe, c, "yT3")
                        pe.wait_ge(rows_loaded, c * 16)
                    for l in (2 * j, 2 * j + 1):
                        part = bank[:, l % 2 * DM:(l % 2 + 1) * DM]
                        for t in range(DT):
                            nc.tensor.matmul(part, yT[:, t, l * P:(l + 1) * P], w_out[:, t, :], start=t == 0, stop=False)
                        last = nc.tensor.matmul(part, ident[:], x_rows[:, l, :], start=False, stop=True)
                elif what == "xt":
                    if j == 0:
                        pe.wait_ge(x1_ready, c * LT)
                    for l in range(LT):
                        last = nc.tensor.transpose(bank[:, l * P:(l + 1) * P], x1[:, l, j * P:(j + 1) * P], ident[:])
                else:
                    wait_read(pe, c, "xt1")
                    for l in range(LT):
                        for k in range(KD):
                            last = nc.tensor.matmul(bank[:, l * NE:(l + 1) * NE], x1T[:, k, l * P:(l + 1) * P],
                                                    w_rt[:, k, :], start=k == 0, stop=k == KD - 1)
                last.then_inc(full[name in PROJECT], 1)

            def chunk(c, parity, kind, main):
                for n in range(NST):
                    for l in range(LT) if main else ():
                        if l == 0:
                            pe.wait_ge(scanned, c * 64 + 4 * n + 4)
                        if kind != "first" or n > 0 or l >= 2:
                            pe.wait_ge(summed, c * 64 + 4 * n + l - 1)
                        for t in range(DT):
                            last = nc.tensor.transpose(ht_bank[l % 2][:, t * P:(t + 1) * P],
                                                       hst[n % 2][:, t, l * P:(l + 1) * P], ident[:])
                        last.then_inc(ht_ready, 1)
                    for name in USES[kind]:
                        if STEP[name] == n:
                            fill(c, parity, kind, name)

            over_chunks(pe, chunk)


def make_ident(nc, ident):
    with nc.semaphore("ident_step") as ident_step, nc.Block() as block:
        @block.gpsimd
        def _(pool):
            nc.gpsimd.memset(ident[:], 0.0).then_inc(ident_step, 1)
            pool.wait_ge(ident_step, 1)
            nc.gpsimd.affine_select(out=ident[:], in_=ident[:], compare_op=ALU.not_equal, fill=1.0, base=0,
                                    pattern=[[-1, P]], channel_multiplier=1).then_inc(ident_step, 1)
            pool.wait_ge(ident_step, 2)


def make_constants(nc, k):
    with ExitStack() as ctx:
        f = ctx.enter_context(nc.sbuf_tensor("int_table", [P, P], I32))
        g = ctx.enter_context(nc.sbuf_tensor("same_rest", [P, P], I32))
        h = ctx.enter_context(nc.sbuf_tensor("above", [P, P], F32))
        made = ctx.enter_context(nc.semaphore("tables_made"))
        step = ctx.enter_context(nc.semaphore("masks_step"))
        block = ctx.enter_context(nc.Block())

        @block.gpsimd
        def _(pool):
            exact = {"allow_small_or_imprecise_dtypes": True}
            nc.gpsimd.iota(k["slot_low"][:], [[1, P]], 0, 0, **exact).then_inc(made, 1)
            nc.gpsimd.iota(k["slot_high"][:], [[1, CAP // P]], 0, 0, **exact).then_inc(made, 1)
            nc.gpsimd.iota(k["tile_id"][:], [[1, TILES]], 0, 0, **exact).then_inc(made, 1)
            nc.gpsimd.iota(k["part_id"][:], [[0, 1]], 0, 1, **exact).then_inc(made, 1)
            nc.gpsimd.iota(k["first_wins"][:], [[-1, NE]], NE, 0, **exact).then_inc(made, 1)
            nc.gpsimd.iota(f[:], [[1, P]], P, -1).then_inc(made, 1)
            nc.gpsimd.memset(k["bit"][:], 1 << 29).then_inc(made, 1)
            nc.gpsimd.memset(k["threshold"][:], 0).then_inc(made, 1)
            nc.gpsimd.memset(k["ones"][:], 1.0).then_inc(made, 1)
            pool.wait_ge(made, 9)

        @block.vector
        def _(dve):
            dve.wait_ge(made, 9)
            nc.vector.tensor_scalar(g[:], f[:], NE - 1, None, ALU.bitwise_and).then_inc(step, 1)
            nc.vector.tensor_scalar(h[:], f[:], float(P), None, ALU.is_gt).then_inc(step, 1)
            dve.wait_ge(step, 2)
            nc.vector.tensor_scalar(k["same_expert"][:], g[:], 0.0, None, ALU.is_equal).then_inc(step, 1)
            dve.wait_ge(step, 3)
            nc.vector.tensor_tensor(k["earlier"][:], k["same_expert"][:], h[:], ALU.mult).then_inc(step, 1)
            dve.wait_ge(step, 4)


def route(nc, k, logits, ident):
    with ExitStack() as ctx:
        def sb(name, shape, dt=F32):
            return ctx.enter_context(nc.sbuf_tensor(name, shape, dt))

        def sem(name):
            return ctx.enter_context(nc.semaphore(name))

        full3 = [P, TILES, NE]
        row_max = sb("row_max", [P, TILES, 1])
        shifted = sb("shifted", full3)
        probs = sb("probs", full3)
        row_sum = sb("row_sum", [P, TILES, 1])
        top = [sb(f"top{i}", [P, TILES, 1]) for i in range(2)]
        mask = [sb(f"mask{i}", full3) for i in range(2)]
        equal = sb("equal", full3)
        key = sb("key", full3)
        key_max = sb("key_max", [P, TILES, 1])
        rest = sb("rest", full3)
        weight = [sb(f"weight{i}", [P, TILES, 1]) for i in range(2)]
        fw = sb("fw", full3)
        ft = sb("ft", [P, 4, P])
        flags = sb("flags", [P, 4, P])
        above = sb("above_t", [P, 4, P])
        tied = sb("tied", [P, 4, P])
        rank = sb("rank", [P, 4, P])
        code = sb("code", [P, 4, P])
        count = sb("count", [P, 1])
        candidate = sb("candidate", [P, 1], I32)
        accept = sb("accept", [P, 1], I32)
        need = sb("need", [P, 1])
        seg = sb("seg", [P, 4])
        seg_sum = sb("seg_sum", [P, 4])
        seg_before = sb("seg_before", [P, 4])
        slot = sb("slot", [P, TILES * NE], I32)
        low = sb("low", [P, TILES * NE], I32)
        high = sb("high", [P, TILES * NE], I32)
        left = [sb(f"left{i}", full3) for i in range(2)]
        bank = ctx.enter_context(nc.psum_tensor("flip", [P, 512], F32))
        total = ctx.enter_context(nc.psum_tensor("total", [P, 1], F32))
        before = ctx.enter_context(nc.psum_tensor("before", [P, 4], F32))

        step = sem("route_step")
        shifted_ready = sem("shifted_ready")
        exp_ready = sem("exp_ready")
        fw_ready = sem("fw_ready")
        flipped = sem("flipped")
        counted = sem("counted")
        totalled = sem("totalled")
        segments = sem("segments")
        offsets = sem("offsets")
        code_ready = sem("code_ready")
        BITS = 30
        block = ctx.enter_context(nc.Block())

        @block.scalar
        def _(act):
            act.wait_ge(shifted_ready, 1)
            nc.scalar.activation(probs[:], shifted[:], ACT.Exp).then_inc(exp_ready, 1)

        @block.tensor
        def _(pe):
            pe.wait_ge(fw_ready, 1)
            for g in range(4):
                last = nc.tensor.transpose(bank[:, g * P:(g + 1) * P],
                                           fw[:].rearrange("p t e -> p (t e)")[:, g * P:(g + 1) * P], ident[:])
            last.then_inc(flipped, 1)
            with pe.Fori(0, BITS) as i:
                pe.wait_ge(counted, i + 1)
                nc.tensor.matmul(total[:], k["same_expert"][:], count[:], start=True, stop=True).then_inc(totalled, 1)
            pe.wait_ge(counted, BITS + 1)
            nc.tensor.matmul(total[:], k["same_expert"][:], count[:], start=True, stop=True).then_inc(totalled, 1)
            for i in range(2):
                pe.wait_ge(segments, i + 1)
                nc.tensor.matmul(before[:], k["earlier"][:], seg[:], start=True, stop=False)
                nc.tensor.matmul(before[:], k["same_expert"][:], seg_before[:], start=False, stop=True
                                 ).then_inc(offsets, 1)
            pe.wait_ge(code_ready, 1)
            for g in range(4):
                last = nc.tensor.transpose(bank[:, g * P:(g + 1) * P], code[:, g, :], ident[:])
            last.then_inc(flipped, 1)

        @block.vector
        def _(dve):
            chain = [0]

            def link(ins):
                chain[0] += 1
                ins.then_inc(step, 1)
                dve.wait_ge(step, chain[0])

            v = nc.vector
            lg = logits[:].rearrange("p (t e) -> p t e", e=NE)
            link(v.tensor_reduce(row_max[:], lg, AX.X, ALU.max))
            v.tensor_tensor(shifted[:], lg, row_max[:].to_broadcast(full3), ALU.subtract).then_inc(shifted_ready, 1)
            dve.wait_ge(exp_ready, 1)
            link(v.tensor_reduce(row_sum[:], probs[:], AX.X, ALU.add))
            link(v.reciprocal(row_sum[:], row_sum[:]))
            link(v.tensor_tensor(probs[:], probs[:], row_sum[:].to_broadcast(full3), ALU.mult))
            for i in range(2):
                src = (probs, rest)[i]
                link(v.tensor_reduce(top[i][:], src[:], AX.X, ALU.max))
                link(v.tensor_tensor(equal[:], src[:], top[i][:].to_broadcast(full3), ALU.is_equal))
                link(v.tensor_tensor(key[:], equal[:], k["first_wins"][:].to_broadcast(full3), ALU.mult))
                link(v.tensor_reduce(key_max[:], key[:], AX.X, ALU.max))
                link(v.tensor_tensor(mask[i][:], key[:], key_max[:].to_broadcast(full3), ALU.is_equal))
                if i == 0:
                    link(v.scalar_tensor_tensor(out=rest[:], in0=mask[0][:], scalar=-2.0, in1=probs[:],
                                                op0=ALU.mult, op1=ALU.add))
            link(v.tensor_tensor(row_sum[:], top[0][:], top[1][:], ALU.add))
            link(v.tensor_scalar(row_sum[:], row_sum[:], 1e-6, None, ALU.add))
            link(v.reciprocal(row_sum[:], row_sum[:]))
            for i in range(2):
                link(v.tensor_tensor(weight[i][:], top[i][:], row_sum[:], ALU.mult))
            link(v.tensor_tensor(equal[:], mask[0][:], weight[0][:].to_broadcast(full3), ALU.mult))
            link(v.tensor_tensor(key[:], mask[1][:], weight[1][:].to_broadcast(full3), ALU.mult))
            v.tensor_tensor(fw[:], equal[:], key[:], ALU.add).then_inc(fw_ready, 1)
            dve.wait_ge(fw_ready, 1)
            link(v.tensor_copy(k["part"][0][:], fw[:]))
            link(v.tensor_tensor(left[0][:], fw[:], k["part"][0][:], ALU.subtract))
            link(v.tensor_copy(k["part"][1][:], left[0][:]))
            link(v.tensor_tensor(left[1][:], left[0][:], k["part"][1][:], ALU.subtract))
            link(v.tensor_copy(k["part"][2][:], left[1][:]))
            dve.wait_ge(flipped, 1)
            link(v.tensor_copy(ft[:], bank[:].rearrange("p (g t) -> p g t", g=4)))

            with dve.Fori(0, BITS) as i:
                v.tensor_tensor(candidate[:], k["threshold"][:], k["bit"][:], ALU.bitwise_or).then_inc(step, 1)
                dve.wait_ge(step, i * 4 + chain[0] + 1)
                v.tensor_scalar(flags[:], ft[:], candidate[:].bitcast(F32), None, ALU.is_ge, ALU.add,
                                accum_out=count[:]).then_inc(counted, 1)
                dve.wait_ge(totalled, i + 1)
                v.tensor_scalar(accept[:], total[:], float(CAP), None, ALU.is_ge).then_inc(step, 1)
                dve.wait_ge(step, i * 4 + chain[0] + 2)
                v.tensor_scalar(k["bit"][:], k["bit"][:], 1, None, ALU.logical_shift_right).then_inc(step, 1)
                v.copy_predicated(k["threshold"][:], accept[:], candidate[:]).then_inc(step, 1)
                dve.wait_ge(step, i * 4 + chain[0] + 4)
            chain[0] += 4 * BITS
            limit = k["threshold"][:].bitcast(F32)
            v.tensor_scalar(above[:], ft[:], limit, None, ALU.is_gt, ALU.add, accum_out=count[:]).then_inc(counted, 1)
            link(v.tensor_scalar(tied[:], ft[:], limit, None, ALU.is_equal))
            dve.wait_ge(totalled, BITS + 1)
            link(v.tensor_scalar(need[:], total[:], -1.0, float(CAP), ALU.mult, ALU.add))

            def number(flags_in, i):
                for g in range(4):
                    link(v.tensor_tensor_scan(rank[:, g, :], k["ones"][:], flags_in[:, g, :], 0.0, ALU.mult, ALU.add))
                link(v.tensor_copy(seg[:], rank[:, :, P - 1]))
                link(v.tensor_tensor_scan(seg_sum[:], k["ones"][:, 0:4], seg[:], 0.0, ALU.mult, ALU.add))
                v.tensor_tensor(seg_before[:], seg_sum[:], seg[:], ALU.subtract).then_inc(segments, 1)
                dve.wait_ge(offsets, i + 1)
                for g in range(4):
                    link(v.tensor_scalar(rank[:, g, :], rank[:, g, :], before[:, g:g + 1], None, ALU.add))

            number(tied, 0)
            link(v.scalar_tensor_tensor(out=flags[:], in0=rank[:], scalar=need[:], in1=tied[:],
                                        op0=ALU.is_le, op1=ALU.mult))
            link(v.tensor_tensor(flags[:], flags[:], above[:], ALU.add))
            number(flags, 1)
            v.tensor_tensor(code[:], rank[:], flags[:], ALU.mult).then_inc(code_ready, 1)
            dve.wait_ge(flipped, 2)
            link(v.tensor_scalar(slot[:], bank[:], -1.0, None, ALU.add))
            link(v.tensor_scalar(low[:], slot[:], P - 1, None, ALU.bitwise_and))
            link(v.tensor_scalar(high[:], slot[:], 7, None, ALU.arith_shift_right))
            link(v.tensor_copy(k["low"][:], low[:].rearrange("p (t e) -> p t e", e=NE)))
            link(v.tensor_copy(k["high"][:], high[:].rearrange("p (t e) -> p t e", e=NE)))


ST = CAP // P
SJ = 2
JC = ST // SJ
FT_ = FF // P
NV = 5


def experts(nc, a, k, dram, ident):
    with ExitStack() as ctx:
        def sb(name, shape, dt=F32):
            return ctx.enter_context(nc.sbuf_tensor(name, shape, dt))

        def sem(name):
            return ctx.enter_context(nc.semaphore(name))

        w_gate = [sb(f"w_gate{i}", [P, KD, FF]) for i in range(2)]
        w_up = [sb(f"w_up{i}", [P, KD, FF]) for i in range(2)]
        w_down = [sb(f"w_down{i}", [P, FT_, DM]) for i in range(2)]
        hot_low = sb("hot_low", [P, TILES, P], BF16)
        hot_high = sb("hot_high", [P, TILES, ST], BF16)
        values = sb("values", [P, TILES, NV, ST], BF16)
        lists = sb("lists", [P, NV, ST])
        pair = sb("pair", [P, ST])
        token = [sb(f"token{i}", [P, ST], U32) for i in range(2)]
        share = [sb(f"share{i}", [P, ST]) for i in range(2)]
        xg = sb("xg", [P, ST, DM])
        xgT = [sb(f"xgT{i}", [P, KD, CAP]) for i in range(2)]
        silu = [sb(f"silu{i}", [P, SJ * P]) for i in range(4)]
        hidden = sb("hidden", [P, FT_, CAP])
        eo = [sb(f"eo{i}", [P, ST, DM]) for i in range(2)]
        gu_bank = [ctx.enter_context(nc.psum_tensor(f"gu{i}", [P, 2, SJ * P], F32)) for i in range(4)]
        dn_bank = [ctx.enter_context(nc.psum_tensor(f"dn{i}", [P, SJ, DM], F32)) for i in range(2)]
        tr_bank = [ctx.enter_context(nc.psum_tensor(f"tr{i}", [P, KD, SJ * P], F32)) for i in range(2)]

        weights_loaded = [sem(f"expert_loaded{i}") for i in range(2)]
        hot_ready = sem("hot_ready")
        values_step = sem("values_step")
        listed = sem("listed")
        list_step = sem("list_step")
        token_ready = sem("token_ready")
        share_ready = sem("share_ready")
        gathered = [sem(f"gathered{j}") for j in range(JC)]
        tr_full = sem("tr_full")
        tr_read = sem("tr_read")
        gu_full = sem("gu_full")
        silu_ready = sem("silu_ready")
        hidden_ready = sem("hidden_ready")
        dn_full = sem("dn_full")
        dn_read = sem("dn_read")
        added = sem("added")
        GU, QT = JC * FT_, TILES // 4

        x1_d, acc_d = dram["x1"], dram["acc"]

        def over_experts(eng, emit):
            emit(-1, 1, "start")
            emit(0, 0, "mid0")
            with eng.Fori(0, (NE - 2) // 2) as i:
                emit(i * 2 + 1, 1, "mid")
                emit(i * 2 + 2, 0, "mid")
            emit(NE - 1, 1, "end")

        block = ctx.enter_context(nc.Block())

        @block.sync
        def _(sp):
            def expert(e, par, kind):
                if kind == "end":
                    return
                nxt = 1 - par
                if kind == "mid":
                    sp.wait_ge(dn_read, e * JC)
                row = (e + 1) * DM
                sp.dma_start(w_gate[nxt][:], a["wg"].rearrange("e d f -> (e d) f")[bass.ds(row, DM), :]
                             .rearrange("(k p) f -> p k f", p=P)).then_inc(weights_loaded[nxt], 16)
                sp.dma_start(w_up[nxt][:], a["wu"].rearrange("e d f -> (e d) f")[bass.ds(row, DM), :]
                             .rearrange("(k p) f -> p k f", p=P)).then_inc(weights_loaded[nxt], 16)
                sp.dma_start(w_down[nxt][:], a["wd"].rearrange("e f d -> (e f) d")[bass.ds((e + 1) * FF, FF), :]
                             .rearrange("(k p) d -> p k d", p=P)).then_inc(weights_loaded[nxt], 16)

            over_experts(sp, expert)

        @block.gpsimd
        def _(pool):
            def gather(e_next, par):
                pool.wait_ge(token_ready, e_next + 1)
                for s in range(ST):
                    nc.gpsimd.indirect_dma_start(
                        out=xg[:, s, :], out_offset=None, in_=x1_d,
                        in_offset=bass.IndirectOffsetOnAxis(ap=token[par][:, s:s + 1], axis=0),
                        bounds_check=TOK - 1).then_inc(gathered[s // SJ], 16)

            def expert(e, par, kind):
                if kind == "start":
                    gather(0, 0)
                    return
                for j in range(JC):
                    if j == 2 and kind != "end":
                        pool.wait_ge(tr_read, (e + 1) * JC)
                        gather(e + 1, 1 - par)
                    pool.wait_ge(dn_read, e * JC + j + 1)
                    if j == 0 and kind != "mid0":
                        pool.wait_ge(added, e * (ST * 16))
                    for s in range(j * SJ, (j + 1) * SJ):
                        nc.gpsimd.indirect_dma_start(
                            out=acc_d, out_offset=bass.IndirectOffsetOnAxis(ap=token[par][:, s:s + 1], axis=0),
                            in_=eo[par][:, s, :], in_offset=None, bounds_check=TOK - 1,
                            compute_op=ALU.add).then_inc(added, 16)

            expert(-1, 1, "start")
            for e in range(NE):
                expert(e, e % 2, "mid0" if e == 0 else "end" if e == NE - 1 else "mid")
            pool.wait_ge(added, NE * ST * 16)

        @block.vector
        def _(dve):
            v = nc.vector

            def prepare(e, par, first):
                if not first:
                    dve.wait_ge(listed, e)
                v.tensor_tensor(hot_high[:], k["high"][:, :, bass.ds(e, 1)].to_broadcast([P, TILES, ST]),
                                k["slot_high"][:].to_broadcast([P, TILES, ST]), ALU.is_equal).then_inc(values_step, 1)
                dve.wait_ge(values_step, e * (NV + 1) + 1)
                sources = [k["tile_id"][:], k["part_id"][:].to_broadcast([P, TILES, 1])] + \
                          [k["part"][i][:, :, bass.ds(e, 1)] for i in range(3)]
                for n, src in enumerate(sources):
                    v.tensor_tensor(values[:, :, n, :], hot_high[:], src.to_broadcast([P, TILES, ST]),
                                    ALU.mult).then_inc(values_step, 1)
                for q in range(4):
                    part = slice(q * QT, (q + 1) * QT)
                    v.tensor_tensor(hot_low[:, part, :], k["low"][:, part, bass.ds(e, 1)].to_broadcast([P, QT, P]),
                                    k["slot_low"][:].to_broadcast([P, QT, P]), ALU.is_equal).then_inc(hot_ready, 1)

            def read_lists(e, par, first):
                dve.wait_ge(listed, e + 1)
                v.tensor_copy(lists[:], tr_bank[0][:].rearrange("p k s -> p (k s)")[:, 0:NV * ST].rearrange(
                    "p (v s) -> p v s", v=NV)).then_inc(list_step, 1)
                dve.wait_ge(list_step, e * 2 + 1)
                if not first:
                    dve.wait_ge(added, (e - 1) * (ST * 16))
                v.scalar_tensor_tensor(out=token[par][:], in0=lists[:, 0, :], scalar=float(P), in1=lists[:, 1, :],
                                       op0=ALU.mult, op1=ALU.add).then_inc(token_ready, 1)
                v.tensor_tensor(pair[:], lists[:, 2, :], lists[:, 3, :], ALU.add).then_inc(list_step, 1)
                dve.wait_ge(list_step, e * 2 + 2)
                if not first:
                    dve.wait_ge(dn_read, (e - 1) * JC)
                v.tensor_tensor(share[par][:], pair[:], lists[:, 4, :], ALU.add).then_inc(share_ready, 1)

            def expert(e, par, kind):
                if kind == "start":
                    prepare(0, 0, True)
                    read_lists(0, 0, True)
                    return
                for n in range(GU):
                    j, f = divmod(n, FT_)
                    dve.wait_ge(silu_ready, e * GU + n + 1)
                    v.tensor_tensor(hidden[:, f, j * SJ * P:(j + 1) * SJ * P], silu[n % 4][:], gu_bank[n % 4][:, 1, :],
                                    ALU.mult).then_inc(hidden_ready, 1)
                    if n == 2 and kind != "end":
                        prepare(e + 1, 1 - par, False)
                    if n == 2 * FT_ and kind != "end":
                        read_lists(e + 1, 1 - par, kind == "mid0")

            over_experts(dve, expert)

        order = []
        for j in range(JC):
            for f in range(FT_):
                order.append(("gu", j * FT_ + f))
                if f == 1 and j:
                    order.append(("dn", j - 1))
                if (j, f) == (1, FT_ - 1):
                    order.append(("list", 0))
                if j == JC - 1 and f in (3, 4, 5, 6):
                    order.append(("tr", f - 3))
        order += [("tr", JC - 1), ("dn", JC - 1)]

        @block.scalar
        def _(act):
            def take_transposed(e, par, j):
                act.wait_ge(tr_full, e * JC + j + 1)
                nc.scalar.activation(xgT[par][:, :, j * SJ * P:(j + 1) * SJ * P], tr_bank[j % 2][:],
                                     ACT.Copy).then_inc(tr_read, 1)

            def expert(e, par, kind):
                if kind == "start":
                    for j in range(JC):
                        take_transposed(0, 0, j)
                    return
                for what, n in order:
                    if what == "gu":
                        act.wait_ge(gu_full, e * GU + n + 1)
                        if kind != "mid0" or n >= 4:
                            act.wait_ge(hidden_ready, e * GU + n - 3)
                        nc.scalar.activation(silu[n % 4][:], gu_bank[n % 4][:, 0, :], ACT.Silu).then_inc(silu_ready, 1)
                    elif what == "dn":
                        act.wait_ge(dn_full, e * JC + n + 1)
                        if n == 0:
                            act.wait_ge(share_ready, e + 1)
                            if kind != "mid0":
                                act.wait_ge(added, e * (ST * 16))
                        for s in range(SJ):
                            last = nc.scalar.activation(eo[par][:, n * SJ + s, :], dn_bank[n % 2][:, s, :], ACT.Copy,
                                                        scale=share[par][:, n * SJ + s:n * SJ + s + 1])
                        last.then_inc(dn_read, 1)
                    elif what == "tr" and kind != "end":
                        take_transposed(e + 1, 1 - par, n)

            over_experts(act, expert)

        @block.tensor
        def _(pe):
            def make_list(e):
                pe.wait_ge(values_step, (e + 1) * (NV + 1))
                for t in range(TILES):
                    if t % QT == 0:
                        pe.wait_ge(hot_ready, e * 4 + t // QT + 1)
                    last = nc.tensor.matmul(tr_bank[0][:].rearrange("p k s -> p (k s)")[:, 0:NV * ST],
                                            hot_low[:, t, :], values[:, t, :, :].rearrange("p v s -> p (v s)"),
                                            start=t == 0, stop=t == TILES - 1)
                last.then_inc(listed, 1)

            def transpose(e, j, first):
                pe.wait_ge(gathered[j], (e + 1) * (SJ * 16))
                if j == 0:
                    pe.wait_ge(token_ready, e + 1)
                if j >= 2:
                    pe.wait_ge(tr_read, e * JC + j - 1)
                for kk in range(KD):
                    for s in range(SJ):
                        last = nc.tensor.transpose(tr_bank[j % 2][:, kk, s * P:(s + 1) * P],
                                                   xg[:, j * SJ + s, kk * P:(kk + 1) * P], ident[:])
                last.then_inc(tr_full, 1)

            def expert(e, par, kind):
                if kind == "start":
                    make_list(0)
                    for j in range(JC):
                        transpose(0, j, True)
                    return
                for what, n in order:
                    if what == "gu":
                        j, f = divmod(n, FT_)
                        if n == 0:
                            pe.wait_ge(weights_loaded[par], (e - par) * 24 + 48)
                        if f == 0:
                            pe.wait_ge(tr_read, e * JC + j + 1)
                        if kind != "mid0" or n >= 4:
                            pe.wait_ge(hidden_ready, e * GU + n - 3)
                        for i, w in enumerate((w_gate, w_up)):
                            for kk in range(KD):
                                last = nc.tensor.matmul(gu_bank[n % 4][:, i, :], w[par][:, kk, f * P:(f + 1) * P],
                                                        xgT[par][:, kk, j * SJ * P:(j + 1) * SJ * P],
                                                        start=kk == 0, stop=kk == KD - 1)
                        last.then_inc(gu_full, 1)
                    elif what == "dn":
                        pe.wait_ge(hidden_ready, e * GU + (n + 1) * FT_)
                        if kind != "mid0" or n >= 2:
                            pe.wait_ge(dn_read, e * JC + n - 1)
                        for s in range(SJ):
                            for f in range(FT_):
                                last = nc.tensor.matmul(dn_bank[n % 2][:, s, :],
                                                        hidden[:, f, (n * SJ + s) * P:(n * SJ + s + 1) * P],
                                                        w_down[par][:, f, :], start=f == 0, stop=f == FT_ - 1)
                        last.then_inc(dn_full, 1)
                    elif what == "list" and kind != "end":
                        pe.wait_ge(tr_read, (e + 1) * JC)
                        make_list(e + 1)
                    elif what == "tr" and kind != "end":
                        transpose(e + 1, n, False)

            over_experts(pe, expert)


def last_norm(nc, dram, out):
    G = 4
    N = TILES // G
    with ExitStack() as ctx:
        def sb(name, shape, dt=F32):
            return ctx.enter_context(nc.sbuf_tensor(name, shape, dt))

        def sem(name):
            return ctx.enter_context(nc.semaphore(name))

        rows = [sb(f"rows{i}", [P, G, DM]) for i in range(4)]
        stats = [sb(f"stats{i}", [P, G, 6]) for i in range(4)]
        mean_var = [sb(f"mean_var{i}", [P, G, 2]) for i in range(4)]
        var_eps = [sb(f"var_eps{i}", [P, G]) for i in range(4)]
        rstd = [sb(f"rstd{i}", [P, G]) for i in range(4)]
        shift = [sb(f"shift{i}", [P, G]) for i in range(4)]
        minus_half = sb("minus_half2", [P, G])
        loaded = [sem(f"rows_in{i}") for i in range(4)]
        const_ready = sem("minus_half_ready")
        aggregated = sem("aggregated")
        var_ready = sem("var_ready2")
        rstd_ready = sem("rstd_ready2")
        shift_ready = sem("shift_ready2")
        normed = sem("normed")
        stored = [sem(f"stored{i}") for i in range(4)]
        acc_d = dram["acc"]
        out_d = out.rearrange("b s d -> (b s) d")
        block = ctx.enter_context(nc.Block())

        @block.sync
        def _(sp):
            for i in range(4):
                sp.dma_start(rows[i][:], acc_d[i * G * P:(i + 1) * G * P, :].rearrange("(g p) d -> p g d", p=P)
                             ).then_inc(loaded[i], 16)
            with sp.Fori(0, N // 4 - 1) as r:
                for i in range(4):
                    sp.wait_ge(stored[i], r * 16 + 16)
                    sp.dma_start(rows[i][:], acc_d[bass.ds((r * 4 + (4 + i)) * (G * P), G * P), :].rearrange(
                        "(g p) d -> p g d", p=P)).then_inc(loaded[i], 16)

        @block.vector
        def _(dve):
            with dve.Fori(0, N // 4) as r:
                for i in range(4):
                    n = r * 4 + i
                    dve.wait_ge(loaded[i], r * 16 + 16)
                    for g in range(G):
                        nc.vector.bn_stats(stats[i][:, g, :], rows[i][:, g, :])
                    dve.drain()
                    for g in range(G):
                        nc.vector.bn_aggr(mean_var[i][:, g, :], stats[i][:, g, :]).then_inc(aggregated, 1)
                    dve.wait_ge(aggregated, n * G + G)
                    nc.vector.tensor_scalar(var_eps[i][:], mean_var[i][:, :, 1], EPS, None, ALU.add).then_inc(var_ready, 1)
                    dve.wait_ge(rstd_ready, n + 1)
                    nc.vector.scalar_tensor_tensor(out=shift[i][:], in0=mean_var[i][:, :, 0], scalar=-1.0, in1=rstd[i][:],
                                                   op0=ALU.mult, op1=ALU.mult).then_inc(shift_ready, 1)

        @block.gpsimd
        def _(pool):
            nc.gpsimd.memset(minus_half[:], -0.5).then_inc(const_ready, 1)
            pool.wait_ge(const_ready, 1)
            with pool.Fori(0, N // 4) as r:
                for i in range(4):
                    pool.wait_ge(var_ready, r * 4 + (i + 1))
                    nc.gpsimd.tensor_tensor(rstd[i][:], var_eps[i][:], minus_half[:], ALU.pow).then_inc(rstd_ready, 1)

        @block.scalar
        def _(act):
            with act.Fori(0, N // 4) as r:
                for i in range(4):
                    n = r * 4 + i
                    act.wait_ge(shift_ready, n + 1)
                    for g in range(G):
                        nc.scalar.activation(rows[i][:, g, :], rows[i][:, g, :], ACT.Identity, bias=shift[i][:, g:g + 1],
                                             scale=rstd[i][:, g:g + 1]).then_inc(normed, 1)
                    act.wait_ge(normed, n * G + G)
                    act.dma_start(out_d[bass.ds(n * (G * P), G * P), :].rearrange("(g p) d -> p g d", p=P), rows[i][:]
                                  ).then_inc(stored[i], 16)
            for i in range(4):
                act.wait_ge(stored[i], N // 4 * 16)


def build(nc, a, out):
    with ExitStack() as ctx:
        def sb(name, shape, dt=F32):
            return ctx.enter_context(nc.sbuf_tensor(name, shape, dt))

        dram = {"b_rows": nc.dram_tensor("b_rows", [2, NST, CL], F32, kind="Internal").ap(),
                "x1": nc.dram_tensor("x1_dram", [TOK, DM], F32, kind="Internal").ap(),
                "acc": nc.dram_tensor("acc_dram", [TOK, DM], F32, kind="Internal").ap()}
        ident = sb("ident", [P, P])
        logits = sb("logits", [P, TILES * NE])
        make_ident(nc, ident)
        attention(nc, a, dram, logits, ident)
        k = {
            "slot_low": sb("slot_low", [P, 1, P], BF16),
            "slot_high": sb("slot_high", [P, 1, CAP // P], BF16),
            "tile_id": sb("tile_id", [P, TILES, 1], BF16),
            "part_id": sb("part_id", [P, 1, 1], BF16),
            "first_wins": sb("first_wins", [P, 1, NE]),
            "bit": sb("bit", [P, 1], I32),
            "threshold": sb("threshold", [P, 1], I32),
            "ones": sb("ones", [P, P]),
            "same_expert": sb("same_expert", [P, P]),
            "earlier": sb("earlier", [P, P]),
            "low": sb("slot_low_of", [P, TILES, NE], BF16),
            "high": sb("slot_high_of", [P, TILES, NE], BF16),
            "part": [sb(f"fw_part{i}", [P, TILES, NE], BF16) for i in range(3)],
        }
        make_constants(nc, k)
        route(nc, k, logits, ident)
        experts(nc, a, k, dram, ident)
        last_norm(nc, dram, out)


def kernel(**inputs):
    import numpy as np
    import concourse.bacc as bacc
    from concourse.bass_utils import run_bass_kernel_spmd

    nc = bacc.Bacc("TRN2", target_bir_lowering=False, num_devices=1)
    g = {k.replace("L0_attn_", "").replace("L0_ffn_", ""): np.asarray(v) for k, v in inputs.items()}
    laid = {
        "x": g["x"], "xT": g["x"].reshape(TOK, DM).T, "W_in": g["W_in"], "W_conv": g["W_conv"], "W_x": g["W_x"],
        "W_dt": g["W_dt"], "b_dt": g["b_dt"].reshape(DT, P).T, "D_param": g["D_param"].reshape(DT, P).T,
        "A_log": g["A_log"], "W_out": g["W_out"], "router_wT": g["router_w"].T,
        "wg": g["wg"], "wu": g["wu"], "wd": g["wd"],
    }
    laid = {k: np.ascontiguousarray(v) for k, v in laid.items()}
    aps = {k: nc.dram_tensor(f"in_{k}", v.shape, mybir.dt.from_np(v.dtype), kind="ExternalInput").ap()
           for k, v in laid.items()}
    out = nc.dram_tensor("out", (BATCH, SEQ, DM), F32, kind="ExternalOutput").ap()
    build(nc, aps, out)
    ran = run_bass_kernel_spmd(nc, [{f"in_{k}": v for k, v in laid.items()}], core_ids=[0])
    return ran.results[0]["out"]
```

```python
from contextlib import ExitStack

import concourse.bass as bass
from concourse import mybir

F32 = mybir.dt.float32
F32R = mybir.dt.float32r
BF16 = mybir.dt.bfloat16
I32 = mybir.dt.int32
U32 = mybir.dt.uint32
ACT = mybir.ActivationFunctionType
ALU = mybir.AluOpType
AX = mybir.AxisListType

P = 128
BATCH, SEQ, DM = 8, 1024, 256
TOK = BATCH * SEQ
DI, NST, RANK = 512, 16, 16
XD = RANK + 2 * NST
CL = 512
CHUNKS = TOK // CL
DT = DI // P
LT = CL // P
KD = DM // P
TILES = TOK // P
EPS = 1e-5
HIGH_BITS = -1 << 12
EXP_AND_LOG = "natural_log_exp_and_others"
NE, FF = 8, 1024
CAP = max(1, int(1.25 * TOK / NE))

PROJECT = [f"u{t}" for t in range(DT)] + [f"r{l}" for l in range(LT)] + ["xd", "cT"] + \
          [f"d{t}" for t in range(DT)] + [f"ud{l}" for l in range(LT)]
CLOSE = [f"yT{t}" for t in range(DT)] + ["o0", "o1", "xt0", "xt1", "lg"]
SLOT = {"u0": (0, 2), "u1": (2, 2), "u2": (4, 2), "u3": (6, 2), "r0": (7, 2), "r1": (9, 2), "yT0": (14, 1), "yT1": (15, 1), "xd": (18, 4), "yT2": (19, 1), "yT3": (22, 1), "d0": (23, 1), "d1": (24, 1), "d2": (26, 1), "d3": (27, 1), "cT": (29, 1), "o0": (30, 5), "o1": (35, 5), "r2": (38, 2), "r3": (42, 2), "ud0": (44, 1), "ud1": (45, 1), "xt0": (47, 1), "xt1": (48, 1), "lg": (50, 4), "ud2": (51, 1), "ud3": (55, 1)}
SLOTS = NST * DT
READ_BEHIND = 8
READ_SLOT = {name: min(first + parts - 1 + READ_BEHIND, SLOTS - 1) for name, (first, parts) in SLOT.items()}
USES = {"first": [n for n in SLOT if n in PROJECT],
        "mid": list(SLOT),
        "last": [n for n in SLOT if n in CLOSE]}

DBU = [n % 3 for n in range(NST - 1)] + [1]
DBU_BACK = [next(k for k in range(1, NST) if DBU[(n - k) % NST] == DBU[n]) for n in range(NST)]
BG = 2
GROUPS = NST // BG

DELTA_AT = (11, 11, 12, 12)
DU_AT = (13, 13, 14, 15)
RSTD_AT = 13

SILU_U_SLOT, SILU_GATE_SLOT, SOFT_SLOTS, NORM_SLOT = 20, 1, (38, 41), 53
CONV_SLOT = {8 + 2 * t + step: (t, 1 - step) for t in range(DT) for step in range(2)}
HISTORY_SLOT, STATS_SLOT = 18, (40, 46)


def count_of(c, name):
    if name in PROJECT:
        return (c + 1) * len(PROJECT) + [n for n in SLOT if n in PROJECT].index(name) + 1
    return (c - 1) * len(CLOSE) + [n for n in SLOT if n in CLOSE].index(name) + 1


def bank_of(parity, kind, name):
    k = USES[kind].index(name)
    swapped = {"first": 0, "mid": 1 - parity, "last": 1 - parity}[kind]
    return (k + swapped) % 2


def two_before(c, kind, name):
    k = USES[kind].index(name)
    if k >= 2:
        return c, USES[kind][k - 2]
    if kind == "first" and isinstance(c, int) and c < 0:
        return None
    before = USES["last"] if kind == "last" and isinstance(c, int) and c == CHUNKS else USES["first"]
    return c - 1, before[k - 2]


def over_chunks(eng, emit):
    emit(-1, 1, "first", False)
    emit(0, 0, "first", True)
    with eng.Fori(0, (CHUNKS - 2) // 2) as i:
        emit(i * 2 + 1, 1, "mid", True)
        emit(i * 2 + 2, 0, "mid", True)
    emit(CHUNKS - 1, 1, "last", True)
    emit(CHUNKS, 0, "last", False)


def attention(nc, a, dram, logits, ident):
    with ExitStack() as ctx:
        def sb(name, shape, dt=F32):
            return ctx.enter_context(nc.sbuf_tensor(name, shape, dt))

        def sem(name):
            return ctx.enter_context(nc.semaphore(name))

        w_in = sb("w_in", [P, KD, 2 * DI])
        w_x = sb("w_x", [P, DT, XD])
        w_dt = sb("w_dt", [RANK, DI])
        w_out = sb("w_out", [P, DT, DM])
        w_rt = sb("w_rt", [P, KD, NE])
        w_conv = sb("w_conv", [P, DT, 3])
        b_dt = sb("b_dt", [P, DT])
        d_par = sb("d_par", [P, DT])
        a_log = sb("a_log", [P, DT, NST])
        a_exp = sb("a_exp", [P, DT, NST])
        a_neg = sb("a_neg", [P, DT, NST])
        diag_d = sb("diag_d", [P, DT, P])
        xT = sb("xT", [P, KD, CL])
        x_rows = sb("x_rows", [P, LT, DM])
        u_pad = sb("u_pad", [P, DT, CL + 2])
        tmp = sb("tmp", [P, DT, CL])
        u = sb("u", [P, DT, CL])
        gate = [sb(f"gate{i}", [P, LT, DI]) for i in range(2)]
        delta = [sb(f"delta{i}", [P, DT, CL]) for i in range(2)]
        du = [sb(f"du{i}", [P, DT, CL]) for i in range(2)]
        xdT = sb("xdT", [XD, CL])
        c_tok = [sb(f"c_tok{i}", [P, LT, XD]) for i in range(2)]
        yacc = [sb(f"yacc{i}", [P, LT, DI]) for i in range(2)]
        b_all = [sb(f"b_all{i}", [P, BG, CL]) for i in range(2)]
        dbu = [sb(f"dbu{i}", [P, DT, CL]) for i in range(3)]
        hst = [sb(f"hst{i}", [P, DT, CL]) for i in range(2)]
        carry = sb("carry", [P, NST, DT])
        yT = sb("yT", [P, DT, CL])
        resid = sb("resid", [P, LT, DM])
        x1 = sb("x1", [P, LT, DM])
        x1T = sb("x1T", [P, KD, CL])
        stats = sb("stats", [P, LT, 6])
        mean_var = sb("mean_var", [P, LT, 2])
        var_eps = sb("var_eps", [P, LT])
        minus_mean = sb("minus_mean", [P, LT])
        minus_half = sb("minus_half", [P, LT])
        rstd = sb("rstd", [P, LT])
        shift = sb("shift", [P, LT])
        da_bank = [ctx.enter_context(nc.psum_tensor(f"da{i}", [P, CL], F32)) for i in range(DT)]
        ht_bank = [ctx.enter_context(nc.psum_tensor(f"ht{i}", [P, DI], F32)) for i in range(2)]
        gen_bank = [ctx.enter_context(nc.psum_tensor(f"gen{i}", [P, 512], F32)) for i in range(2)]

        weights_in = sem("weights_in")
        setup = sem("setup")
        a_step = sem("a_step")
        xt_loaded = sem("xt_loaded")
        rows_loaded = sem("rows_loaded")
        full = {True: sem("project_full"), False: sem("close_full")}
        read = {True: sem("project_read"), False: sem("close_read")}
        conv_step = sem("conv_step")
        pad_ready = sem("pad_ready")
        u_ready = sem("u_ready")
        gate_ready = sem("gate_ready")
        soft_step = sem("soft_step")
        delta_ready = sem("delta_ready")
        du_ready = sem("du_ready")
        b_stored = sem("b_stored")
        b_loaded = [sem(f"b_loaded{i}") for i in range(2)]
        dbu_ready = sem("dbu_ready")
        da_ready = sem("da_ready")
        scanned = sem("scanned")
        carried = sem("carried")
        ht_ready = sem("ht_ready")
        summed = sem("summed")
        gated = sem("gated")
        stats_step = sem("stats_step")
        var_ready = sem("var_ready")
        rstd_ready = sem("rstd_ready")
        shift_ready = sem("shift_ready")
        x1_ready = sem("x1_ready")
        x1_stored = sem("x1_stored")
        N_WEIGHTS = 9

        xT_d = a["xT"].rearrange("(k p) t -> p k t", p=P)
        rows_d = a["x"].rearrange("b s d -> (b s) d")
        b_rows = dram["b_rows"]

        def wait_full(eng, c, name):
            eng.wait_ge(full[name in PROJECT], count_of(c, name))

        def wait_read(eng, c, name):
            eng.wait_ge(read[name in PROJECT], count_of(c, name))

        block = ctx.enter_context(nc.Block())

        @block.sync
        def _(sp):
            for dst, src in ((w_in, a["W_in"].rearrange("(k p) n -> p k n", p=P)),
                             (w_x, a["W_x"].rearrange("(k p) n -> p k n", p=P)),
                             (w_dt, a["W_dt"]),
                             (w_out, a["W_out"].rearrange("(k p) n -> p k n", p=P)),
                             (w_rt, a["router_wT"].rearrange("(k p) n -> p k n", p=P)),
                             (w_conv, a["W_conv"].rearrange("(k p) n -> p k n", p=P)),
                             (b_dt, a["b_dt"]),
                             (d_par, a["D_param"]),
                             (a_log, a["A_log"].rearrange("(k p) n -> p k n", p=P))):
                sp.dma_start(dst[:], src).then_inc(weights_in, 16)

            def chunk(c, parity, kind, main):
                def value(x):
                    return x if isinstance(x, int) else sp.snap(x)

                xd_now, o1_now = value(count_of(c, "xd")), value(count_of(c, "o1"))
                used = [value(c * NST + BG * (g - 1)) for g in range(GROUPS)]
                normalised, rows_of_b = value(c * LT), value(c * 16 + 16)
                token0, token_prev = value(c * CL), value((c - 1) * CL)
                if main:
                    sp.wait_ge(b_stored, rows_of_b)
                if kind != "last":
                    sp.dma_start(xT[:], xT_d[:, :, bass.ds(token0 + CL, CL)]).then_inc(xt_loaded, 16)
                for g in range(GROUPS):
                    if g == GROUPS - 1 and kind != "last":
                        sp.wait_ge(read[True], xd_now)
                        sp.dma_start(b_rows[1 - parity, :, :], xdT[RANK:RANK + NST, :]).then_inc(b_stored, 16)
                    if main:
                        if kind != "first" or g >= 2:
                            sp.wait_ge(dbu_ready, used[g])
                        src = b_rows[parity:parity + 1, BG * g:BG * (g + 1), :]
                        sp.dma_start(b_all[g % 2][:], src.to_broadcast([P, BG, CL])).then_inc(b_loaded[g % 2], 16)
                if kind != "first":
                    sp.wait_ge(x1_ready, normalised)
                    for dst in (dram["x1"], dram["acc"]):
                        sp.dma_start(dst[bass.ds(token_prev, CL), :].rearrange("(l p) d -> p l d", p=P),
                                     x1[:]).then_inc(x1_stored, 16)
                if main:
                    if kind != "first":
                        sp.wait_ge(read[False], o1_now)
                    sp.dma_start(x_rows[:], rows_d[bass.ds(token0, CL), :].rearrange("(l p) d -> p l d", p=P)
                                 ).then_inc(rows_loaded, 16)
                if kind == "first":
                    sp.wait_ge(read[True], count_of(c, "r3"))

            over_chunks(sp, chunk)
            sp.wait_ge(x1_stored, CHUNKS * 32)

        @block.gpsimd
        def _(pool):
            nc.gpsimd.memset(minus_half[:], -0.5).then_inc(setup, 1)
            pool.wait_ge(setup, 1)

            def chunk(c, parity, kind, main):
                other = 1 - parity
                for n in range(NST):
                    if main:
                        if n == 0:
                            pool.wait_ge(du_ready, (c + 1) * DT)
                        if n % BG == 0:
                            pool.wait_ge(b_loaded[n // BG % 2], c * (GROUPS * 8) + n // (2 * BG) * 16 + 16)
                        if kind != "first" or n >= 3:
                            pool.wait_ge(scanned, c * 64 + 4 * (n - DBU_BACK[n]) + 4)
                        b_n = b_all[n // BG % 2][:, n % BG:n % BG + 1, :].to_broadcast([P, DT, CL])
                        nc.gpsimd.tensor_tensor(dbu[DBU[n]][:], du[parity][:], b_n, ALU.mult).then_inc(dbu_ready, 1)
                    for l in range(LT):
                        if n == 1 + l and kind != "first":
                            pool.wait_ge(summed, (c - 1) * 64 + 61 + l)
                            if l == 0:
                                pool.wait_ge(gate_ready, c)
                            nc.gpsimd.tensor_tensor(yacc[other][:, l, :], yacc[other][:, l, :], gate[other][:, l, :],
                                                    ALU.mult).then_inc(gated, 1)
                    if n == RSTD_AT and kind != "first":
                        pool.wait_ge(var_ready, c)
                        nc.gpsimd.tensor_tensor(rstd[:], var_eps[:], minus_half[:], ALU.pow).then_inc(rstd_ready, 1)
                        pool.wait_ge(rstd_ready, c)
                        nc.gpsimd.tensor_tensor(shift[:], minus_mean[:], rstd[:], ALU.mult).then_inc(shift_ready, 1)
                    for t in range(DT):
                        if n == DELTA_AT[t] and kind != "last":
                            if t == 0:
                                pool.wait_ge(soft_step, 2 * (c + 2))
                            nc.gpsimd.tensor_tensor(delta[other][:, t, :], delta[other][:, t, :], tmp[:, t, :],
                                                    ALU.add).then_inc(delta_ready, 1)
                    for t in range(DT):
                        if n == DU_AT[t] and kind != "last":
                            pool.wait_ge(delta_ready, (c + 1) * DT + t + 1)
                            nc.gpsimd.tensor_tensor(du[other][:, t, :], delta[other][:, t, :], u[:, t, :], ALU.mult
                                                    ).then_inc(du_ready, 1)

            over_chunks(pool, chunk)

        @block.scalar
        def _(act):
            act.wait_ge(weights_in, N_WEIGHTS * 16)
            nc.scalar.activation(a_exp[:], a_log[:], ACT.Exp).then_inc(a_step, 1)
            act.wait_ge(a_step, 1)
            nc.scalar.activation(a_neg[:], a_exp[:], ACT.Copy, scale=-1.0).then_inc(a_step, 1)
            act.wait_ge(a_step, 2)
            nc.scalar.preload_act_table_set(EXP_AND_LOG)

            def copy_out(c, parity, kind, main, name):
                other = 1 - parity
                bank = gen_bank[bank_of(parity, kind, name)]
                project = name in PROJECT
                wait_full(act, c, name)
                what, j = name.rstrip("0123"), int(name[-1]) if name[-1].isdigit() else 0
                if what == "u":
                    if j == 0:
                        act.wait_ge(pad_ready, c + 2)
                        if main:
                            act.wait_ge(delta_ready, (c + 1) * DT)
                    nc.scalar.activation(u_pad[:, j, 2:], bank[:], ACT.Copy)
                    last = nc.scalar.activation(tmp[:, j, :], bank[:], ACT.Copy, scale=w_conv[:, j, 2:3])
                elif what == "r":
                    if kind != "first":
                        act.wait_ge(gated, (c - 1) * LT + j + 1)
                    last = nc.scalar.activation(gate[other][:, j, :], bank[:], ACT.Copy)
                elif what == "xd":
                    if main:
                        act.wait_ge(b_stored, c * 16 + 16)
                    last = nc.scalar.activation(xdT[:], bank[0:XD, :], ACT.Copy)
                elif what == "cT":
                    if kind != "first":
                        act.wait_ge(summed, c * 64)
                    last = nc.scalar.activation(c_tok[other][:], bank[:, 0:LT * XD].rearrange(
                        "p (l n) -> p l n", l=LT), ACT.Copy)
                elif what == "d":
                    if j == 0:
                        act.wait_ge(u_ready, c + 2)
                    nc.scalar.activation(tmp[:, j, :], bank[:], ACT.Abs, bias=b_dt[:, j:j + 1])
                    last = nc.scalar.activation(delta[other][:, j, :], bank[:], ACT.Relu, bias=b_dt[:, j:j + 1])
                elif what == "ud":
                    last = nc.scalar.activation(yacc[other][:, j, :], bank[:], ACT.Copy)
                elif what == "yT":
                    last = nc.scalar.activation(yT[:, j, :], bank[:], ACT.Copy)
                elif what == "o":
                    last = nc.scalar.activation(resid[:, 2 * j:2 * j + 2, :], bank[:].rearrange(
                        "p (l d) -> p l d", l=2), ACT.Copy)
                elif what == "xt":
                    last = nc.scalar.activation(x1T[:, j, :], bank[:], ACT.Copy)
                else:
                    dst = logits[:, bass.ds((c - 1) * (LT * NE), LT * NE)]
                    last = nc.scalar.activation(dst, bank[:, 0:LT * NE], ACT.Copy)
                last.then_inc(read[project], 1)

            def chunk(c, parity, kind, main):
                other = 1 - parity
                for slot in range(SLOTS):
                    n, t = slot // DT, slot % DT
                    if main:
                        if slot == 0:
                            act.wait_ge(delta_ready, (c + 1) * DT)
                        if kind != "first" or n >= 1:
                            act.wait_ge(scanned, c * 64 + slot - 3)
                        nc.scalar.activation(da_bank[t][:], delta[parity][:, t, :], ACT.Exp,
                                             scale=a_neg[:, t, n:n + 1]).then_inc(da_ready, 1)
                    if slot == SILU_U_SLOT and kind != "last":
                        act.wait_ge(conv_step, (c + 2) * 2 * DT)
                        if main:
                            act.wait_ge(du_ready, (c + 1) * DT)
                        nc.scalar.activation(u[:], tmp[:], ACT.Silu).then_inc(u_ready, 1)
                        nc.scalar.preload_act_table_set(EXP_AND_LOG)
                    for name in USES[kind]:
                        if READ_SLOT[name] == slot:
                            copy_out(c, parity, kind, main, name)
                    if slot == SOFT_SLOTS[0] and kind != "last":
                        wait_read(act, c, "d3")
                        nc.scalar.activation(tmp[:], tmp[:], ACT.Exp, scale=-1.0).then_inc(soft_step, 1)
                    if slot == SOFT_SLOTS[1] and kind != "last":
                        act.wait_ge(soft_step, 2 * (c + 1) + 1)
                        nc.scalar.activation(tmp[:], tmp[:], ACT.Ln, bias=1.0).then_inc(soft_step, 1)
                    if slot == NORM_SLOT and kind != "first":
                        act.wait_ge(shift_ready, c)
                        for l in range(LT):
                            nc.scalar.activation(x1[:, l, :], resid[:, l, :], ACT.Identity, bias=shift[:, l:l + 1],
                                                 scale=rstd[:, l:l + 1]).then_inc(x1_ready, 1)
                    if slot == SILU_GATE_SLOT and main:
                        wait_read(act, c - 1, "r3")
                        nc.scalar.activation(gate[parity][:], gate[parity][:], ACT.Silu).then_inc(gate_ready, 1)
                        nc.scalar.preload_act_table_set(EXP_AND_LOG)
                if kind != "first":
                    act.wait_ge(x1_stored, c * 32)

            over_chunks(act, chunk)

        @block.vector
        def _(dve):
            dve.wait_ge(weights_in, N_WEIGHTS * 16)
            for t in range(DT):
                nc.vector.tensor_scalar(diag_d[:, t, :], ident[:], d_par[:, t:t + 1], None, ALU.mult
                                        ).then_inc(setup, 1)
            nc.vector.memset(u_pad[:, :, 0:2], 0.0).then_inc(pad_ready, 1)

            def add_state(c, parity, n, l):
                dve.wait_ge(ht_ready, c * 64 + 4 * n + l + 1)
                if n == 0:
                    wait_read(dve, c - 1, f"ud{l}")
                else:
                    dve.wait_ge(summed, c * 64 + 4 * (n - 1) + l + 1)
                nc.vector.scalar_tensor_tensor(
                    out=yacc[parity][:, l, :], in0=ht_bank[l % 2][:],
                    scalar=c_tok[parity][:, l, RANK + NST + n:RANK + NST + n + 1],
                    in1=yacc[parity][:, l, :], op0=ALU.mult, op1=ALU.add).then_inc(summed, 1)

            def chunk(c, parity, kind, main):
                other = 1 - parity
                for slot in range(SLOTS):
                    n, t = slot // DT, slot % DT
                    if main:
                        dve.wait_ge(da_ready, c * 64 + slot + 1)
                        if t == 0:
                            dve.wait_ge(dbu_ready, c * NST + n + 1)
                            if kind != "first" or n >= 2:
                                dve.wait_ge(ht_ready, c * 64 + 4 * (n - 1))
                            if parity == 1 and n < 2:
                                dve.wait_ge(carried, (c - 1) * (NST // 2) + NST - 1 + n)
                            if parity == 0 and n >= 2:
                                dve.wait_ge(carried, c * (NST // 2) + n - 1)
                        initial = carry[:, n, t:t + 1] if parity == 1 else 0.0
                        nc.vector.tensor_tensor_scan(hst[n % 2][:, t, :], da_bank[t][:], dbu[DBU[n]][:, t, :],
                                                     initial, ALU.mult, ALU.add).then_inc(scanned, 1)
                    if main and n > 0:
                        add_state(c, parity, n - 1, t)
                    if n == 0 and kind != "first":
                        add_state(c - 1, other, NST - 1, t)
                    if t == 1 and (main and parity == 0 and n > 0 or main and parity == 1 and n == 0):
                        m = (n - 1) % NST
                        dve.wait_ge(scanned, c * 64 + 4 * n)
                        nc.vector.tensor_copy(carry[:, m, :], hst[m % 2][:, :, CL - 1]).then_inc(carried, 1)
                    if kind != "last" and slot in CONV_SLOT:
                        tile, tap = CONV_SLOT[slot]
                        if tap == 1:
                            wait_read(dve, c, f"u{tile}")
                        else:
                            dve.wait_ge(conv_step, (c + 1) * 2 * DT + 2 * tile + 1)
                        nc.vector.scalar_tensor_tensor(
                            out=tmp[:, tile, :], in0=u_pad[:, tile, tap:tap + CL], scalar=w_conv[:, tile, tap:tap + 1],
                            in1=tmp[:, tile, :], op0=ALU.mult, op1=ALU.add).then_inc(conv_step, 1)
                    if kind != "last" and slot == HISTORY_SLOT:
                        dve.wait_ge(conv_step, (c + 2) * 2 * DT)
                        if parity == 1:
                            nc.vector.tensor_copy(u_pad[:, :, 0:2], u_pad[:, :, CL:CL + 2]).then_inc(pad_ready, 1)
                        else:
                            nc.vector.memset(u_pad[:, :, 0:2], 0.0).then_inc(pad_ready, 1)
                    if kind != "first" and slot in STATS_SLOT:
                        j = STATS_SLOT.index(slot)
                        wait_read(dve, c, f"o{j}")
                        for l in (2 * j, 2 * j + 1):
                            nc.vector.bn_stats(stats[:, l, :], resid[:, l, :])
                    if kind != "first" and slot == STATS_SLOT[1]:
                        dve.drain()
                        for l in range(LT):
                            nc.vector.bn_aggr(mean_var[:, l, :], stats[:, l, :]).then_inc(stats_step, 1)
                        dve.wait_ge(stats_step, c * LT)
                        nc.vector.tensor_scalar(minus_mean[:], mean_var[:, :, 0], -1.0, None, ALU.mult)
                        nc.vector.tensor_scalar(var_eps[:], mean_var[:, :, 1], EPS, None, ALU.add).then_inc(var_ready, 1)

            over_chunks(dve, chunk)

        @block.tensor
        def _(pe):
            pe.wait_ge(weights_in, N_WEIGHTS * 16)
            pe.wait_ge(setup, 1 + DT)

            def fill(c, parity, kind, name, part):
                other = 1 - parity
                bank = gen_bank[bank_of(parity, kind, name)]
                parts = SLOT[name][1]
                before = two_before(c, kind, name)
                if part == 0 and before is not None:
                    wait_read(pe, *before)
                what, j = name.rstrip("0123"), int(name[-1]) if name[-1].isdigit() else 0
                if what == "u":
                    if name == "u0" and part == 0:
                        pe.wait_ge(xt_loaded, c * 16 + 32)
                    last = nc.tensor.matmul(bank[:], w_in[:, part, j * P:(j + 1) * P], xT[:, part, :],
                                            start=part == 0, stop=part == KD - 1)
                elif what == "r":
                    last = nc.tensor.matmul(bank[:], xT[:, part, j * P:(j + 1) * P], w_in[:, part, DI:],
                                            start=part == 0, stop=part == KD - 1)
                elif what == "xd":
                    if part == 0:
                        pe.wait_ge(u_ready, c + 2)
                    last = nc.tensor.matmul(bank[0:XD, :], w_x[:, part, :], u[:, part, :], start=part == 0,
                                            stop=part == DT - 1)
                elif what == "cT":
                    for l in range(LT):
                        last = nc.tensor.matmul(bank[:, l * XD:(l + 1) * XD], xdT[:, l * P:(l + 1) * P],
                                                ident[0:XD, 0:XD], start=True, stop=True)
                elif what == "d":
                    if j == 0:
                        wait_read(pe, c, "xd")
                    last = nc.tensor.matmul(bank[:], w_dt[:, j * P:(j + 1) * P], xdT[0:RANK, :], start=True, stop=True)
                elif what == "ud":
                    for t in range(DT):
                        last = nc.tensor.matmul(bank[:, t * P:(t + 1) * P], u[:, t, j * P:(j + 1) * P],
                                                diag_d[:, t, :], start=True, stop=True)
                elif what == "yT":
                    if j == 0:
                        pe.wait_ge(gated, c * LT)
                    for l in range(LT):
                        last = nc.tensor.transpose(bank[:, l * P:(l + 1) * P], yacc[other][:, l, j * P:(j + 1) * P],
                                                   ident[:])
                elif what == "o":
                    if name == "o0" and part == 0:
                        wait_read(pe, c, "yT3")
                        pe.wait_ge(rows_loaded, c * 16)
                    for l, t in [(l, t) for l in (2 * j, 2 * j + 1) for t in range(DT + 1)][2 * part:2 * part + 2]:
                        acc = bank[:, l % 2 * DM:(l % 2 + 1) * DM]
                        if t < DT:
                            nc.tensor.matmul(acc, yT[:, t, l * P:(l + 1) * P], w_out[:, t, :], start=t == 0, stop=False)
                        else:
                            last = nc.tensor.matmul(acc, ident[:], x_rows[:, l, :], start=False, stop=True)
                elif what == "xt":
                    if j == 0:
                        pe.wait_ge(x1_ready, c * LT)
                    for l in range(LT):
                        last = nc.tensor.transpose(bank[:, l * P:(l + 1) * P], x1[:, l, j * P:(j + 1) * P], ident[:])
                else:
                    if part == 0:
                        wait_read(pe, c, "xt1")
                    for k in range(KD):
                        last = nc.tensor.matmul(bank[:, part * NE:(part + 1) * NE], x1T[:, k, part * P:(part + 1) * P],
                                                w_rt[:, k, :], start=k == 0, stop=k == KD - 1)
                if part == parts - 1:
                    last.then_inc(full[name in PROJECT], 1)

            def chunk(c, parity, kind, main):
                for slot in range(SLOTS):
                    n, l = slot // LT, slot % LT
                    if main:
                        if l == 0:
                            pe.wait_ge(scanned, c * 64 + 4 * n + 4)
                        if kind != "first" or n > 0 or l >= 2:
                            pe.wait_ge(summed, c * 64 + slot - 1)
                        for t in range(DT):
                            last = nc.tensor.transpose(ht_bank[l % 2][:, t * P:(t + 1) * P],
                                                       hst[n % 2][:, t, l * P:(l + 1) * P], ident[:])
                        last.then_inc(ht_ready, 1)
                    for name in USES[kind]:
                        first, parts = SLOT[name]
                        if first <= slot < first + parts:
                            fill(c, parity, kind, name, slot - first)

            over_chunks(pe, chunk)


def make_ident(nc, ident):
    with nc.semaphore("ident_step") as ident_step, nc.Block() as block:
        @block.gpsimd
        def _(pool):
            nc.gpsimd.memset(ident[:], 0.0).then_inc(ident_step, 1)
            pool.wait_ge(ident_step, 1)
            nc.gpsimd.affine_select(out=ident[:], in_=ident[:], compare_op=ALU.not_equal, fill=1.0, base=0,
                                    pattern=[[-1, P]], channel_multiplier=1).then_inc(ident_step, 1)
            pool.wait_ge(ident_step, 2)


def make_constants(nc, k):
    with ExitStack() as ctx:
        f = ctx.enter_context(nc.sbuf_tensor("int_table", [P, P], I32))
        g = ctx.enter_context(nc.sbuf_tensor("same_rest", [P, P], I32))
        h = ctx.enter_context(nc.sbuf_tensor("above", [P, P], F32))
        made = ctx.enter_context(nc.semaphore("tables_made"))
        step = ctx.enter_context(nc.semaphore("masks_step"))
        block = ctx.enter_context(nc.Block())

        @block.gpsimd
        def _(pool):
            exact = {"allow_small_or_imprecise_dtypes": True}
            nc.gpsimd.iota(k["slot_low"][:], [[1, P]], 0, 0, **exact).then_inc(made, 1)
            nc.gpsimd.iota(k["slot_high"][:], [[1, CAP // P]], 0, 0, **exact).then_inc(made, 1)
            nc.gpsimd.iota(k["tile_id"][:], [[1, TILES]], 0, 0, **exact).then_inc(made, 1)
            nc.gpsimd.iota(k["part_id"][:], [[0, 1]], 0, 1, **exact).then_inc(made, 1)
            nc.gpsimd.iota(k["first_wins"][:], [[-1, NE]], NE, 0, **exact).then_inc(made, 1)
            nc.gpsimd.iota(f[:], [[1, P]], P, -1).then_inc(made, 1)
            nc.gpsimd.memset(k["bit"][:], 1 << 29).then_inc(made, 1)
            nc.gpsimd.memset(k["threshold"][:], 0).then_inc(made, 1)
            nc.gpsimd.memset(k["ones"][:], 1.0).then_inc(made, 1)
            pool.wait_ge(made, 9)

        @block.vector
        def _(dve):
            dve.wait_ge(made, 9)
            nc.vector.tensor_scalar(g[:], f[:], NE - 1, None, ALU.bitwise_and).then_inc(step, 1)
            nc.vector.tensor_scalar(h[:], f[:], float(P), None, ALU.is_gt).then_inc(step, 1)
            dve.wait_ge(step, 2)
            nc.vector.tensor_scalar(k["same_expert"][:], g[:], 0.0, None, ALU.is_equal).then_inc(step, 1)
            dve.wait_ge(step, 3)
            nc.vector.tensor_tensor(k["earlier"][:], k["same_expert"][:], h[:], ALU.mult).then_inc(step, 1)
            dve.wait_ge(step, 4)


def route(nc, k, logits, ident):
    with ExitStack() as ctx:
        def sb(name, shape, dt=F32):
            return ctx.enter_context(nc.sbuf_tensor(name, shape, dt))

        def sem(name):
            return ctx.enter_context(nc.semaphore(name))

        full3 = [P, TILES, NE]
        row_max = sb("row_max", [P, TILES, 1])
        shifted = sb("shifted", full3)
        probs = sb("probs", full3)
        row_sum = sb("row_sum", [P, TILES, 1])
        top = [sb(f"top{i}", [P, TILES, 1]) for i in range(2)]
        mask = [sb(f"mask{i}", full3) for i in range(2)]
        equal = sb("equal", full3)
        key = sb("key", full3)
        key_max = sb("key_max", [P, TILES, 1])
        rest = sb("rest", full3)
        weight = [sb(f"weight{i}", [P, TILES, 1]) for i in range(2)]
        fw = sb("fw", full3)
        ft = sb("ft", [P, 4, P])
        flags = sb("flags", [P, 4, P])
        above = sb("above_t", [P, 4, P])
        tied = sb("tied", [P, 4, P])
        rank = sb("rank", [P, 4, P])
        code = sb("code", [P, 4, P])
        count = sb("count", [P, 1])
        candidate = sb("candidate", [P, 1], I32)
        accept = sb("accept", [P, 1], I32)
        need = sb("need", [P, 1])
        seg = sb("seg", [P, 4])
        seg_sum = sb("seg_sum", [P, 4])
        seg_before = sb("seg_before", [P, 4])
        slot = sb("slot", [P, TILES * NE], I32)
        low = sb("low", [P, TILES * NE], I32)
        high = sb("high", [P, TILES * NE], I32)
        left = [sb(f"left{i}", full3) for i in range(2)]
        bank = ctx.enter_context(nc.psum_tensor("flip", [P, 512], F32))
        total = ctx.enter_context(nc.psum_tensor("total", [P, 1], F32))
        before = ctx.enter_context(nc.psum_tensor("before", [P, 4], F32))

        step = sem("route_step")
        shifted_ready = sem("shifted_ready")
        exp_ready = sem("exp_ready")
        fw_ready = sem("fw_ready")
        flipped = sem("flipped")
        counted = sem("counted")
        totalled = sem("totalled")
        segments = sem("segments")
        offsets = sem("offsets")
        code_ready = sem("code_ready")
        BITS = 30
        block = ctx.enter_context(nc.Block())

        @block.scalar
        def _(act):
            act.wait_ge(shifted_ready, 1)
            nc.scalar.activation(probs[:], shifted[:], ACT.Exp).then_inc(exp_ready, 1)

        @block.tensor
        def _(pe):
            pe.wait_ge(fw_ready, 1)
            for g in range(4):
                last = nc.tensor.transpose(bank[:, g * P:(g + 1) * P],
                                           fw[:].rearrange("p t e -> p (t e)")[:, g * P:(g + 1) * P], ident[:])
            last.then_inc(flipped, 1)
            with pe.Fori(0, BITS) as i:
                pe.wait_ge(counted, i + 1)
                nc.tensor.matmul(total[:], k["same_expert"][:], count[:], start=True, stop=True).then_inc(totalled, 1)
            pe.wait_ge(counted, BITS + 1)
            nc.tensor.matmul(total[:], k["same_expert"][:], count[:], start=True, stop=True).then_inc(totalled, 1)
            for i in range(2):
                pe.wait_ge(segments, i + 1)
                nc.tensor.matmul(before[:], k["earlier"][:], seg[:], start=True, stop=False)
                nc.tensor.matmul(before[:], k["same_expert"][:], seg_before[:], start=False, stop=True
                                 ).then_inc(offsets, 1)
            pe.wait_ge(code_ready, 1)
            for g in range(4):
                last = nc.tensor.transpose(bank[:, g * P:(g + 1) * P], code[:, g, :], ident[:])
            last.then_inc(flipped, 1)

        @block.vector
        def _(dve):
            chain = [0]

            def link(ins):
                chain[0] += 1
                ins.then_inc(step, 1)
                dve.wait_ge(step, chain[0])

            v = nc.vector
            lg = logits[:].rearrange("p (t e) -> p t e", e=NE)
            link(v.tensor_reduce(row_max[:], lg, AX.X, ALU.max))
            v.tensor_tensor(shifted[:], lg, row_max[:].to_broadcast(full3), ALU.subtract).then_inc(shifted_ready, 1)
            dve.wait_ge(exp_ready, 1)
            link(v.tensor_reduce(row_sum[:], probs[:], AX.X, ALU.add))
            link(v.reciprocal(row_sum[:], row_sum[:]))
            link(v.tensor_tensor(probs[:], probs[:], row_sum[:].to_broadcast(full3), ALU.mult))
            for i in range(2):
                src = (probs, rest)[i]
                link(v.tensor_reduce(top[i][:], src[:], AX.X, ALU.max))
                link(v.tensor_tensor(equal[:], src[:], top[i][:].to_broadcast(full3), ALU.is_equal))
                link(v.tensor_tensor(key[:], equal[:], k["first_wins"][:].to_broadcast(full3), ALU.mult))
                link(v.tensor_reduce(key_max[:], key[:], AX.X, ALU.max))
                link(v.tensor_tensor(mask[i][:], key[:], key_max[:].to_broadcast(full3), ALU.is_equal))
                if i == 0:
                    link(v.scalar_tensor_tensor(out=rest[:], in0=mask[0][:], scalar=-2.0, in1=probs[:],
                                                op0=ALU.mult, op1=ALU.add))
            link(v.tensor_tensor(row_sum[:], top[0][:], top[1][:], ALU.add))
            link(v.tensor_scalar(row_sum[:], row_sum[:], 1e-6, None, ALU.add))
            link(v.reciprocal(row_sum[:], row_sum[:]))
            for i in range(2):
                link(v.tensor_tensor(weight[i][:], top[i][:], row_sum[:], ALU.mult))
            link(v.tensor_tensor(equal[:], mask[0][:], weight[0][:].to_broadcast(full3), ALU.mult))
            link(v.tensor_tensor(key[:], mask[1][:], weight[1][:].to_broadcast(full3), ALU.mult))
            v.tensor_tensor(fw[:], equal[:], key[:], ALU.add).then_inc(fw_ready, 1)
            dve.wait_ge(fw_ready, 1)
            link(v.tensor_copy(k["part"][0][:], fw[:]))
            link(v.tensor_tensor(left[0][:], fw[:], k["part"][0][:], ALU.subtract))
            link(v.tensor_copy(k["part"][1][:], left[0][:]))
            link(v.tensor_tensor(left[1][:], left[0][:], k["part"][1][:], ALU.subtract))
            link(v.tensor_copy(k["part"][2][:], left[1][:]))
            dve.wait_ge(flipped, 1)
            link(v.tensor_copy(ft[:], bank[:].rearrange("p (g t) -> p g t", g=4)))

            with dve.Fori(0, BITS) as i:
                v.tensor_tensor(candidate[:], k["threshold"][:], k["bit"][:], ALU.bitwise_or).then_inc(step, 1)
                dve.wait_ge(step, i * 4 + chain[0] + 1)
                v.tensor_scalar(flags[:], ft[:], candidate[:].bitcast(F32), None, ALU.is_ge, ALU.add,
                                accum_out=count[:]).then_inc(counted, 1)
                dve.wait_ge(totalled, i + 1)
                v.tensor_scalar(accept[:], total[:], float(CAP), None, ALU.is_ge).then_inc(step, 1)
                dve.wait_ge(step, i * 4 + chain[0] + 2)
                v.tensor_scalar(k["bit"][:], k["bit"][:], 1, None, ALU.logical_shift_right).then_inc(step, 1)
                v.copy_predicated(k["threshold"][:], accept[:], candidate[:]).then_inc(step, 1)
                dve.wait_ge(step, i * 4 + chain[0] + 4)
            chain[0] += 4 * BITS
            limit = k["threshold"][:].bitcast(F32)
            v.tensor_scalar(above[:], ft[:], limit, None, ALU.is_gt, ALU.add, accum_out=count[:]).then_inc(counted, 1)
            link(v.tensor_scalar(tied[:], ft[:], limit, None, ALU.is_equal))
            dve.wait_ge(totalled, BITS + 1)
            link(v.tensor_scalar(need[:], total[:], -1.0, float(CAP), ALU.mult, ALU.add))

            def number(flags_in, i):
                for g in range(4):
                    link(v.tensor_tensor_scan(rank[:, g, :], k["ones"][:], flags_in[:, g, :], 0.0, ALU.mult, ALU.add))
                link(v.tensor_copy(seg[:], rank[:, :, P - 1]))
                link(v.tensor_tensor_scan(seg_sum[:], k["ones"][:, 0:4], seg[:], 0.0, ALU.mult, ALU.add))
                v.tensor_tensor(seg_before[:], seg_sum[:], seg[:], ALU.subtract).then_inc(segments, 1)
                dve.wait_ge(offsets, i + 1)
                for g in range(4):
                    link(v.tensor_scalar(rank[:, g, :], rank[:, g, :], before[:, g:g + 1], None, ALU.add))

            number(tied, 0)
            link(v.scalar_tensor_tensor(out=flags[:], in0=rank[:], scalar=need[:], in1=tied[:],
                                        op0=ALU.is_le, op1=ALU.mult))
            link(v.tensor_tensor(flags[:], flags[:], above[:], ALU.add))
            number(flags, 1)
            v.tensor_tensor(code[:], rank[:], flags[:], ALU.mult).then_inc(code_ready, 1)
            dve.wait_ge(flipped, 2)
            link(v.tensor_scalar(slot[:], bank[:], -1.0, None, ALU.add))
            link(v.tensor_scalar(low[:], slot[:], P - 1, None, ALU.bitwise_and))
            link(v.tensor_scalar(high[:], slot[:], 7, None, ALU.arith_shift_right))
            link(v.tensor_copy(k["low"][:], low[:].rearrange("p (t e) -> p t e", e=NE)))
            link(v.tensor_copy(k["high"][:], high[:].rearrange("p (t e) -> p t e", e=NE)))


ST = CAP // P
SJ = 2
JC = ST // SJ
FT_ = FF // P
PIECES = FT_ + FT_ // 2
PREPARE_AT, LIST_AT, TR_AT = 4, 19, (30, 32, 34, 36, 39)
DOWN_PIECE_AT = (4, 5, 6, 7)
NV = 5


def experts(nc, a, k, dram, ident):
    with ExitStack() as ctx:
        def sb(name, shape, dt=F32):
            return ctx.enter_context(nc.sbuf_tensor(name, shape, dt))

        def sem(name):
            return ctx.enter_context(nc.semaphore(name))

        gu_raw = sb("gu_raw", [P, 2, KD, FF])
        down_raw = sb("down_raw", [P, FT_, DM])
        gu_part = [sb(f"gu_part{i}", [P, 2, KD, FF], F32R) for i in range(2)]
        down_part = [sb(f"down_part{i}", [P, FT_, DM], F32R) for i in range(2)]
        w_mask = [sb(f"w_mask{i}", [P, 2 * KD * P], I32) for i in range(3)]
        x_mask = sb("x_mask", [P, KD, SJ * P], I32)
        h_mask = [sb(f"h_mask{i}", [P, SJ * P], I32) for i in range(2)]
        hot_low = sb("hot_low", [P, TILES, P], BF16)
        hot_high = sb("hot_high", [P, TILES, ST], BF16)
        values = sb("values", [P, TILES, NV, ST], BF16)
        lists = sb("lists", [P, NV, ST])
        pair = sb("pair", [P, ST])
        token = [sb(f"token{i}", [P, ST], U32) for i in range(2)]
        share = [sb(f"share{i}", [P, ST]) for i in range(2)]
        xg = sb("xg", [P, ST, DM])
        x_part = [sb(f"x_part{i}", [P, KD, CAP], F32R) for i in range(2)]
        silu = [sb(f"silu{i}", [P, SJ * P]) for i in range(4)]
        hid_part = [[sb(f"hid{b}_part{i}", [P, FT_, SJ * P], F32R) for i in range(2)] for b in range(2)]
        eo = sb("eo", [P, ST, DM])
        gu_bank = [ctx.enter_context(nc.psum_tensor(f"gu{i}", [P, 2, SJ * P], F32)) for i in range(4)]
        dn_bank = [ctx.enter_context(nc.psum_tensor(f"dn{i}", [P, SJ, DM], F32)) for i in range(2)]
        tr_bank = [ctx.enter_context(nc.psum_tensor(f"tr{i}", [P, KD, SJ * P], F32)) for i in range(2)]

        weights_loaded = sem("expert_loaded")
        w_masked = sem("w_masked")
        w_high = sem("w_high")
        w_low = sem("w_low")
        x_masked = sem("x_masked")
        x_high = sem("x_high")
        h_masked = sem("h_masked")
        h_high = sem("h_high")
        hot_ready = sem("hot_ready")
        values_step = sem("values_step")
        listed = sem("listed")
        list_step = sem("list_step")
        token_ready = sem("token_ready")
        share_ready = sem("share_ready")
        gathered = [sem(f"gathered{j}") for j in range(JC)]
        tr_full = sem("tr_full")
        tr_read = sem("tr_read")
        gu_full = sem("gu_full")
        silu_ready = sem("silu_ready")
        product_ready = sem("product_ready")
        hidden_ready = sem("hidden_ready")
        dn_full = sem("dn_full")
        dn_read = sem("dn_read")
        added = sem("added")
        GU, QT = JC * FT_, TILES // 8

        x1_d, acc_d = dram["x1"], dram["acc"]

        def over_experts(eng, emit):
            emit(-1, 1, "start")
            emit(0, 0, "mid0")
            with eng.Fori(0, (NE - 2) // 2) as i:
                emit(i * 2 + 1, 1, "mid")
                emit(i * 2 + 2, 0, "mid")
            emit(NE - 1, 1, "end")

        block = ctx.enter_context(nc.Block())

        @block.sync
        def _(sp):
            def expert(e, par, kind):
                if kind == "end":
                    return
                if kind != "start":
                    sp.wait_ge(w_low, (e + 1) * PIECES)
                row = (e + 1) * DM
                for i, w in enumerate(("wg", "wu")):
                    sp.dma_start(gu_raw[:, i], a[w].rearrange("e d f -> (e d) f")[bass.ds(row, DM), :]
                                 .rearrange("(k p) f -> p k f", p=P)).then_inc(weights_loaded, 16)
                sp.dma_start(down_raw[:], a["wd"].rearrange("e f d -> (e f) d")[bass.ds((e + 1) * FF, FF), :]
                             .rearrange("(k p) d -> p k d", p=P)).then_inc(weights_loaded, 16)

            over_experts(sp, expert)

        def raw_piece(p):
            def cut(gu, down):
                return gu[:, :, :, p * P:(p + 1) * P] if p < FT_ else down[:, 2 * (p - FT_):2 * (p - FT_) + 2, :]
            return cut(gu_raw, down_raw), [cut(gu_part[i], down_part[i]) for i in range(2)]

        def mask_of(p, dtype):
            flat = w_mask[p % 3][:] if dtype == I32 else w_mask[p % 3][:].bitcast(dtype)
            return flat.rearrange("p (i k f) -> p i k f", i=2, k=KD) if p < FT_ else \
                flat.rearrange("p (k d) -> p k d", k=2)

        @block.gpsimd
        def _(pool):
            def low_parts(e, pieces):
                for p in pieces:
                    pool.wait_ge(w_masked, e * PIECES + p + 1)
                    if e > 0 and p < FT_:
                        pool.wait_ge(gu_full, e * GU - FT_ + p + 1)
                    elif e > 0:
                        pool.wait_ge(dn_full, e * JC)
                    raw, parts = raw_piece(p)
                    nc.gpsimd.tensor_tensor(parts[1], raw, mask_of(p, F32), ALU.subtract).then_inc(w_low, 1)

            def gather(e_next, par):
                pool.wait_ge(token_ready, e_next + 1)
                for s in range(ST):
                    nc.gpsimd.indirect_dma_start(
                        out=xg[:, s, :], out_offset=None, in_=x1_d,
                        in_offset=bass.IndirectOffsetOnAxis(ap=token[par][:, s:s + 1], axis=0),
                        bounds_check=TOK - 1).then_inc(gathered[s // SJ], 16)

            def expert(e, par, kind):
                if kind == "start":
                    gather(0, 0)
                    low_parts(0, range(PIECES))
                    return
                for j in range(-1, JC):
                    if j == -1 and kind == "mid0" or j == JC - 1 and kind != "end":
                        continue
                    if j == 2 and kind != "end":
                        pool.wait_ge(tr_read, (e + 1) * JC)
                        gather(e + 1, 1 - par)
                    pool.wait_ge(dn_read, e * JC + j + 1)
                    if j == 0 and kind != "mid0":
                        pool.wait_ge(added, e * (ST * 16))
                    owner, chunk = (par, j) if j >= 0 else (1 - par, JC - 1)
                    for s in range(chunk * SJ, (chunk + 1) * SJ):
                        nc.gpsimd.indirect_dma_start(
                            out=acc_d, out_offset=bass.IndirectOffsetOnAxis(ap=token[owner][:, s:s + 1], axis=0),
                            in_=eo[:, s, :], in_offset=None, bounds_check=TOK - 1,
                            compute_op=ALU.add).then_inc(added, 16)
                    if j == -1:
                        low_parts(e, range(FT_, PIECES))
                if kind != "end":
                    low_parts(e + 1, range(FT_))

            expert(-1, 1, "start")
            for e in range(NE):
                expert(e, e % 2, "mid0" if e == 0 else "end" if e == NE - 1 else "mid")
            pool.wait_ge(added, NE * ST * 16)

        @block.vector
        def _(dve):
            v = nc.vector

            def prepare(e, i, first):
                if i == 0:
                    if not first:
                        dve.wait_ge(listed, e)
                    v.tensor_tensor(hot_high[:], k["high"][:, :, bass.ds(e, 1)].to_broadcast([P, TILES, ST]),
                                    k["slot_high"][:].to_broadcast([P, TILES, ST]), ALU.is_equal
                                    ).then_inc(values_step, 1)
                elif i <= NV:
                    if i == 1:
                        dve.wait_ge(values_step, e * (NV + 1) + 1)
                    src = (k["tile_id"][:] if i == 1 else k["part_id"][:].to_broadcast([P, TILES, 1]) if i == 2 else
                           k["part"][i - 3][:, :, bass.ds(e, 1)])
                    v.tensor_tensor(values[:, :, i - 1, :], hot_high[:], src.to_broadcast([P, TILES, ST]),
                                    ALU.mult).then_inc(values_step, 1)
                else:
                    part = slice((i - NV - 1) * QT, (i - NV) * QT)
                    v.tensor_tensor(hot_low[:, part, :], k["low"][:, part, bass.ds(e, 1)].to_broadcast([P, QT, P]),
                                    k["slot_low"][:].to_broadcast([P, QT, P]), ALU.is_equal).then_inc(hot_ready, 1)

            def read_lists(e, par, first):
                dve.wait_ge(listed, e + 1)
                v.tensor_copy(lists[:], tr_bank[0][:].rearrange("p k s -> p (k s)")[:, 0:NV * ST].rearrange(
                    "p (v s) -> p v s", v=NV)).then_inc(list_step, 1)
                dve.wait_ge(list_step, e * 2 + 1)
                if not first:
                    dve.wait_ge(added, (e - 1) * (ST * 16))
                v.scalar_tensor_tensor(out=token[par][:], in0=lists[:, 0, :], scalar=float(P), in1=lists[:, 1, :],
                                       op0=ALU.mult, op1=ALU.add).then_inc(token_ready, 1)
                v.tensor_tensor(pair[:], lists[:, 2, :], lists[:, 3, :], ALU.add).then_inc(list_step, 1)
                dve.wait_ge(list_step, e * 2 + 2)
                if not first:
                    dve.wait_ge(dn_read, (e - 1) * JC)
                v.tensor_tensor(share[par][:], pair[:], lists[:, 4, :], ALU.add).then_inc(share_ready, 1)

            def mask_piece(e, p, kind):
                if p == 0:
                    dve.wait_ge(weights_loaded, (e + 1) * 48)
                if kind != "start" or p >= 3:
                    dve.wait_ge(w_high, e * PIECES + p - 2)
                    dve.wait_ge(w_low, e * PIECES + p - 2)
                raw, _ = raw_piece(p)
                v.tensor_scalar(mask_of(p, I32), raw.bitcast(I32), HIGH_BITS, None, ALU.bitwise_and
                                ).then_inc(w_masked, 1)

            def split_tokens(e, j, kind):
                dve.wait_ge(tr_full, e * JC + j + 1)
                if kind != "start" or j > 0:
                    dve.wait_ge(x_high, e * JC + j)
                    dve.wait_ge(tr_read, e * JC + j)
                v.tensor_scalar(x_mask[:], tr_bank[j % 2][:].bitcast(I32), HIGH_BITS, None, ALU.bitwise_and
                                ).then_inc(x_masked, 1)
                dve.wait_ge(x_masked, e * JC + j + 1)
                v.tensor_tensor(x_part[1][:, :, j * SJ * P:(j + 1) * SJ * P], tr_bank[j % 2][:],
                                x_mask[:].bitcast(F32), ALU.subtract).then_inc(tr_read, 1)

            def low_hidden(e, par, n):
                j, f = divmod(n, FT_)
                dve.wait_ge(h_masked, e * GU + n + 1)
                v.tensor_tensor(hid_part[(j + par) % 2][1][:, f, :], silu[n % 4][:], h_mask[n % 2][:].bitcast(F32),
                                ALU.subtract).then_inc(hidden_ready, 1)

            def expert(e, par, kind):
                if kind == "start":
                    for i in range(NV + 9):
                        prepare(0, i, True)
                    read_lists(0, 0, True)
                    for p in range(PIECES):
                        mask_piece(0, p, kind)
                    for j in range(JC):
                        split_tokens(0, j, kind)
                    return
                for n in range(GU):
                    j, f = divmod(n, FT_)
                    dve.wait_ge(silu_ready, e * GU + n + 1)
                    v.tensor_tensor(silu[n % 4][:], silu[n % 4][:], gu_bank[n % 4][:, 1, :],
                                    ALU.mult).then_inc(product_ready, 1)
                    if n > 0:
                        low_hidden(e, par, n - 1)
                    if f == 0 and (kind != "mid0" or j >= 2):
                        dve.wait_ge(dn_full, e * JC + j - 1)
                    dve.wait_ge(product_ready, e * GU + n + 1)
                    if kind != "mid0" or n >= 2:
                        dve.wait_ge(h_high, e * GU + n - 1)
                        dve.wait_ge(hidden_ready, e * GU + n - 1)
                    v.tensor_scalar(h_mask[n % 2][:], silu[n % 4][:].bitcast(I32), HIGH_BITS, None, ALU.bitwise_and
                                    ).then_inc(h_masked, 1)
                    if n + 1 in DOWN_PIECE_AT and kind != "mid0":
                        mask_piece(e, FT_ + DOWN_PIECE_AT.index(n + 1), kind)
                    if 0 <= n - PREPARE_AT < NV + 9 and kind != "end":
                        prepare(e + 1, n - PREPARE_AT, False)
                    if n == LIST_AT + 1 and kind != "end":
                        read_lists(e + 1, 1 - par, kind == "mid0")
                    if j == JC - 1 and kind != "end":
                        mask_piece(e + 1, f, kind)
                    if n - 1 in TR_AT and kind != "end":
                        split_tokens(e + 1, TR_AT.index(n - 1), kind)
                low_hidden(e, par, GU - 1)
                if kind != "end":
                    split_tokens(e + 1, JC - 1, kind)

            over_experts(dve, expert)

        order = []
        for j in range(JC):
            for f in range(FT_):
                n = j * FT_ + f
                order.append(("gu", n))
                if n:
                    order.append(("h", n - 1))
                if f == 3:
                    order.append(("dn", j - 1))
                if n in DOWN_PIECE_AT:
                    order.append(("w", FT_ + DOWN_PIECE_AT.index(n)))
                if n == LIST_AT:
                    order.append(("list", 0))
                if j == JC - 1 and f >= 1:
                    order.append(("w", f - 1))
                if n in TR_AT:
                    order.append(("tr", TR_AT.index(n)))
                if n - 2 in TR_AT:
                    order.append(("x", TR_AT.index(n - 2)))
        order += [("h", GU - 1), ("w", FT_ - 1), ("x", JC - 1), ("dn", JC - 1)]

        def skipped(kind, n):
            return n == -1 and kind == "mid0" or n == JC - 1 and kind != "end"

        @block.scalar
        def _(act):
            def high_tokens(e, j):
                act.wait_ge(x_masked, e * JC + j + 1)
                nc.scalar.activation(x_part[0][:, :, j * SJ * P:(j + 1) * SJ * P], x_mask[:].bitcast(F32),
                                     ACT.Copy).then_inc(x_high, 1)

            def high_weights(e, p):
                act.wait_ge(w_masked, e * PIECES + p + 1)
                nc.scalar.activation(raw_piece(p)[1][0], mask_of(p, F32), ACT.Copy).then_inc(w_high, 1)

            def expert(e, par, kind):
                if kind == "start":
                    for p in range(PIECES):
                        high_weights(0, p)
                    for j in range(JC):
                        high_tokens(0, j)
                    return
                for what, n in order:
                    if what == "gu":
                        act.wait_ge(gu_full, e * GU + n + 1)
                        if kind != "mid0" or n >= 4:
                            act.wait_ge(hidden_ready, e * GU + n - 3)
                        nc.scalar.activation(silu[n % 4][:], gu_bank[n % 4][:, 0, :], ACT.Silu).then_inc(silu_ready, 1)
                    elif what == "h":
                        act.wait_ge(h_masked, e * GU + n + 1)
                        j, f = divmod(n, FT_)
                        if f == 0 and (kind != "mid0" or j >= 2):
                            act.wait_ge(dn_full, e * JC + j - 1)
                        nc.scalar.activation(hid_part[(j + par) % 2][0][:, f, :], h_mask[n % 2][:].bitcast(F32),
                                             ACT.Copy).then_inc(h_high, 1)
                    elif what == "dn" and not skipped(kind, n):
                        act.wait_ge(dn_full, e * JC + n + 1)
                        owner, chunk = (par, n) if n >= 0 else (1 - par, JC - 1)
                        if n == 0:
                            act.wait_ge(share_ready, e + 1)
                            if kind != "mid0":
                                act.wait_ge(added, e * (ST * 16))
                        for s in range(SJ):
                            tile = chunk * SJ + s
                            last = nc.scalar.activation(eo[:, tile, :], dn_bank[(n + par) % 2][:, s, :], ACT.Copy,
                                                        scale=share[owner][:, tile:tile + 1])
                        last.then_inc(dn_read, 1)
                    elif what == "w" and n >= FT_:
                        if kind != "mid0":
                            high_weights(e, n)
                    elif what == "w" and kind != "end":
                        high_weights(e + 1, n)
                    elif what == "x" and kind != "end":
                        high_tokens(e + 1, n)

            over_experts(act, expert)

        @block.tensor
        def _(pe):
            def make_list(e):
                pe.wait_ge(values_step, (e + 1) * (NV + 1))
                for t in range(TILES):
                    if t % QT == 0:
                        pe.wait_ge(hot_ready, e * 8 + t // QT + 1)
                    last = nc.tensor.matmul(tr_bank[0][:].rearrange("p k s -> p (k s)")[:, 0:NV * ST],
                                            hot_low[:, t, :], values[:, t, :, :].rearrange("p v s -> p (v s)"),
                                            start=t == 0, stop=t == TILES - 1)
                last.then_inc(listed, 1)

            def transpose(e, j, first):
                pe.wait_ge(gathered[j], (e + 1) * (SJ * 16))
                if j == 0:
                    pe.wait_ge(token_ready, e + 1)
                if j >= 2:
                    pe.wait_ge(tr_read, e * JC + j - 1)
                for kk in range(KD):
                    for s in range(SJ):
                        last = nc.tensor.transpose(tr_bank[j % 2][:, kk, s * P:(s + 1) * P],
                                                   xg[:, j * SJ + s, kk * P:(kk + 1) * P], ident[:])
                last.then_inc(tr_full, 1)

            def expert(e, par, kind):
                if kind == "start":
                    make_list(0)
                    for j in range(JC):
                        transpose(0, j, True)
                    return
                for what, n in order:
                    if what == "gu":
                        j, f = divmod(n, FT_)
                        if j == 0:
                            pe.wait_ge(w_high, e * PIECES + f + 1)
                            pe.wait_ge(w_low, e * PIECES + f + 1)
                        if f == 0:
                            pe.wait_ge(tr_read, e * JC + j + 1)
                            pe.wait_ge(x_high, e * JC + j + 1)
                        if kind != "mid0" or n >= 4:
                            pe.wait_ge(product_ready, e * GU + n - 3)
                        for i in range(2):
                            products = [(kk, wp, xp) for kk in range(KD) for wp, xp in ((0, 0), (0, 1), (1, 0))]
                            for m, (kk, wp, xp) in enumerate(products):
                                last = nc.tensor.matmul(gu_bank[n % 4][:, i, :],
                                                        gu_part[wp][:, i, kk, f * P:(f + 1) * P],
                                                        x_part[xp][:, kk, j * SJ * P:(j + 1) * SJ * P],
                                                        start=m == 0, stop=m == len(products) - 1)
                        last.then_inc(gu_full, 1)
                    elif what == "dn" and not skipped(kind, n):
                        pe.wait_ge(hidden_ready, e * GU + (n + 1) * FT_)
                        pe.wait_ge(h_high, e * GU + (n + 1) * FT_)
                        if n == 0:
                            pe.wait_ge(w_high, (e + 1) * PIECES)
                            pe.wait_ge(w_low, (e + 1) * PIECES)
                        if kind != "mid0" or n >= 2:
                            pe.wait_ge(dn_read, e * JC + n - 1)
                        for s in range(SJ):
                            products = [(f, hp, wp) for f in range(FT_) for hp, wp in ((0, 0), (0, 1), (1, 0))]
                            for m, (f, hp, wp) in enumerate(products):
                                last = nc.tensor.matmul(dn_bank[(n + par) % 2][:, s, :],
                                                        hid_part[(n + par) % 2][hp][:, f, s * P:(s + 1) * P],
                                                        down_part[wp][:, f, :], start=m == 0,
                                                        stop=m == len(products) - 1)
                        last.then_inc(dn_full, 1)
                    elif what == "list" and kind != "end":
                        pe.wait_ge(tr_read, (e + 1) * JC)
                        make_list(e + 1)
                    elif what == "tr" and kind != "end":
                        transpose(e + 1, n, False)

            over_experts(pe, expert)


def last_norm(nc, dram, out):
    G = 4
    N = TILES // G
    with ExitStack() as ctx:
        def sb(name, shape, dt=F32):
            return ctx.enter_context(nc.sbuf_tensor(name, shape, dt))

        def sem(name):
            return ctx.enter_context(nc.semaphore(name))

        rows = [sb(f"rows{i}", [P, G, DM]) for i in range(4)]
        stats = [sb(f"stats{i}", [P, G, 6]) for i in range(4)]
        mean_var = [sb(f"mean_var{i}", [P, G, 2]) for i in range(4)]
        var_eps = [sb(f"var_eps{i}", [P, G]) for i in range(4)]
        rstd = [sb(f"rstd{i}", [P, G]) for i in range(4)]
        shift = [sb(f"shift{i}", [P, G]) for i in range(4)]
        minus_half = sb("minus_half2", [P, G])
        loaded = [sem(f"rows_in{i}") for i in range(4)]
        const_ready = sem("minus_half_ready")
        aggregated = sem("aggregated")
        var_ready = sem("var_ready2")
        rstd_ready = sem("rstd_ready2")
        shift_ready = sem("shift_ready2")
        normed = sem("normed")
        stored = [sem(f"stored{i}") for i in range(4)]
        acc_d = dram["acc"]
        out_d = out.rearrange("b s d -> (b s) d")
        block = ctx.enter_context(nc.Block())

        @block.sync
        def _(sp):
            for i in range(4):
                sp.dma_start(rows[i][:], acc_d[i * G * P:(i + 1) * G * P, :].rearrange("(g p) d -> p g d", p=P)
                             ).then_inc(loaded[i], 16)
            with sp.Fori(0, N // 4 - 1) as r:
                for i in range(4):
                    sp.wait_ge(stored[i], r * 16 + 16)
                    sp.dma_start(rows[i][:], acc_d[bass.ds((r * 4 + (4 + i)) * (G * P), G * P), :].rearrange(
                        "(g p) d -> p g d", p=P)).then_inc(loaded[i], 16)

        @block.vector
        def _(dve):
            with dve.Fori(0, N // 4) as r:
                for i in range(4):
                    n = r * 4 + i
                    dve.wait_ge(loaded[i], r * 16 + 16)
                    for g in range(G):
                        nc.vector.bn_stats(stats[i][:, g, :], rows[i][:, g, :])
                    dve.drain()
                    for g in range(G):
                        nc.vector.bn_aggr(mean_var[i][:, g, :], stats[i][:, g, :]).then_inc(aggregated, 1)
                    dve.wait_ge(aggregated, n * G + G)
                    nc.vector.tensor_scalar(var_eps[i][:], mean_var[i][:, :, 1], EPS, None, ALU.add).then_inc(var_ready, 1)
                    dve.wait_ge(rstd_ready, n + 1)
                    nc.vector.scalar_tensor_tensor(out=shift[i][:], in0=mean_var[i][:, :, 0], scalar=-1.0, in1=rstd[i][:],
                                                   op0=ALU.mult, op1=ALU.mult).then_inc(shift_ready, 1)

        @block.gpsimd
        def _(pool):
            nc.gpsimd.memset(minus_half[:], -0.5).then_inc(const_ready, 1)
            pool.wait_ge(const_ready, 1)
            with pool.Fori(0, N // 4) as r:
                for i in range(4):
                    pool.wait_ge(var_ready, r * 4 + (i + 1))
                    nc.gpsimd.tensor_tensor(rstd[i][:], var_eps[i][:], minus_half[:], ALU.pow).then_inc(rstd_ready, 1)

        @block.scalar
        def _(act):
            with act.Fori(0, N // 4) as r:
                for i in range(4):
                    n = r * 4 + i
                    act.wait_ge(shift_ready, n + 1)
                    for g in range(G):
                        nc.scalar.activation(rows[i][:, g, :], rows[i][:, g, :], ACT.Identity, bias=shift[i][:, g:g + 1],
                                             scale=rstd[i][:, g:g + 1]).then_inc(normed, 1)
                    act.wait_ge(normed, n * G + G)
                    act.dma_start(out_d[bass.ds(n * (G * P), G * P), :].rearrange("(g p) d -> p g d", p=P), rows[i][:]
                                  ).then_inc(stored[i], 16)
            for i in range(4):
                act.wait_ge(stored[i], N // 4 * 16)


def build(nc, a, out):
    with ExitStack() as ctx:
        def sb(name, shape, dt=F32):
            return ctx.enter_context(nc.sbuf_tensor(name, shape, dt))

        dram = {"b_rows": nc.dram_tensor("b_rows", [2, NST, CL], F32, kind="Internal").ap(),
                "x1": nc.dram_tensor("x1_dram", [TOK, DM], F32, kind="Internal").ap(),
                "acc": nc.dram_tensor("acc_dram", [TOK, DM], F32, kind="Internal").ap()}
        ident = sb("ident", [P, P])
        logits = sb("logits", [P, TILES * NE])
        make_ident(nc, ident)
        attention(nc, a, dram, logits, ident)
        k = {
            "slot_low": sb("slot_low", [P, 1, P], BF16),
            "slot_high": sb("slot_high", [P, 1, CAP // P], BF16),
            "tile_id": sb("tile_id", [P, TILES, 1], BF16),
            "part_id": sb("part_id", [P, 1, 1], BF16),
            "first_wins": sb("first_wins", [P, 1, NE]),
            "bit": sb("bit", [P, 1], I32),
            "threshold": sb("threshold", [P, 1], I32),
            "ones": sb("ones", [P, P]),
            "same_expert": sb("same_expert", [P, P]),
            "earlier": sb("earlier", [P, P]),
            "low": sb("slot_low_of", [P, TILES, NE], BF16),
            "high": sb("slot_high_of", [P, TILES, NE], BF16),
            "part": [sb(f"fw_part{i}", [P, TILES, NE], BF16) for i in range(3)],
        }
        make_constants(nc, k)
        route(nc, k, logits, ident)
        experts(nc, a, k, dram, ident)
        last_norm(nc, dram, out)


def kernel(**inputs):
    import numpy as np
    import concourse.bacc as bacc
    from concourse.bass_utils import run_bass_kernel_spmd

    nc = bacc.Bacc("TRN2", target_bir_lowering=False, num_devices=1)
    g = {k.replace("L0_attn_", "").replace("L0_ffn_", ""): np.asarray(v) for k, v in inputs.items()}
    laid = {
        "x": g["x"], "xT": g["x"].reshape(TOK, DM).T, "W_in": g["W_in"], "W_conv": g["W_conv"], "W_x": g["W_x"],
        "W_dt": g["W_dt"], "b_dt": g["b_dt"].reshape(DT, P).T, "D_param": g["D_param"].reshape(DT, P).T,
        "A_log": g["A_log"], "W_out": g["W_out"], "router_wT": g["router_w"].T,
        "wg": g["wg"], "wu": g["wu"], "wd": g["wd"],
    }
    laid = {k: np.ascontiguousarray(v) for k, v in laid.items()}
    aps = {k: nc.dram_tensor(f"in_{k}", v.shape, mybir.dt.from_np(v.dtype), kind="ExternalInput").ap()
           for k, v in laid.items()}
    out = nc.dram_tensor("out", (BATCH, SEQ, DM), F32, kind="ExternalOutput").ap()
    build(nc, aps, out)
    ran = run_bass_kernel_spmd(nc, [{f"in_{k}": v for k, v in laid.items()}], core_ids=[0])
    return ran.results[0]["out"]
```

```python
from contextlib import ExitStack

import concourse.bass as bass
from concourse import mybir

F32 = mybir.dt.float32
F32R = mybir.dt.float32r
BF16 = mybir.dt.bfloat16
I32 = mybir.dt.int32
U32 = mybir.dt.uint32
ACT = mybir.ActivationFunctionType
ALU = mybir.AluOpType
AX = mybir.AxisListType

P = 128
BATCH, SEQ, DM = 8, 1024, 256
TOK = BATCH * SEQ
DI, NST, RANK = 512, 16, 16
XD = RANK + 2 * NST
CL = 512
CHUNKS = TOK // CL
DT = DI // P
LT = CL // P
KD = DM // P
TILES = TOK // P
EPS = 1e-5
HIGH_BITS = -1 << 12
EXP_AND_LOG = "natural_log_exp_and_others"
NE, FF = 8, 1024
CAP = max(1, int(1.25 * TOK / NE))

PROJECT = [f"u{t}" for t in range(DT)] + [f"r{l}" for l in range(LT)] + ["xd", "cT"] + \
          [f"d{t}" for t in range(DT)] + [f"ud{l}" for l in range(LT)]
CLOSE = [f"yT{t}" for t in range(DT)] + ["o0", "o1", "xt0", "xt1", "lg"]
SLOT = {"u0": (1, 2), "u1": (3, 2), "u2": (5, 2), "u3": (7, 2), "r0": (7, 2), "r1": (9, 2),
        "yT0": (14, 1), "yT1": (15, 1), "xd": (18, 4), "yT2": (19, 1), "yT3": (22, 1), "d0": (23, 1),
        "d1": (24, 1), "d2": (26, 1), "d3": (27, 1), "cT": (29, 1), "o0": (30, 5), "o1": (35, 5),
        "r2": (40, 2), "r3": (42, 2), "ud0": (44, 1), "ud1": (46, 1), "xt0": (47, 1), "xt1": (49, 1),
        "lg": (51, 4), "ud2": (51, 1), "ud3": (56, 1)}
SLOTS = NST * DT
READ_BEHIND = 8
READ_SLOT = {name: min(first + parts - 1 + READ_BEHIND, SLOTS - 1) for name, (first, parts) in SLOT.items()}
USES = {"first": [n for n in SLOT if n in PROJECT],
        "mid": list(SLOT),
        "last": [n for n in SLOT if n in CLOSE]}

DBU = [n % 3 for n in range(NST - 1)] + [1]
DBU_BACK = [next(k for k in range(1, NST) if DBU[(n - k) % NST] == DBU[n]) for n in range(NST)]
BG = 2
GROUPS = NST // BG

GATE_AT = (1, 2, 3, 4)
DU_AT = (13, 14, 14, 15)
RSTD_AT = 12

SILU_U_SLOT, SILU_GATE_SLOT, SOFT_SLOTS, NORM_SLOT = 18, 1, (38, 41), 52
CONV_SLOT = {7 + 2 * t + step: (t, 1 - step) for t in range(DT) for step in range(2)}
DELTA_SLOT = (50, 52, 54, 57)
HISTORY_SLOT, STATS_SLOT = 18, (43, 47)


def count_of(c, name):
    if name in PROJECT:
        return (c + 1) * len(PROJECT) + [n for n in SLOT if n in PROJECT].index(name) + 1
    return (c - 1) * len(CLOSE) + [n for n in SLOT if n in CLOSE].index(name) + 1


def bank_of(parity, kind, name):
    k = USES[kind].index(name)
    swapped = {"first": 0, "mid": 1 - parity, "last": 1 - parity}[kind]
    return (k + swapped) % 2


def two_before(c, kind, name):
    k = USES[kind].index(name)
    if k >= 2:
        return c, USES[kind][k - 2]
    if kind == "first" and isinstance(c, int) and c < 0:
        return None
    before = USES["last"] if kind == "last" and isinstance(c, int) and c == CHUNKS else USES["first"]
    return c - 1, before[k - 2]


def over_chunks(eng, emit):
    emit(-1, 1, "first", False)
    emit(0, 0, "first", True)
    with eng.Fori(0, (CHUNKS - 2) // 2) as i:
        emit(i * 2 + 1, 1, "mid", True)
        emit(i * 2 + 2, 0, "mid", True)
    emit(CHUNKS - 1, 1, "last", True)
    emit(CHUNKS, 0, "last", False)


def attention(nc, a, dram, logits, ident):
    with ExitStack() as ctx:
        def sb(name, shape, dt=F32):
            return ctx.enter_context(nc.sbuf_tensor(name, shape, dt))

        def sem(name):
            return ctx.enter_context(nc.semaphore(name))

        w_in = sb("w_in", [P, KD, 2 * DI])
        w_x = sb("w_x", [P, DT, XD])
        w_dt = sb("w_dt", [RANK, DI])
        w_out = sb("w_out", [P, DT, DM])
        w_rt = sb("w_rt", [P, KD, NE])
        w_conv = sb("w_conv", [P, DT, 3])
        b_dt = sb("b_dt", [P, DT])
        d_par = sb("d_par", [P, DT])
        a_log = sb("a_log", [P, DT, NST])
        a_exp = sb("a_exp", [P, DT, NST])
        a_neg = sb("a_neg", [P, DT, NST])
        diag_d = sb("diag_d", [P, DT, P])
        xT = sb("xT", [P, KD, CL])
        x_rows = sb("x_rows", [P, LT, DM])
        u_pad = sb("u_pad", [P, DT, CL + 2])
        tmp = sb("tmp", [P, DT, CL])
        u = sb("u", [P, DT, CL])
        gate = [sb(f"gate{i}", [P, LT, DI]) for i in range(2)]
        delta = [sb(f"delta{i}", [P, DT, CL]) for i in range(2)]
        du = [sb(f"du{i}", [P, DT, CL]) for i in range(2)]
        xdT = sb("xdT", [XD, CL])
        c_tok = [sb(f"c_tok{i}", [P, LT, XD]) for i in range(2)]
        yacc = [sb(f"yacc{i}", [P, LT, DI]) for i in range(2)]
        b_all = [sb(f"b_all{i}", [P, BG, CL]) for i in range(2)]
        dbu = [sb(f"dbu{i}", [P, DT, CL]) for i in range(3)]
        hst = [sb(f"hst{i}", [P, DT, CL]) for i in range(2)]
        carry = sb("carry", [P, NST, DT])
        yT = sb("yT", [P, DT, CL])
        resid = sb("resid", [P, LT, DM])
        x1 = sb("x1", [P, LT, DM])
        x1T = sb("x1T", [P, KD, CL])
        row_sum = sb("row_sum_x", [P, LT])
        var = sb("var", [P, LT])
        one_by_dm = sb("one_by_dm", [P, LT])
        eps = sb("eps", [P, LT])
        sq_sum = sb("sq_sum", [P, LT])
        var_eps = sb("var_eps", [P, LT])
        minus_mean = sb("minus_mean", [P, LT])
        minus_half = sb("minus_half", [P, LT])
        rstd = sb("rstd", [P, LT])
        shift = sb("shift", [P, LT])
        da_bank = [ctx.enter_context(nc.psum_tensor(f"da{i}", [P, CL], F32)) for i in range(DT)]
        ht_bank = [ctx.enter_context(nc.psum_tensor(f"ht{i}", [P, DI], F32)) for i in range(2)]
        gen_bank = [ctx.enter_context(nc.psum_tensor(f"gen{i}", [P, 512], F32)) for i in range(2)]

        weights_in = sem("weights_in")
        setup = sem("setup")
        a_step = sem("a_step")
        xt_loaded = sem("xt_loaded")
        rows_loaded = sem("rows_loaded")
        full = {True: sem("project_full"), False: sem("close_full")}
        read = {True: sem("project_read"), False: sem("close_read")}
        conv_step = sem("conv_step")
        pad_ready = sem("pad_ready")
        u_ready = sem("u_ready")
        gate_ready = sem("gate_ready")
        soft_step = sem("soft_step")
        delta_ready = sem("delta_ready")
        du_ready = sem("du_ready")
        b_stored = sem("b_stored")
        b_loaded = [sem(f"b_loaded{i}") for i in range(2)]
        dbu_ready = sem("dbu_ready")
        da_ready = sem("da_ready")
        scanned = sem("scanned")
        carried = sem("carried")
        ht_ready = sem("ht_ready")
        summed = sem("summed")
        gated = sem("gated")
        mean_ready = sem("mean_ready")
        squares_ready = sem("squares_ready")
        var_ready = sem("var_ready")
        rstd_ready = sem("rstd_ready")
        shift_ready = sem("shift_ready")
        x1_ready = sem("x1_ready")
        x1_stored = sem("x1_stored")
        N_WEIGHTS = 9

        xT_d = a["xT"].rearrange("(k p) t -> p k t", p=P)
        rows_d = a["x"].rearrange("b s d -> (b s) d")
        b_rows = dram["b_rows"]

        def wait_full(eng, c, name):
            eng.wait_ge(full[name in PROJECT], count_of(c, name))

        def wait_read(eng, c, name):
            eng.wait_ge(read[name in PROJECT], count_of(c, name))

        block = ctx.enter_context(nc.Block())

        @block.sync
        def _(sp):
            for dst, src in ((w_in, a["W_in"].rearrange("(k p) n -> p k n", p=P)),
                             (w_x, a["W_x"].rearrange("(k p) n -> p k n", p=P)),
                             (w_dt, a["W_dt"]),
                             (w_out, a["W_out"].rearrange("(k p) n -> p k n", p=P)),
                             (w_rt, a["router_wT"].rearrange("(k p) n -> p k n", p=P)),
                             (w_conv, a["W_conv"].rearrange("(k p) n -> p k n", p=P)),
                             (b_dt, a["b_dt"]),
                             (d_par, a["D_param"]),
                             (a_log, a["A_log"].rearrange("(k p) n -> p k n", p=P))):
                sp.dma_start(dst[:], src).then_inc(weights_in, 16)

            def chunk(c, parity, kind, main):
                def value(x):
                    return x if isinstance(x, int) else sp.snap(x)

                xd_now, o1_now = value(count_of(c, "xd")), value(count_of(c, "o1"))
                used = [value(c * NST + BG * (g - 1)) for g in range(GROUPS)]
                normalised, rows_of_b = value(c * LT), value(c * 16 + 16)
                token0, token_prev = value(c * CL), value((c - 1) * CL)
                if main:
                    sp.wait_ge(b_stored, rows_of_b)
                if kind != "last":
                    sp.dma_start(xT[:], xT_d[:, :, bass.ds(token0 + CL, CL)]).then_inc(xt_loaded, 16)
                for g in range(GROUPS):
                    if g == GROUPS - 1 and kind != "last":
                        sp.wait_ge(read[True], xd_now)
                        sp.dma_start(b_rows[1 - parity, :, :], xdT[RANK:RANK + NST, :]).then_inc(b_stored, 16)
                    if main:
                        if kind != "first" or g >= 2:
                            sp.wait_ge(dbu_ready, used[g])
                        src = b_rows[parity:parity + 1, BG * g:BG * (g + 1), :]
                        sp.dma_start(b_all[g % 2][:], src.to_broadcast([P, BG, CL])).then_inc(b_loaded[g % 2], 16)
                if kind != "first":
                    sp.wait_ge(x1_ready, normalised)
                    for dst in (dram["x1"], dram["acc"]):
                        sp.dma_start(dst[bass.ds(token_prev, CL), :].rearrange("(l p) d -> p l d", p=P),
                                     x1[:]).then_inc(x1_stored, 16)
                if main:
                    if kind != "first":
                        sp.wait_ge(read[False], o1_now)
                    sp.dma_start(x_rows[:], rows_d[bass.ds(token0, CL), :].rearrange("(l p) d -> p l d", p=P)
                                 ).then_inc(rows_loaded, 16)
                if kind == "first":
                    sp.wait_ge(read[True], count_of(c, "r3"))

            over_chunks(sp, chunk)
            sp.wait_ge(x1_stored, CHUNKS * 32)

        @block.gpsimd
        def _(pool):
            nc.gpsimd.memset(minus_half[:], -0.5)
            nc.gpsimd.memset(one_by_dm[:], 1.0 / DM)
            nc.gpsimd.memset(eps[:], EPS).then_inc(setup, 1)
            pool.wait_ge(setup, 1)

            def chunk(c, parity, kind, main):
                other = 1 - parity
                for n in range(NST):
                    if main:
                        if n == 0:
                            pool.wait_ge(du_ready, (c + 1) * DT)
                        if n % BG == 0:
                            pool.wait_ge(b_loaded[n // BG % 2], c * (GROUPS * 8) + n // (2 * BG) * 16 + 16)
                        if kind != "first" or n >= 3:
                            pool.wait_ge(scanned, c * 64 + 4 * (n - DBU_BACK[n]) + 4)
                        b_n = b_all[n // BG % 2][:, n % BG:n % BG + 1, :].to_broadcast([P, DT, CL])
                        nc.gpsimd.tensor_tensor(dbu[DBU[n]][:], du[parity][:], b_n, ALU.mult).then_inc(dbu_ready, 1)
                    for l in range(LT):
                        if n == GATE_AT[l] and kind != "first":
                            pool.wait_ge(summed, (c - 1) * 64 + 61 + l)
                            if l == 0:
                                pool.wait_ge(gate_ready, c)
                            nc.gpsimd.tensor_tensor(yacc[other][:, l, :], yacc[other][:, l, :], gate[other][:, l, :],
                                                    ALU.mult).then_inc(gated, 1)
                    if n == RSTD_AT and kind != "first":
                        pool.wait_ge(squares_ready, c * 2)
                        nc.gpsimd.tensor_tensor(var[:], sq_sum[:], one_by_dm[:], ALU.mult).then_inc(var_ready, 1)
                        pool.wait_ge(var_ready, c * 2 - 1)
                        nc.gpsimd.tensor_tensor(var_eps[:], var[:], eps[:], ALU.add).then_inc(var_ready, 1)
                        pool.wait_ge(var_ready, c * 2)
                        nc.gpsimd.tensor_tensor(rstd[:], var_eps[:], minus_half[:], ALU.pow).then_inc(rstd_ready, 1)
                        pool.wait_ge(rstd_ready, c)
                        nc.gpsimd.tensor_tensor(shift[:], minus_mean[:], rstd[:], ALU.mult).then_inc(shift_ready, 1)
                    for t in range(DT):
                        if n == DU_AT[t] and kind != "last":
                            pool.wait_ge(delta_ready, (c + 1) * DT + t + 1)
                            nc.gpsimd.tensor_tensor(du[other][:, t, :], delta[other][:, t, :], u[:, t, :], ALU.mult
                                                    ).then_inc(du_ready, 1)

            over_chunks(pool, chunk)

        @block.scalar
        def _(act):
            act.wait_ge(weights_in, N_WEIGHTS * 16)
            nc.scalar.activation(a_exp[:], a_log[:], ACT.Exp).then_inc(a_step, 1)
            act.wait_ge(a_step, 1)
            nc.scalar.activation(a_neg[:], a_exp[:], ACT.Copy, scale=-1.0).then_inc(a_step, 1)
            act.wait_ge(a_step, 2)
            nc.scalar.preload_act_table_set(EXP_AND_LOG)

            def copy_out(c, parity, kind, main, name):
                other = 1 - parity
                bank = gen_bank[bank_of(parity, kind, name)]
                project = name in PROJECT
                wait_full(act, c, name)
                what, j = name.rstrip("0123"), int(name[-1]) if name[-1].isdigit() else 0
                if what == "u":
                    if j == 0:
                        act.wait_ge(pad_ready, c + 2)
                        if main:
                            act.wait_ge(delta_ready, (c + 1) * DT)
                    nc.scalar.activation(u_pad[:, j, 2:], bank[:], ACT.Copy)
                    last = nc.scalar.activation(tmp[:, j, :], bank[:], ACT.Copy, scale=w_conv[:, j, 2:3])
                elif what == "r":
                    if kind != "first":
                        act.wait_ge(gated, (c - 1) * LT + j + 1)
                    last = nc.scalar.activation(gate[other][:, j, :], bank[:], ACT.Copy)
                elif what == "xd":
                    if main:
                        act.wait_ge(b_stored, c * 16 + 16)
                    last = nc.scalar.activation(xdT[:], bank[0:XD, :], ACT.Copy)
                elif what == "cT":
                    if kind != "first":
                        act.wait_ge(summed, c * 64)
                    last = nc.scalar.activation(c_tok[other][:], bank[:, 0:LT * XD].rearrange(
                        "p (l n) -> p l n", l=LT), ACT.Copy)
                elif what == "d":
                    if j == 0:
                        act.wait_ge(u_ready, c + 2)
                    nc.scalar.activation(tmp[:, j, :], bank[:], ACT.Abs, bias=b_dt[:, j:j + 1])
                    last = nc.scalar.activation(delta[other][:, j, :], bank[:], ACT.Relu, bias=b_dt[:, j:j + 1])
                elif what == "ud":
                    last = nc.scalar.activation(yacc[other][:, j, :], bank[:], ACT.Copy)
                elif what == "yT":
                    last = nc.scalar.activation(yT[:, j, :], bank[:], ACT.Copy)
                elif what == "o":
                    for l in (2 * j, 2 * j + 1):
                        last = nc.scalar.activation(resid[:, l, :], bank[:, l % 2 * DM:(l % 2 + 1) * DM], ACT.Copy,
                                                    accum_out=row_sum[:, l:l + 1])
                elif what == "xt":
                    last = nc.scalar.activation(x1T[:, j, :], bank[:], ACT.Copy)
                else:
                    dst = logits[:, bass.ds((c - 1) * (LT * NE), LT * NE)]
                    last = nc.scalar.activation(dst, bank[:, 0:LT * NE], ACT.Copy)
                last.then_inc(read[project], 1)

            def chunk(c, parity, kind, main):
                other = 1 - parity
                for slot in range(SLOTS):
                    n, t = slot // DT, slot % DT
                    if main:
                        if slot == 0:
                            act.wait_ge(delta_ready, (c + 1) * DT)
                        if kind != "first" or n >= 1:
                            act.wait_ge(scanned, c * 64 + slot - 3)
                        nc.scalar.activation(da_bank[t][:], delta[parity][:, t, :], ACT.Exp,
                                             scale=a_neg[:, t, n:n + 1]).then_inc(da_ready, 1)
                    if slot == SILU_U_SLOT and kind != "last":
                        act.wait_ge(conv_step, (c + 2) * 2 * DT)
                        if main:
                            act.wait_ge(du_ready, (c + 1) * DT)
                        nc.scalar.activation(u[:], tmp[:], ACT.Silu).then_inc(u_ready, 1)
                        nc.scalar.preload_act_table_set(EXP_AND_LOG)
                    for name in USES[kind]:
                        if READ_SLOT[name] == slot:
                            copy_out(c, parity, kind, main, name)
                    if slot == SOFT_SLOTS[0] and kind != "last":
                        wait_read(act, c, "d3")
                        nc.scalar.activation(tmp[:], tmp[:], ACT.Exp, scale=-1.0).then_inc(soft_step, 1)
                    if slot == SOFT_SLOTS[1] and kind != "last":
                        act.wait_ge(soft_step, 2 * (c + 1) + 1)
                        nc.scalar.activation(tmp[:], tmp[:], ACT.Ln, bias=1.0).then_inc(soft_step, 1)
                    if slot in STATS_SLOT and kind != "first":
                        j = STATS_SLOT.index(slot)
                        wait_read(act, c, f"o{j}")
                        nc.scalar.activation(minus_mean[:, 2 * j:2 * j + 2], row_sum[:, 2 * j:2 * j + 2], ACT.Copy,
                                             scale=-1.0 / DM).then_inc(mean_ready, 1)
                        act.wait_ge(mean_ready, (c - 1) * 2 + j + 1)
                        for l in (2 * j, 2 * j + 1):
                            last = nc.scalar.activation(x1[:, l, :], resid[:, l, :], ACT.Square,
                                                        bias=minus_mean[:, l:l + 1], accum_out=sq_sum[:, l:l + 1])
                        last.then_inc(squares_ready, 1)
                    if slot == NORM_SLOT and kind != "first":
                        act.wait_ge(squares_ready, c * 2)
                        act.wait_ge(shift_ready, c)
                        for l in range(LT):
                            nc.scalar.activation(x1[:, l, :], resid[:, l, :], ACT.Identity, bias=shift[:, l:l + 1],
                                                 scale=rstd[:, l:l + 1]).then_inc(x1_ready, 1)
                    if slot == SILU_GATE_SLOT and main:
                        wait_read(act, c - 1, "r3")
                        nc.scalar.activation(gate[parity][:], gate[parity][:], ACT.Silu).then_inc(gate_ready, 1)
                        nc.scalar.preload_act_table_set(EXP_AND_LOG)
                if kind != "first":
                    act.wait_ge(x1_stored, c * 32)

            over_chunks(act, chunk)

        @block.vector
        def _(dve):
            dve.wait_ge(weights_in, N_WEIGHTS * 16)
            for t in range(DT):
                nc.vector.tensor_scalar(diag_d[:, t, :], ident[:], d_par[:, t:t + 1], None, ALU.mult
                                        ).then_inc(setup, 1)
            nc.vector.memset(u_pad[:, :, 0:2], 0.0).then_inc(pad_ready, 1)

            def add_state(c, parity, n, l):
                dve.wait_ge(ht_ready, c * 64 + 4 * n + l + 1)
                if n == 0:
                    wait_read(dve, c - 1, f"ud{l}")
                else:
                    dve.wait_ge(summed, c * 64 + 4 * (n - 1) + l + 1)
                nc.vector.scalar_tensor_tensor(
                    out=yacc[parity][:, l, :], in0=ht_bank[l % 2][:],
                    scalar=c_tok[parity][:, l, RANK + NST + n:RANK + NST + n + 1],
                    in1=yacc[parity][:, l, :], op0=ALU.mult, op1=ALU.add).then_inc(summed, 1)

            def chunk(c, parity, kind, main):
                other = 1 - parity
                for slot in range(SLOTS):
                    n, t = slot // DT, slot % DT
                    if main:
                        dve.wait_ge(da_ready, c * 64 + slot + 1)
                        if t == 0:
                            dve.wait_ge(dbu_ready, c * NST + n + 1)
                            if kind != "first" or n >= 2:
                                dve.wait_ge(ht_ready, c * 64 + 4 * (n - 1))
                            if parity == 1 and n < 2:
                                dve.wait_ge(carried, (c - 1) * (NST // 2) + NST - 1 + n)
                            if parity == 0 and n >= 2:
                                dve.wait_ge(carried, c * (NST // 2) + n - 1)
                        initial = carry[:, n, t:t + 1] if parity == 1 else 0.0
                        nc.vector.tensor_tensor_scan(hst[n % 2][:, t, :], da_bank[t][:], dbu[DBU[n]][:, t, :],
                                                     initial, ALU.mult, ALU.add).then_inc(scanned, 1)
                    if main and n > 0:
                        add_state(c, parity, n - 1, t)
                    if n == 0 and kind != "first":
                        add_state(c - 1, other, NST - 1, t)
                    if t == 1 and (main and parity == 0 and n > 0 or main and parity == 1 and n == 0):
                        m = (n - 1) % NST
                        dve.wait_ge(scanned, c * 64 + 4 * n)
                        nc.vector.tensor_copy(carry[:, m, :], hst[m % 2][:, :, CL - 1]).then_inc(carried, 1)
                    if kind != "last" and slot in CONV_SLOT:
                        tile, tap = CONV_SLOT[slot]
                        if tap == 1:
                            wait_read(dve, c, f"u{tile}")
                        else:
                            dve.wait_ge(conv_step, (c + 1) * 2 * DT + 2 * tile + 1)
                        nc.vector.scalar_tensor_tensor(
                            out=tmp[:, tile, :], in0=u_pad[:, tile, tap:tap + CL], scalar=w_conv[:, tile, tap:tap + 1],
                            in1=tmp[:, tile, :], op0=ALU.mult, op1=ALU.add).then_inc(conv_step, 1)
                    if kind != "last" and slot in DELTA_SLOT:
                        tile = DELTA_SLOT.index(slot)
                        if tile == 0:
                            dve.wait_ge(soft_step, 2 * (c + 2))
                        nc.vector.tensor_tensor(delta[other][:, tile, :], delta[other][:, tile, :], tmp[:, tile, :],
                                                ALU.add).then_inc(delta_ready, 1)
                    if kind != "last" and slot == HISTORY_SLOT:
                        dve.wait_ge(conv_step, (c + 2) * 2 * DT)
                        if parity == 1:
                            nc.vector.tensor_copy(u_pad[:, :, 0:2], u_pad[:, :, CL:CL + 2]).then_inc(pad_ready, 1)
                        else:
                            nc.vector.memset(u_pad[:, :, 0:2], 0.0).then_inc(pad_ready, 1)

            over_chunks(dve, chunk)

        @block.tensor
        def _(pe):
            pe.wait_ge(weights_in, N_WEIGHTS * 16)
            pe.wait_ge(setup, 1 + DT)

            def fill(c, parity, kind, name, part):
                other = 1 - parity
                bank = gen_bank[bank_of(parity, kind, name)]
                parts = SLOT[name][1]
                before = two_before(c, kind, name)
                if part == 0 and before is not None:
                    wait_read(pe, *before)
                what, j = name.rstrip("0123"), int(name[-1]) if name[-1].isdigit() else 0
                if what == "u":
                    if name == "u0" and part == 0:
                        pe.wait_ge(xt_loaded, c * 16 + 32)
                    last = nc.tensor.matmul(bank[:], w_in[:, part, j * P:(j + 1) * P], xT[:, part, :],
                                            start=part == 0, stop=part == KD - 1)
                elif what == "r":
                    last = nc.tensor.matmul(bank[:], xT[:, part, j * P:(j + 1) * P], w_in[:, part, DI:],
                                            start=part == 0, stop=part == KD - 1)
                elif what == "xd":
                    if part == 0:
                        pe.wait_ge(u_ready, c + 2)
                    last = nc.tensor.matmul(bank[0:XD, :], w_x[:, part, :], u[:, part, :], start=part == 0,
                                            stop=part == DT - 1)
                elif what == "cT":
                    for l in range(LT):
                        last = nc.tensor.matmul(bank[:, l * XD:(l + 1) * XD], xdT[:, l * P:(l + 1) * P],
                                                ident[0:XD, 0:XD], start=True, stop=True)
                elif what == "d":
                    if j == 0:
                        wait_read(pe, c, "xd")
                    last = nc.tensor.matmul(bank[:], w_dt[:, j * P:(j + 1) * P], xdT[0:RANK, :], start=True, stop=True)
                elif what == "ud":
                    for t in range(DT):
                        last = nc.tensor.matmul(bank[:, t * P:(t + 1) * P], u[:, t, j * P:(j + 1) * P],
                                                diag_d[:, t, :], start=True, stop=True)
                elif what == "yT":
                    if j == 0:
                        pe.wait_ge(gated, c * LT)
                    for l in range(LT):
                        last = nc.tensor.transpose(bank[:, l * P:(l + 1) * P], yacc[other][:, l, j * P:(j + 1) * P],
                                                   ident[:])
                elif what == "o":
                    if name == "o0" and part == 0:
                        wait_read(pe, c, "yT3")
                        pe.wait_ge(rows_loaded, c * 16)
                    for l, t in [(l, t) for l in (2 * j, 2 * j + 1) for t in range(DT + 1)][2 * part:2 * part + 2]:
                        acc = bank[:, l % 2 * DM:(l % 2 + 1) * DM]
                        if t < DT:
                            nc.tensor.matmul(acc, yT[:, t, l * P:(l + 1) * P], w_out[:, t, :], start=t == 0, stop=False)
                        else:
                            last = nc.tensor.matmul(acc, ident[:], x_rows[:, l, :], start=False, stop=True)
                elif what == "xt":
                    if j == 0:
                        pe.wait_ge(x1_ready, c * LT)
                    for l in range(LT):
                        last = nc.tensor.transpose(bank[:, l * P:(l + 1) * P], x1[:, l, j * P:(j + 1) * P], ident[:])
                else:
                    if part == 0:
                        wait_read(pe, c, "xt1")
                    for k in range(KD):
                        last = nc.tensor.matmul(bank[:, part * NE:(part + 1) * NE], x1T[:, k, part * P:(part + 1) * P],
                                                w_rt[:, k, :], start=k == 0, stop=k == KD - 1)
                if part == parts - 1:
                    last.then_inc(full[name in PROJECT], 1)

            def chunk(c, parity, kind, main):
                for slot in range(SLOTS):
                    n, l = slot // LT, slot % LT
                    if main:
                        if l == 0:
                            pe.wait_ge(scanned, c * 64 + 4 * n + 4)
                        if kind != "first" or n > 0 or l >= 2:
                            pe.wait_ge(summed, c * 64 + slot - 1)
                        for t in range(DT):
                            last = nc.tensor.transpose(ht_bank[l % 2][:, t * P:(t + 1) * P],
                                                       hst[n % 2][:, t, l * P:(l + 1) * P], ident[:])
                        last.then_inc(ht_ready, 1)
                    for name in USES[kind]:
                        first, parts = SLOT[name]
                        if first <= slot < first + parts:
                            fill(c, parity, kind, name, slot - first)

            over_chunks(pe, chunk)


def make_ident(nc, ident):
    with nc.semaphore("ident_step") as ident_step, nc.Block() as block:
        @block.gpsimd
        def _(pool):
            nc.gpsimd.memset(ident[:], 0.0).then_inc(ident_step, 1)
            pool.wait_ge(ident_step, 1)
            nc.gpsimd.affine_select(out=ident[:], in_=ident[:], compare_op=ALU.not_equal, fill=1.0, base=0,
                                    pattern=[[-1, P]], channel_multiplier=1).then_inc(ident_step, 1)
            pool.wait_ge(ident_step, 2)


def make_constants(nc, k):
    with ExitStack() as ctx:
        f = ctx.enter_context(nc.sbuf_tensor("int_table", [P, P], I32))
        g = ctx.enter_context(nc.sbuf_tensor("same_rest", [P, P], I32))
        h = ctx.enter_context(nc.sbuf_tensor("above", [P, P], F32))
        made = ctx.enter_context(nc.semaphore("tables_made"))
        step = ctx.enter_context(nc.semaphore("masks_step"))
        block = ctx.enter_context(nc.Block())

        @block.gpsimd
        def _(pool):
            exact = {"allow_small_or_imprecise_dtypes": True}
            nc.gpsimd.iota(k["slot_low"][:], [[1, P]], 0, 0, **exact).then_inc(made, 1)
            nc.gpsimd.iota(k["slot_high"][:], [[1, CAP // P]], 0, 0, **exact).then_inc(made, 1)
            nc.gpsimd.iota(k["tile_id"][:], [[1, TILES]], 0, 0, **exact).then_inc(made, 1)
            nc.gpsimd.iota(k["part_id"][:], [[0, 1]], 0, 1, **exact).then_inc(made, 1)
            nc.gpsimd.iota(k["first_wins"][:], [[-1, NE]], NE, 0, **exact).then_inc(made, 1)
            nc.gpsimd.iota(f[:], [[1, P]], P, -1).then_inc(made, 1)
            nc.gpsimd.memset(k["bit"][:], 1 << 29).then_inc(made, 1)
            nc.gpsimd.memset(k["threshold"][:], 0).then_inc(made, 1)
            nc.gpsimd.memset(k["ones"][:], 1.0).then_inc(made, 1)
            pool.wait_ge(made, 9)

        @block.vector
        def _(dve):
            dve.wait_ge(made, 9)
            nc.vector.tensor_scalar(g[:], f[:], NE - 1, None, ALU.bitwise_and).then_inc(step, 1)
            nc.vector.tensor_scalar(h[:], f[:], float(P), None, ALU.is_gt).then_inc(step, 1)
            dve.wait_ge(step, 2)
            nc.vector.tensor_scalar(k["same_expert"][:], g[:], 0.0, None, ALU.is_equal).then_inc(step, 1)
            dve.wait_ge(step, 3)
            nc.vector.tensor_tensor(k["earlier"][:], k["same_expert"][:], h[:], ALU.mult).then_inc(step, 1)
            dve.wait_ge(step, 4)


ST = CAP // P
SJ = 2
JC = ST // SJ
FT_ = FF // P
PIECE = 2 * KD * P
PIECES = FT_ + FT_ // 2
PREPARE_AT, LIST_AT, TR_AT = 4, 19, (30, 32, 34, 36, 39)
DOWN_PIECE_AT = (4, 5, 6, 7)
FIRST_TR_AT = (0, 2, 4, 6)
NV = 5


def weight_buffers(nc, ctx):
    def sb(name, shape, dt=F32):
        return ctx.enter_context(nc.sbuf_tensor(name, shape, dt))

    def sem(name):
        return ctx.enter_context(nc.semaphore(name))

    raw = sb("w_raw", [P, PIECES * PIECE])
    part = [sb(f"w_part{i}", [P, PIECES * PIECE], F32R) for i in range(2)]

    def gate_up(t):
        return t[:, 0:FT_ * PIECE].rearrange("p (i k f) -> p i k f", i=2, k=KD)

    def down(t):
        return t[:, FT_ * PIECE:].rearrange("p (k d) -> p k d", k=FT_)

    return {
        "raw": raw, "part": part,
        "gu_raw": gate_up(raw), "down_raw": down(raw),
        "gu_part": [gate_up(t) for t in part], "down_part": [down(t) for t in part],
        "mask": [sb(f"w_mask{i}", [P, PIECE], I32) for i in range(3)],
        "loaded": sem("expert_loaded"),
        "masked": sem("w_masked"),
        "high": sem("w_high"),
        "low": sem("w_low"),
    }


def load_weights(sp, a, w, e):
    for i, name in enumerate(("wg", "wu")):
        sp.dma_start(w["gu_raw"][:, i], a[name].rearrange("e d f -> (e d) f")[bass.ds(e * DM, DM), :]
                     .rearrange("(k p) f -> p k f", p=P)).then_inc(w["loaded"], 16)
    sp.dma_start(w["down_raw"], a["wd"].rearrange("e f d -> (e f) d")[bass.ds(e * FF, FF), :]
                 .rearrange("(k p) d -> p k d", p=P)).then_inc(w["loaded"], 16)


def raw_piece(w, p):
    def cut(gu, down):
        return gu[:, :, :, p * P:(p + 1) * P] if p < FT_ else down[:, 2 * (p - FT_):2 * (p - FT_) + 2, :]
    return cut(w["gu_raw"], w["down_raw"]), [cut(w["gu_part"][i], w["down_part"][i]) for i in range(2)]


def mask_of(w, p, dtype):
    flat = w["mask"][p % 3][:] if dtype == I32 else w["mask"][p % 3][:].bitcast(dtype)
    return flat.rearrange("p (i k f) -> p i k f", i=2, k=KD) if p < FT_ else \
        flat.rearrange("p (k d) -> p k d", k=2)


def route(nc, a, k, w, logits, ident):
    with ExitStack() as ctx:
        def sb(name, shape, dt=F32):
            return ctx.enter_context(nc.sbuf_tensor(name, shape, dt))

        def sem(name):
            return ctx.enter_context(nc.semaphore(name))

        full3 = [P, TILES, NE]
        row_max = sb("row_max", [P, TILES, 1])
        shifted = sb("shifted", full3)
        probs = sb("probs", full3)
        row_sum = sb("row_sum", [P, TILES, 1])
        top = [sb(f"top{i}", [P, TILES, 1]) for i in range(2)]
        mask = [sb(f"mask{i}", full3) for i in range(2)]
        equal = sb("equal", full3)
        key = sb("key", full3)
        key_max = sb("key_max", [P, TILES, 1])
        rest = sb("rest", full3)
        weight = [sb(f"weight{i}", [P, TILES, 1]) for i in range(2)]
        fw = sb("fw", full3)
        ft = sb("ft", [P, 4, P])
        flags = sb("flags", [P, 4, P])
        above = sb("above_t", [P, 4, P])
        tied = sb("tied", [P, 4, P])
        rank = sb("rank", [P, 4, P])
        code = sb("code", [P, 4, P])
        count = sb("count", [P, 1])
        candidate = sb("candidate", [P, 1], I32)
        accept = sb("accept", [P, 1], I32)
        need = sb("need", [P, 1])
        seg = sb("seg", [P, 4])
        seg_sum = sb("seg_sum", [P, 4])
        seg_before = sb("seg_before", [P, 4])
        slot = sb("slot", [P, TILES * NE], I32)
        low = sb("low", [P, TILES * NE], I32)
        high = sb("high", [P, TILES * NE], I32)
        left = [sb(f"left{i}", full3) for i in range(2)]
        bank = ctx.enter_context(nc.psum_tensor("flip", [P, 512], F32))
        total = ctx.enter_context(nc.psum_tensor("total", [P, 1], F32))
        before = ctx.enter_context(nc.psum_tensor("before", [P, 4], F32))

        step = sem("route_step")
        shifted_ready = sem("shifted_ready")
        exp_ready = sem("exp_ready")
        fw_ready = sem("fw_ready")
        flipped = sem("flipped")
        counted = sem("counted")
        totalled = sem("totalled")
        segments = sem("segments")
        offsets = sem("offsets")
        code_ready = sem("code_ready")
        BITS = 30
        AT_ONCE = 5
        assert BITS // AT_ONCE * 2 == PIECES
        block = ctx.enter_context(nc.Block())

        @block.sync
        def _(sp):
            load_weights(sp, a, w, 0)

        @block.gpsimd
        def _(pool):
            for p in range(PIECES):
                piece = slice(p * PIECE, (p + 1) * PIECE)
                pool.wait_ge(w["masked"], p + 1)
                nc.gpsimd.tensor_tensor(w["part"][1][:, piece], w["raw"][:, piece], w["mask"][p % 2][:].bitcast(F32),
                                        ALU.subtract).then_inc(w["low"], 1)

        @block.scalar
        def _(act):
            act.wait_ge(shifted_ready, 1)
            nc.scalar.activation(probs[:], shifted[:], ACT.Exp).then_inc(exp_ready, 1)
            for p in range(PIECES):
                act.wait_ge(w["masked"], p + 1)
                nc.scalar.activation(w["part"][0][:, p * PIECE:(p + 1) * PIECE], w["mask"][p % 2][:].bitcast(F32),
                                     ACT.Copy).then_inc(w["high"], 1)

        @block.tensor
        def _(pe):
            pe.wait_ge(fw_ready, 1)
            for g in range(4):
                last = nc.tensor.transpose(bank[:, g * P:(g + 1) * P],
                                           fw[:].rearrange("p t e -> p (t e)")[:, g * P:(g + 1) * P], ident[:])
            last.then_inc(flipped, 1)
            with pe.Fori(0, BITS // AT_ONCE) as i:
                for b in range(AT_ONCE):
                    pe.wait_ge(counted, i * AT_ONCE + (b + 1))
                    nc.tensor.matmul(total[:], k["same_expert"][:], count[:], start=True, stop=True
                                     ).then_inc(totalled, 1)
            pe.wait_ge(counted, BITS + 1)
            nc.tensor.matmul(total[:], k["same_expert"][:], count[:], start=True, stop=True).then_inc(totalled, 1)
            for i in range(2):
                pe.wait_ge(segments, i + 1)
                nc.tensor.matmul(before[:], k["earlier"][:], seg[:], start=True, stop=False)
                nc.tensor.matmul(before[:], k["same_expert"][:], seg_before[:], start=False, stop=True
                                 ).then_inc(offsets, 1)
            pe.wait_ge(code_ready, 1)
            for g in range(4):
                last = nc.tensor.transpose(bank[:, g * P:(g + 1) * P], code[:, g, :], ident[:])
            last.then_inc(flipped, 1)

        @block.vector
        def _(dve):
            chain = [0]

            def mark(ins):
                chain[0] += 1
                ins.then_inc(step, 1)

            def link(ins):
                mark(ins)
                dve.wait_ge(step, chain[0])

            v = nc.vector
            lg = logits[:].rearrange("p (t e) -> p t e", e=NE)
            link(v.tensor_reduce(row_max[:], lg, AX.X, ALU.max))
            v.tensor_tensor(shifted[:], lg, row_max[:].to_broadcast(full3), ALU.subtract).then_inc(shifted_ready, 1)
            dve.wait_ge(exp_ready, 1)
            link(v.tensor_reduce(row_sum[:], probs[:], AX.X, ALU.add))
            link(v.reciprocal(row_sum[:], row_sum[:]))
            link(v.tensor_tensor(probs[:], probs[:], row_sum[:].to_broadcast(full3), ALU.mult))
            for i in range(2):
                src = (probs, rest)[i]
                link(v.tensor_reduce(top[i][:], src[:], AX.X, ALU.max))
                link(v.tensor_tensor(equal[:], src[:], top[i][:].to_broadcast(full3), ALU.is_equal))
                link(v.tensor_tensor(key[:], equal[:], k["first_wins"][:].to_broadcast(full3), ALU.mult))
                link(v.tensor_reduce(key_max[:], key[:], AX.X, ALU.max))
                link(v.tensor_tensor(mask[i][:], key[:], key_max[:].to_broadcast(full3), ALU.is_equal))
                if i == 0:
                    link(v.scalar_tensor_tensor(out=rest[:], in0=mask[0][:], scalar=-2.0, in1=probs[:],
                                                op0=ALU.mult, op1=ALU.add))
            link(v.tensor_tensor(row_sum[:], top[0][:], top[1][:], ALU.add))
            link(v.tensor_scalar(row_sum[:], row_sum[:], 1e-6, None, ALU.add))
            link(v.reciprocal(row_sum[:], row_sum[:]))
            mark(v.tensor_tensor(weight[0][:], top[0][:], row_sum[:], ALU.mult))
            link(v.tensor_tensor(weight[1][:], top[1][:], row_sum[:], ALU.mult))
            mark(v.tensor_tensor(equal[:], mask[0][:], weight[0][:].to_broadcast(full3), ALU.mult))
            link(v.tensor_tensor(key[:], mask[1][:], weight[1][:].to_broadcast(full3), ALU.mult))
            v.tensor_tensor(fw[:], equal[:], key[:], ALU.add).then_inc(fw_ready, 1)
            dve.wait_ge(fw_ready, 1)
            link(v.tensor_copy(k["part"][0][:], fw[:]))
            link(v.tensor_tensor(left[0][:], fw[:], k["part"][0][:], ALU.subtract))
            link(v.tensor_copy(k["part"][1][:], left[0][:]))
            link(v.tensor_tensor(left[1][:], left[0][:], k["part"][1][:], ALU.subtract))
            link(v.tensor_copy(k["part"][2][:], left[1][:]))
            dve.wait_ge(flipped, 1)
            link(v.tensor_copy(ft[:], bank[:].rearrange("p (g t) -> p g t", g=4)))

            dve.wait_ge(w["loaded"], 48)
            with dve.Fori(0, BITS // AT_ONCE) as i:
                for b in range(AT_ONCE):
                    done = i * (4 * AT_ONCE) + (chain[0] + 4 * b)
                    v.tensor_tensor(candidate[:], k["threshold"][:], k["bit"][:], ALU.bitwise_or).then_inc(step, 1)
                    dve.wait_ge(step, done + 1)
                    v.tensor_scalar(flags[:], ft[:], candidate[:].bitcast(F32), None, ALU.is_ge, ALU.add,
                                    accum_out=count[:]).then_inc(counted, 1)
                    if b < 2:
                        v.tensor_scalar(w["mask"][b][:],
                                        w["raw"][:, bass.ds(i * (2 * PIECE) + b * PIECE, PIECE)].bitcast(I32),
                                        HIGH_BITS, None, ALU.bitwise_and).then_inc(w["masked"], 1)
                    dve.wait_ge(totalled, i * AT_ONCE + (b + 1))
                    v.tensor_scalar(accept[:], total[:], float(CAP), None, ALU.is_ge).then_inc(step, 1)
                    dve.wait_ge(step, done + 2)
                    v.tensor_scalar(k["bit"][:], k["bit"][:], 1, None, ALU.logical_shift_right).then_inc(step, 1)
                    v.copy_predicated(k["threshold"][:], accept[:], candidate[:]).then_inc(step, 1)
                    dve.wait_ge(step, done + 4)
                dve.wait_ge(w["high"], i * 2 + 2)
                dve.wait_ge(w["low"], i * 2 + 2)
            chain[0] += 4 * BITS
            limit = k["threshold"][:].bitcast(F32)
            v.tensor_scalar(above[:], ft[:], limit, None, ALU.is_gt, ALU.add, accum_out=count[:]).then_inc(counted, 1)
            link(v.tensor_scalar(tied[:], ft[:], limit, None, ALU.is_equal))
            dve.wait_ge(totalled, BITS + 1)
            link(v.tensor_scalar(need[:], total[:], -1.0, float(CAP), ALU.mult, ALU.add))

            def number(flags_in, i):
                for g in range(4):
                    (link if g == 3 else mark)(v.tensor_tensor_scan(
                        rank[:, g, :], k["ones"][:], flags_in[:, g, :], 0.0, ALU.mult, ALU.add))
                link(v.tensor_copy(seg[:], rank[:, :, P - 1]))
                link(v.tensor_tensor_scan(seg_sum[:], k["ones"][:, 0:4], seg[:], 0.0, ALU.mult, ALU.add))
                v.tensor_tensor(seg_before[:], seg_sum[:], seg[:], ALU.subtract).then_inc(segments, 1)
                dve.wait_ge(offsets, i + 1)
                for g in range(4):
                    (link if g == 3 else mark)(v.tensor_scalar(
                        rank[:, g, :], rank[:, g, :], before[:, g:g + 1], None, ALU.add))

            number(tied, 0)
            link(v.scalar_tensor_tensor(out=flags[:], in0=rank[:], scalar=need[:], in1=tied[:],
                                        op0=ALU.is_le, op1=ALU.mult))
            link(v.tensor_tensor(flags[:], flags[:], above[:], ALU.add))
            number(flags, 1)
            v.tensor_tensor(code[:], rank[:], flags[:], ALU.mult).then_inc(code_ready, 1)
            dve.wait_ge(flipped, 2)
            link(v.tensor_scalar(slot[:], bank[:], -1.0, None, ALU.add))
            mark(v.tensor_scalar(low[:], slot[:], P - 1, None, ALU.bitwise_and))
            link(v.tensor_scalar(high[:], slot[:], 7, None, ALU.arith_shift_right))
            mark(v.tensor_copy(k["low"][:], low[:].rearrange("p (t e) -> p t e", e=NE)))
            link(v.tensor_copy(k["high"][:], high[:].rearrange("p (t e) -> p t e", e=NE)))


def experts(nc, a, k, w, dram, ident):
    with ExitStack() as ctx:
        def sb(name, shape, dt=F32):
            return ctx.enter_context(nc.sbuf_tensor(name, shape, dt))

        def sem(name):
            return ctx.enter_context(nc.semaphore(name))

        gu_part, down_part, w_mask = w["gu_part"], w["down_part"], w["mask"]
        x_mask = sb("x_mask", [P, KD, SJ * P], I32)
        h_mask = [sb(f"h_mask{i}", [P, SJ * P], I32) for i in range(2)]
        hot_low = sb("hot_low", [P, TILES, P], BF16)
        hot_high = sb("hot_high", [P, TILES, ST], BF16)
        values = sb("values", [P, TILES, NV, ST], BF16)
        lists = sb("lists", [P, NV, ST])
        pair = sb("pair", [P, ST])
        token = [sb(f"token{i}", [P, ST], U32) for i in range(2)]
        share = [sb(f"share{i}", [P, ST]) for i in range(2)]
        xg = sb("xg", [P, ST, DM])
        x_part = [sb(f"x_part{i}", [P, KD, CAP], F32R) for i in range(2)]
        silu = [sb(f"silu{i}", [P, SJ * P]) for i in range(4)]
        hid_part = [[sb(f"hid{b}_part{i}", [P, FT_, SJ * P], F32R) for i in range(2)] for b in range(2)]
        eo = sb("eo", [P, ST, DM])
        gu_bank = [ctx.enter_context(nc.psum_tensor(f"gu{i}", [P, 2, SJ * P], F32)) for i in range(4)]
        dn_bank = [ctx.enter_context(nc.psum_tensor(f"dn{i}", [P, SJ, DM], F32)) for i in range(2)]
        tr_bank = [ctx.enter_context(nc.psum_tensor(f"tr{i}", [P, KD, SJ * P], F32)) for i in range(2)]

        weights_loaded, w_masked, w_high, w_low = (w[n] for n in ("loaded", "masked", "high", "low"))
        x_masked = sem("x_masked")
        x_high = sem("x_high")
        h_masked = sem("h_masked")
        h_high = sem("h_high")
        hot_ready = sem("hot_ready")
        values_step = sem("values_step")
        listed = sem("listed")
        list_step = sem("list_step")
        token_ready = sem("token_ready")
        share_ready = sem("share_ready")
        gathered = [sem(f"gathered{j}") for j in range(JC)]
        tr_full = sem("tr_full")
        tr_read = sem("tr_read")
        gu_full = sem("gu_full")
        silu_ready = sem("silu_ready")
        product_ready = sem("product_ready")
        hidden_ready = sem("hidden_ready")
        dn_full = sem("dn_full")
        dn_read = sem("dn_read")
        added = sem("added")
        GU, QT = JC * FT_, TILES // 8

        x1_d, acc_d = dram["x1"], dram["acc"]

        def over_experts(eng, emit):
            emit(-1, 1, "start")
            emit(0, 0, "mid0")
            with eng.Fori(0, (NE - 2) // 2) as i:
                emit(i * 2 + 1, 1, "mid")
                emit(i * 2 + 2, 0, "mid")
            emit(NE - 1, 1, "end")

        block = ctx.enter_context(nc.Block())

        @block.sync
        def _(sp):
            def expert(e, par, kind):
                if kind in ("start", "end"):
                    return
                sp.wait_ge(w_low, (e + 1) * PIECES)
                load_weights(sp, a, w, e + 1)

            over_experts(sp, expert)

        @block.gpsimd
        def _(pool):
            def low_parts(e, pieces):
                for p in pieces:
                    pool.wait_ge(w_masked, e * PIECES + p + 1)
                    if p < FT_:
                        pool.wait_ge(gu_full, e * GU - FT_ + p + 1)
                    else:
                        pool.wait_ge(dn_full, e * JC)
                    raw, parts = raw_piece(w, p)
                    nc.gpsimd.tensor_tensor(parts[1], raw, mask_of(w, p, F32), ALU.subtract).then_inc(w_low, 1)

            def gather(e_next, par):
                pool.wait_ge(token_ready, e_next + 1)
                for s in range(ST):
                    nc.gpsimd.indirect_dma_start(
                        out=xg[:, s, :], out_offset=None, in_=x1_d,
                        in_offset=bass.IndirectOffsetOnAxis(ap=token[par][:, s:s + 1], axis=0),
                        bounds_check=TOK - 1).then_inc(gathered[s // SJ], 16)

            def expert(e, par, kind):
                if kind == "start":
                    gather(0, 0)
                    return
                for j in range(-1, JC):
                    if j == -1 and kind == "mid0" or j == JC - 1 and kind != "end":
                        continue
                    if j == 2 and kind != "end":
                        pool.wait_ge(tr_read, (e + 1) * JC)
                        gather(e + 1, 1 - par)
                    pool.wait_ge(dn_read, e * JC + j + 1)
                    if j == 0 and kind != "mid0":
                        pool.wait_ge(added, e * (ST * 16))
                    owner, chunk = (par, j) if j >= 0 else (1 - par, JC - 1)
                    for s in range(chunk * SJ, (chunk + 1) * SJ):
                        nc.gpsimd.indirect_dma_start(
                            out=acc_d, out_offset=bass.IndirectOffsetOnAxis(ap=token[owner][:, s:s + 1], axis=0),
                            in_=eo[:, s, :], in_offset=None, bounds_check=TOK - 1,
                            compute_op=ALU.add).then_inc(added, 16)
                    if j == -1:
                        low_parts(e, range(FT_, PIECES))
                if kind != "end":
                    low_parts(e + 1, range(FT_))

            expert(-1, 1, "start")
            for e in range(NE):
                expert(e, e % 2, "mid0" if e == 0 else "end" if e == NE - 1 else "mid")
            pool.wait_ge(added, NE * ST * 16)

        @block.vector
        def _(dve):
            v = nc.vector

            def prepare(e, i, first):
                if i == 0:
                    if not first:
                        dve.wait_ge(listed, e)
                    v.tensor_tensor(hot_high[:], k["high"][:, :, bass.ds(e, 1)].to_broadcast([P, TILES, ST]),
                                    k["slot_high"][:].to_broadcast([P, TILES, ST]), ALU.is_equal
                                    ).then_inc(values_step, 1)
                elif i <= NV:
                    if i == 1:
                        dve.wait_ge(values_step, e * (NV + 1) + 1)
                    src = (k["tile_id"][:] if i == 1 else k["part_id"][:].to_broadcast([P, TILES, 1]) if i == 2 else
                           k["part"][i - 3][:, :, bass.ds(e, 1)])
                    v.tensor_tensor(values[:, :, i - 1, :], hot_high[:], src.to_broadcast([P, TILES, ST]),
                                    ALU.mult).then_inc(values_step, 1)
                else:
                    part = slice((i - NV - 1) * QT, (i - NV) * QT)
                    v.tensor_tensor(hot_low[:, part, :], k["low"][:, part, bass.ds(e, 1)].to_broadcast([P, QT, P]),
                                    k["slot_low"][:].to_broadcast([P, QT, P]), ALU.is_equal).then_inc(hot_ready, 1)

            def read_lists(e, par, first):
                dve.wait_ge(listed, e + 1)
                v.tensor_copy(lists[:], tr_bank[0][:].rearrange("p k s -> p (k s)")[:, 0:NV * ST].rearrange(
                    "p (v s) -> p v s", v=NV)).then_inc(list_step, 1)
                dve.wait_ge(list_step, e * 2 + 1)
                if not first:
                    dve.wait_ge(added, (e - 1) * (ST * 16))
                v.scalar_tensor_tensor(out=token[par][:], in0=lists[:, 0, :], scalar=float(P), in1=lists[:, 1, :],
                                       op0=ALU.mult, op1=ALU.add).then_inc(token_ready, 1)
                v.tensor_tensor(pair[:], lists[:, 2, :], lists[:, 3, :], ALU.add).then_inc(list_step, 1)
                dve.wait_ge(list_step, e * 2 + 2)
                if not first:
                    dve.wait_ge(dn_read, (e - 1) * JC)
                v.tensor_tensor(share[par][:], pair[:], lists[:, 4, :], ALU.add).then_inc(share_ready, 1)

            def mask_piece(e, p):
                if p == 0:
                    dve.wait_ge(weights_loaded, (e + 1) * 48)
                dve.wait_ge(w_high, e * PIECES + p - 2)
                dve.wait_ge(w_low, e * PIECES + p - 2)
                raw, _ = raw_piece(w, p)
                v.tensor_scalar(mask_of(w, p, I32), raw.bitcast(I32), HIGH_BITS, None, ALU.bitwise_and
                                ).then_inc(w_masked, 1)

            def split_tokens(e, j, kind):
                dve.wait_ge(tr_full, e * JC + j + 1)
                if kind != "start" or j > 0:
                    dve.wait_ge(x_high, e * JC + j)
                    dve.wait_ge(tr_read, e * JC + j)
                v.tensor_scalar(x_mask[:], tr_bank[j % 2][:].bitcast(I32), HIGH_BITS, None, ALU.bitwise_and
                                ).then_inc(x_masked, 1)
                dve.wait_ge(x_masked, e * JC + j + 1)
                v.tensor_tensor(x_part[1][:, :, j * SJ * P:(j + 1) * SJ * P], tr_bank[j % 2][:],
                                x_mask[:].bitcast(F32), ALU.subtract).then_inc(tr_read, 1)

            def low_hidden(e, par, n):
                j, f = divmod(n, FT_)
                dve.wait_ge(h_masked, e * GU + n + 1)
                v.tensor_tensor(hid_part[(j + par) % 2][1][:, f, :], silu[n % 4][:], h_mask[n % 2][:].bitcast(F32),
                                ALU.subtract).then_inc(hidden_ready, 1)

            def expert(e, par, kind):
                if kind == "start":
                    for i in range(NV + 9):
                        prepare(0, i, True)
                    read_lists(0, 0, True)
                    split_tokens(0, 0, kind)
                    return
                for n in range(GU):
                    j, f = divmod(n, FT_)
                    dve.wait_ge(silu_ready, e * GU + n + 1)
                    v.tensor_tensor(silu[n % 4][:], silu[n % 4][:], gu_bank[n % 4][:, 1, :],
                                    ALU.mult).then_inc(product_ready, 1)
                    if n > 0:
                        low_hidden(e, par, n - 1)
                    if f == 0 and (kind != "mid0" or j >= 2):
                        dve.wait_ge(dn_full, e * JC + j - 1)
                    dve.wait_ge(product_ready, e * GU + n + 1)
                    if kind != "mid0" or n >= 2:
                        dve.wait_ge(h_high, e * GU + n - 1)
                        dve.wait_ge(hidden_ready, e * GU + n - 1)
                    v.tensor_scalar(h_mask[n % 2][:], silu[n % 4][:].bitcast(I32), HIGH_BITS, None, ALU.bitwise_and
                                    ).then_inc(h_masked, 1)
                    if n + 1 in DOWN_PIECE_AT and kind != "mid0":
                        mask_piece(e, FT_ + DOWN_PIECE_AT.index(n + 1))
                    if 0 <= n - PREPARE_AT < NV + 9 and kind != "end":
                        prepare(e + 1, n - PREPARE_AT, False)
                    if n == LIST_AT + 1 and kind != "end":
                        read_lists(e + 1, 1 - par, kind == "mid0")
                    if j == JC - 1 and kind != "end":
                        mask_piece(e + 1, f)
                    if n - 1 in TR_AT and kind != "end":
                        split_tokens(e + 1, TR_AT.index(n - 1), kind)
                    if n - 1 in FIRST_TR_AT and kind == "mid0":
                        split_tokens(0, 1 + FIRST_TR_AT.index(n - 1), kind)
                low_hidden(e, par, GU - 1)
                if kind != "end":
                    split_tokens(e + 1, JC - 1, kind)

            over_experts(dve, expert)

        order = []
        for j in range(JC):
            for f in range(FT_):
                n = j * FT_ + f
                order.append(("gu", n))
                if n:
                    order.append(("h", n - 1))
                if f == 3:
                    order.append(("dn", j - 1))
                if n in DOWN_PIECE_AT:
                    order.append(("w", FT_ + DOWN_PIECE_AT.index(n)))
                if n == LIST_AT:
                    order.append(("list", 0))
                if j == JC - 1 and f >= 1:
                    order.append(("w", f - 1))
                if n in TR_AT:
                    order.append(("tr", TR_AT.index(n)))
                if n - 2 in TR_AT:
                    order.append(("x", TR_AT.index(n - 2)))
                if n in FIRST_TR_AT:
                    order.append(("first tr", 1 + FIRST_TR_AT.index(n)))
                if n - 2 in FIRST_TR_AT:
                    order.append(("first x", 1 + FIRST_TR_AT.index(n - 2)))
        order += [("h", GU - 1), ("w", FT_ - 1), ("x", JC - 1), ("dn", JC - 1)]

        def skipped(kind, n):
            return n == -1 and kind == "mid0" or n == JC - 1 and kind != "end"

        @block.scalar
        def _(act):
            def high_tokens(e, j):
                act.wait_ge(x_masked, e * JC + j + 1)
                nc.scalar.activation(x_part[0][:, :, j * SJ * P:(j + 1) * SJ * P], x_mask[:].bitcast(F32),
                                     ACT.Copy).then_inc(x_high, 1)

            def high_weights(e, p):
                act.wait_ge(w_masked, e * PIECES + p + 1)
                nc.scalar.activation(raw_piece(w, p)[1][0], mask_of(w, p, F32), ACT.Copy).then_inc(w_high, 1)

            def expert(e, par, kind):
                if kind == "start":
                    high_tokens(0, 0)
                    return
                for what, n in order:
                    if what == "gu":
                        act.wait_ge(gu_full, e * GU + n + 1)
                        if kind != "mid0" or n >= 4:
                            act.wait_ge(hidden_ready, e * GU + n - 3)
                        nc.scalar.activation(silu[n % 4][:], gu_bank[n % 4][:, 0, :], ACT.Silu).then_inc(silu_ready, 1)
                    elif what == "h":
                        act.wait_ge(h_masked, e * GU + n + 1)
                        j, f = divmod(n, FT_)
                        if f == 0 and (kind != "mid0" or j >= 2):
                            act.wait_ge(dn_full, e * JC + j - 1)
                        nc.scalar.activation(hid_part[(j + par) % 2][0][:, f, :], h_mask[n % 2][:].bitcast(F32),
                                             ACT.Copy).then_inc(h_high, 1)
                    elif what == "dn" and not skipped(kind, n):
                        act.wait_ge(dn_full, e * JC + n + 1)
                        owner, chunk = (par, n) if n >= 0 else (1 - par, JC - 1)
                        if n == 0:
                            act.wait_ge(share_ready, e + 1)
                            if kind != "mid0":
                                act.wait_ge(added, e * (ST * 16))
                        for s in range(SJ):
                            tile = chunk * SJ + s
                            last = nc.scalar.activation(eo[:, tile, :], dn_bank[(n + par) % 2][:, s, :], ACT.Copy,
                                                        scale=share[owner][:, tile:tile + 1])
                        last.then_inc(dn_read, 1)
                    elif what == "w" and n >= FT_:
                        if kind != "mid0":
                            high_weights(e, n)
                    elif what == "w" and kind != "end":
                        high_weights(e + 1, n)
                    elif what == "first x" and kind == "mid0":
                        high_tokens(0, n)
                    elif what == "x" and kind != "end":
                        high_tokens(e + 1, n)

            over_experts(act, expert)

        @block.tensor
        def _(pe):
            def make_list(e):
                pe.wait_ge(values_step, (e + 1) * (NV + 1))
                for t in range(TILES):
                    if t % QT == 0:
                        pe.wait_ge(hot_ready, e * 8 + t // QT + 1)
                    last = nc.tensor.matmul(tr_bank[0][:].rearrange("p k s -> p (k s)")[:, 0:NV * ST],
                                            hot_low[:, t, :], values[:, t, :, :].rearrange("p v s -> p (v s)"),
                                            start=t == 0, stop=t == TILES - 1)
                last.then_inc(listed, 1)

            def transpose(e, j):
                pe.wait_ge(gathered[j], (e + 1) * (SJ * 16))
                if j == 0:
                    pe.wait_ge(token_ready, e + 1)
                if j >= 2:
                    pe.wait_ge(tr_read, e * JC + j - 1)
                for kk in range(KD):
                    for s in range(SJ):
                        last = nc.tensor.transpose(tr_bank[j % 2][:, kk, s * P:(s + 1) * P],
                                                   xg[:, j * SJ + s, kk * P:(kk + 1) * P], ident[:])
                last.then_inc(tr_full, 1)

            def expert(e, par, kind):
                if kind == "start":
                    make_list(0)
                    transpose(0, 0)
                    return
                for what, n in order:
                    if what == "gu":
                        j, f = divmod(n, FT_)
                        if j == 0:
                            pe.wait_ge(w_high, e * PIECES + f + 1)
                            pe.wait_ge(w_low, e * PIECES + f + 1)
                        if f == 0:
                            pe.wait_ge(tr_read, e * JC + j + 1)
                            pe.wait_ge(x_high, e * JC + j + 1)
                        if kind != "mid0" or n >= 4:
                            pe.wait_ge(product_ready, e * GU + n - 3)
                        for i in range(2):
                            products = [(kk, wp, xp) for kk in range(KD) for wp, xp in ((0, 0), (0, 1), (1, 0))]
                            for m, (kk, wp, xp) in enumerate(products):
                                last = nc.tensor.matmul(gu_bank[n % 4][:, i, :],
                                                        gu_part[wp][:, i, kk, f * P:(f + 1) * P],
                                                        x_part[xp][:, kk, j * SJ * P:(j + 1) * SJ * P],
                                                        start=m == 0, stop=m == len(products) - 1)
                        last.then_inc(gu_full, 1)
                    elif what == "dn" and not skipped(kind, n):
                        pe.wait_ge(hidden_ready, e * GU + (n + 1) * FT_)
                        pe.wait_ge(h_high, e * GU + (n + 1) * FT_)
                        if n == 0:
                            pe.wait_ge(w_high, (e + 1) * PIECES)
                            pe.wait_ge(w_low, (e + 1) * PIECES)
                        if kind != "mid0" or n >= 2:
                            pe.wait_ge(dn_read, e * JC + n - 1)
                        for s in range(SJ):
                            products = [(f, hp, wp) for f in range(FT_) for hp, wp in ((0, 0), (0, 1), (1, 0))]
                            for m, (f, hp, wp) in enumerate(products):
                                last = nc.tensor.matmul(dn_bank[(n + par) % 2][:, s, :],
                                                        hid_part[(n + par) % 2][hp][:, f, s * P:(s + 1) * P],
                                                        down_part[wp][:, f, :], start=m == 0,
                                                        stop=m == len(products) - 1)
                        last.then_inc(dn_full, 1)
                    elif what == "first tr" and kind == "mid0":
                        transpose(0, n)
                    elif what == "list" and kind != "end":
                        pe.wait_ge(tr_read, (e + 1) * JC)
                        make_list(e + 1)
                    elif what == "tr" and kind != "end":
                        transpose(e + 1, n)

            over_experts(pe, expert)


def last_norm(nc, dram, out):
    G = 4
    N = TILES // G
    R = 8
    with ExitStack() as ctx:
        def sb(name, shape, dt=F32):
            return ctx.enter_context(nc.sbuf_tensor(name, shape, dt))

        def sem(name):
            return ctx.enter_context(nc.semaphore(name))

        rows = [sb(f"rows{i}", [P, G, DM]) for i in range(R)]
        stats = [sb(f"stats{i}", [P, G, 6]) for i in range(R)]
        mean_var = [sb(f"mean_var{i}", [P, G, 2]) for i in range(R)]
        var_eps = [sb(f"var_eps{i}", [P, G]) for i in range(R)]
        rstd = [sb(f"rstd{i}", [P, G]) for i in range(R)]
        shift = [sb(f"shift{i}", [P, G]) for i in range(R)]
        minus_mean = [sb(f"minus_mean{i}", [P, G]) for i in range(R)]
        minus_half = sb("minus_half2", [P, G])
        loaded = [sem(f"rows_in{i}") for i in range(R)]
        const_ready = sem("minus_half_ready")
        aggregated = sem("aggregated")
        var_ready = sem("var_ready2")
        rstd_ready = sem("rstd_ready2")
        shift_ready = sem("shift_ready2")
        normed = sem("normed")
        stored = [sem(f"stored{i}") for i in range(R)]
        acc_d = dram["acc"]
        out_d = out.rearrange("b s d -> (b s) d")
        block = ctx.enter_context(nc.Block())

        @block.sync
        def _(sp):
            for i in range(R):
                sp.dma_start(rows[i][:], acc_d[i * G * P:(i + 1) * G * P, :].rearrange("(g p) d -> p g d", p=P)
                             ).then_inc(loaded[i], 16)
            with sp.Fori(0, N // R - 1) as r:
                for i in range(R):
                    sp.wait_ge(stored[i], r * 16 + 16)
                    sp.dma_start(rows[i][:], acc_d[bass.ds((r * R + (R + i)) * (G * P), G * P), :].rearrange(
                        "(g p) d -> p g d", p=P)).then_inc(loaded[i], 16)

        @block.vector
        def _(dve):
            with dve.Fori(0, N // R) as r:
                for i in range(R):
                    n = r * R + i
                    dve.wait_ge(loaded[i], r * 16 + 16)
                    for g in range(G):
                        nc.vector.bn_stats(stats[i][:, g, :], rows[i][:, g, :])
                    dve.drain()
                    for g in range(G):
                        nc.vector.bn_aggr(mean_var[i][:, g, :], stats[i][:, g, :]).then_inc(aggregated, 1)
                    dve.wait_ge(aggregated, n * G + G)
                    nc.vector.tensor_scalar(minus_mean[i][:], mean_var[i][:, :, 0], -1.0, None, ALU.mult)
                    nc.vector.tensor_scalar(var_eps[i][:], mean_var[i][:, :, 1], EPS, None, ALU.add
                                            ).then_inc(var_ready, 1)

        @block.gpsimd
        def _(pool):
            nc.gpsimd.memset(minus_half[:], -0.5).then_inc(const_ready, 1)
            pool.wait_ge(const_ready, 1)
            with pool.Fori(0, N // R) as r:
                for i in range(R):
                    pool.wait_ge(var_ready, r * R + (i + 1))
                    nc.gpsimd.tensor_tensor(rstd[i][:], var_eps[i][:], minus_half[:], ALU.pow).then_inc(rstd_ready, 1)
                    pool.wait_ge(rstd_ready, r * R + (i + 1))
                    nc.gpsimd.tensor_tensor(shift[i][:], minus_mean[i][:], rstd[i][:], ALU.mult
                                            ).then_inc(shift_ready, 1)

        @block.scalar
        def _(act):
            with act.Fori(0, N // R) as r:
                for i in range(R):
                    n = r * R + i
                    act.wait_ge(shift_ready, n + 1)
                    for g in range(G):
                        nc.scalar.activation(rows[i][:, g, :], rows[i][:, g, :], ACT.Identity, bias=shift[i][:, g:g + 1],
                                             scale=rstd[i][:, g:g + 1]).then_inc(normed, 1)
                    act.wait_ge(normed, n * G + G)
                    act.dma_start(out_d[bass.ds(n * (G * P), G * P), :].rearrange("(g p) d -> p g d", p=P), rows[i][:]
                                  ).then_inc(stored[i], 16)
            for i in range(R):
                act.wait_ge(stored[i], N // R * 16)


def build(nc, a, out):
    with ExitStack() as ctx:
        def sb(name, shape, dt=F32):
            return ctx.enter_context(nc.sbuf_tensor(name, shape, dt))

        dram = {"b_rows": nc.dram_tensor("b_rows", [2, NST, CL], F32, kind="Internal").ap(),
                "x1": nc.dram_tensor("x1_dram", [TOK, DM], F32, kind="Internal").ap(),
                "acc": nc.dram_tensor("acc_dram", [TOK, DM], F32, kind="Internal").ap()}
        ident = sb("ident", [P, P])
        logits = sb("logits", [P, TILES * NE])
        make_ident(nc, ident)
        attention(nc, a, dram, logits, ident)
        k = {
            "slot_low": sb("slot_low", [P, 1, P], BF16),
            "slot_high": sb("slot_high", [P, 1, CAP // P], BF16),
            "tile_id": sb("tile_id", [P, TILES, 1], BF16),
            "part_id": sb("part_id", [P, 1, 1], BF16),
            "first_wins": sb("first_wins", [P, 1, NE]),
            "bit": sb("bit", [P, 1], I32),
            "threshold": sb("threshold", [P, 1], I32),
            "ones": sb("ones", [P, P]),
            "same_expert": sb("same_expert", [P, P]),
            "earlier": sb("earlier", [P, P]),
            "low": sb("slot_low_of", [P, TILES, NE], BF16),
            "high": sb("slot_high_of", [P, TILES, NE], BF16),
            "part": [sb(f"fw_part{i}", [P, TILES, NE], BF16) for i in range(3)],
        }
        make_constants(nc, k)
        with ExitStack() as weights:
            w = weight_buffers(nc, weights)
            route(nc, a, k, w, logits, ident)
            experts(nc, a, k, w, dram, ident)
        last_norm(nc, dram, out)


def kernel(**inputs):
    import numpy as np
    import concourse.bacc as bacc
    from concourse.bass_utils import run_bass_kernel_spmd

    nc = bacc.Bacc("TRN2", target_bir_lowering=False, num_devices=1)
    g = {k.replace("L0_attn_", "").replace("L0_ffn_", ""): np.asarray(v) for k, v in inputs.items()}
    laid = {
        "x": g["x"], "xT": g["x"].reshape(TOK, DM).T, "W_in": g["W_in"], "W_conv": g["W_conv"], "W_x": g["W_x"],
        "W_dt": g["W_dt"], "b_dt": g["b_dt"].reshape(DT, P).T, "D_param": g["D_param"].reshape(DT, P).T,
        "A_log": g["A_log"], "W_out": g["W_out"], "router_wT": g["router_w"].T,
        "wg": g["wg"], "wu": g["wu"], "wd": g["wd"],
    }
    laid = {k: np.ascontiguousarray(v) for k, v in laid.items()}
    aps = {k: nc.dram_tensor(f"in_{k}", v.shape, mybir.dt.from_np(v.dtype), kind="ExternalInput").ap()
           for k, v in laid.items()}
    out = nc.dram_tensor("out", (BATCH, SEQ, DM), F32, kind="ExternalOutput").ap()
    build(nc, aps, out)
    ran = run_bass_kernel_spmd(nc, [{f"in_{k}": v for k, v in laid.items()}], core_ids=[0])
    return ran.results[0]["out"]
```
